# Optimizing a Trainium2 kernel written in Bass

```python
import numpy as np
import jax
import jax.numpy as jnp

def _softmax(x, axis=-1):
    return jax.nn.softmax(x, axis=axis)

def _gelu(x):
    return jax.nn.gelu(x, approximate=True)

def _silu(x):
    return jax.nn.silu(x)

def _sigmoid(x):
    return jax.nn.sigmoid(x)

def _layernorm(x, axis=-1, eps=1e-05):
    m = jnp.mean(x, axis=axis, keepdims=True)
    v = jnp.var(x, axis=axis, keepdims=True)
    return (x - m) / jnp.sqrt(v + eps)

def _scatter_add(tgt, idx, src, axis=0):
    return tgt.at[idx].add(src)

def _segment_sum(src, seg, n):
    return jax.ops.segment_sum(src, seg, n)
kernel_name = 'mk_gnn_ffn_d1_gnn_r8_ca4a8a'

def setup_inputs(seed: int=0):
    np.random.seed(seed)
    _w = jnp.asarray

    def _rec_inputs():
        import jax
        import jax.numpy as jnp
        _gk = jax.random.key(seed)
        x = -0.0003713 + 1 * jax.random.normal(jax.random.fold_in(_gk, 1), (6250, 256), jnp.float32)
        _s = jax.random.randint(jax.random.fold_in(_gk, 2), (50000,), 0, 6250, jnp.int32)
        _d = jax.random.randint(jax.random.fold_in(_gk, 3), (50000,), 0, 6250, jnp.int32)
        _loop = jnp.arange(6250, dtype=jnp.int32)
        src = jnp.concatenate([_s, _d, _loop])
        dst = jnp.concatenate([_d, _s, _loop])
        _o = jnp.argsort(dst, stable=True)
        src = src[_o]
        dst = dst[_o]
        return (x, src, dst)
    x, src, dst = _rec_inputs()

    def _L0_gnn_setup():
        import jax, jax.numpy as jnp
        import numpy as np
        N = 6250
        E = 100000
        F_DIM = 256
        H = 4
        C = 64
        SLOPE = 0.2

        def gat_layer(x, src, dst, W, a_src, a_dst, bias, heads, out_ch):
            n = x.shape[0]
            xW = (x @ W).reshape(n, heads, out_ch)
            alpha_s = jnp.sum(xW * a_src, axis=-1)
            alpha_d = jnp.sum(xW * a_dst, axis=-1)
            e = jax.nn.leaky_relu(alpha_s[src] + alpha_d[dst], SLOPE)
            m = jax.ops.segment_max(e, dst, num_segments=n)
            w = jnp.exp(e - m[dst])
            z = jax.ops.segment_sum(w, dst, num_segments=n)
            alpha = w / z[dst]
            out = jax.ops.segment_sum(xW[src] * alpha[:, :, None], dst, num_segments=n)
            return out.reshape(n, heads * out_ch) + bias
        key = jax.random.key(seed)
        ks = jax.random.split(key, 11)
        s = 0.05
        return {'x': jax.random.normal(ks[0], (N, F_DIM), jnp.float32), 'edge_index': jax.random.randint(ks[1], (2, E), 0, N), 'W1': jax.random.normal(ks[2], (F_DIM, H * C), jnp.float32) * s, 'a_src1': jax.random.normal(ks[3], (H, C), jnp.float32) * s, 'a_dst1': jax.random.normal(ks[4], (H, C), jnp.float32) * s, 'b1': jnp.zeros((H * C,), jnp.float32), 'W2': jax.random.normal(ks[5], (H * C, F_DIM), jnp.float32) * s, 'a_src2': jax.random.normal(ks[6], (1, F_DIM), jnp.float32) * s, 'a_dst2': jax.random.normal(ks[7], (1, F_DIM), jnp.float32) * s, 'b2': jnp.zeros((F_DIM,), jnp.float32)}
    _L0_gnn_all = _L0_gnn_setup()
    _L0_gnn_in = {k: v for k, v in _L0_gnn_all.items() if k in ('W1', 'a_src1', 'a_dst1', 'b1', 'W2', 'a_src2', 'a_dst2', 'b2')}
    del _L0_gnn_all

    def _L0_ffn_setup():
        import jax, jax.numpy as jnp
        import numpy as np
        BN_EPS = 0.001

        def _bn(h, g, b, m, v):
            return g * (h - m) * jax.lax.rsqrt(v + BN_EPS) + b
        key = jax.random.key(seed)
        ks = jax.random.split(key, 8)
        B, F, Df = (256, 64, 256)
        E, H, D = (8, 256, 256)
        s1 = 1.0 / np.sqrt(Df)
        s2 = 1.0 / np.sqrt(H)
        return {'x': jax.random.normal(ks[0], (B, F, Df), jnp.float32), 'Wr': jax.random.normal(ks[1], (Df, E), jnp.float32) * s1, 'br': jnp.zeros((E,), jnp.float32), 'W1': jax.random.normal(ks[2], (E, Df, H), jnp.float32) * s1, 'b1': jnp.zeros((E, H), jnp.float32), 'g1': jnp.ones((E, H), jnp.float32), 'be1': jnp.zeros((E, H), jnp.float32), 'm1': jnp.zeros((E, H), jnp.float32), 'v1': jnp.ones((E, H), jnp.float32), 'W2': jax.random.normal(ks[3], (E, H, H), jnp.float32) * s2, 'b2': jnp.zeros((E, H), jnp.float32), 'g2': jnp.ones((E, H), jnp.float32), 'be2': jnp.zeros((E, H), jnp.float32), 'm2': jnp.zeros((E, H), jnp.float32), 'v2': jnp.ones((E, H), jnp.float32), 'Wo': jax.random.normal(ks[4], (E, H, D), jnp.float32) * s2, 'bo': jnp.zeros((E, D), jnp.float32)}
    _L0_ffn_all = _L0_ffn_setup()
    _L0_ffn_in = {k: v for k, v in _L0_ffn_all.items() if k in ('Wr', 'br', 'W1', 'b1', 'g1', 'be1', 'm1', 'v1', 'W2', 'b2', 'g2', 'be2', 'm2', 'v2', 'Wo', 'bo')}
    del _L0_ffn_all
    return {'x': x, 'src': src, 'dst': dst, 'L0_gnn_W1': _L0_gnn_in['W1'], 'L0_gnn_a_src1': _L0_gnn_in['a_src1'], 'L0_gnn_a_dst1': _L0_gnn_in['a_dst1'], 'L0_gnn_b1': _L0_gnn_in['b1'], 'L0_gnn_W2': _L0_gnn_in['W2'], 'L0_gnn_a_src2': _L0_gnn_in['a_src2'], 'L0_gnn_a_dst2': _L0_gnn_in['a_dst2'], 'L0_gnn_b2': _L0_gnn_in['b2'], 'L0_ffn_Wr': _L0_ffn_in['Wr'], 'L0_ffn_br': _L0_ffn_in['br'], 'L0_ffn_W1': _L0_ffn_in['W1'], 'L0_ffn_b1': _L0_ffn_in['b1'], 'L0_ffn_g1': _L0_ffn_in['g1'], 'L0_ffn_be1': _L0_ffn_in['be1'], 'L0_ffn_m1': _L0_ffn_in['m1'], 'L0_ffn_v1': _L0_ffn_in['v1'], 'L0_ffn_W2': _L0_ffn_in['W2'], 'L0_ffn_b2': _L0_ffn_in['b2'], 'L0_ffn_g2': _L0_ffn_in['g2'], 'L0_ffn_be2': _L0_ffn_in['be2'], 'L0_ffn_m2': _L0_ffn_in['m2'], 'L0_ffn_v2': _L0_ffn_in['v2'], 'L0_ffn_Wo': _L0_ffn_in['Wo'], 'L0_ffn_bo': _L0_ffn_in['bo']}

def reference(x, src, dst, L0_gnn_W1, L0_gnn_a_src1, L0_gnn_a_dst1, L0_gnn_b1, L0_gnn_W2, L0_gnn_a_src2, L0_gnn_a_dst2, L0_gnn_b2, L0_ffn_Wr, L0_ffn_br, L0_ffn_W1, L0_ffn_b1, L0_ffn_g1, L0_ffn_be1, L0_ffn_m1, L0_ffn_v1, L0_ffn_W2, L0_ffn_b2, L0_ffn_g2, L0_ffn_be2, L0_ffn_m2, L0_ffn_v2, L0_ffn_Wo, L0_ffn_bo):
    import jax
    import jax.numpy as jnp

    def _L0_gnn_ref(x, edge_index, W1, a_src1, a_dst1, b1, W2, a_src2, a_dst2, b2):
        import jax, jax.numpy as jnp
        import numpy as np
        N = 6250
        E = 100000
        F_DIM = 256
        H = 4
        C = 64
        SLOPE = 0.2

        def gat_layer(x, src, dst, W, a_src, a_dst, bias, heads, out_ch):
            n = x.shape[0]
            xW = (x @ W).reshape(n, heads, out_ch)
            alpha_s = jnp.sum(xW * a_src, axis=-1)
            alpha_d = jnp.sum(xW * a_dst, axis=-1)
            e = jax.nn.leaky_relu(alpha_s[src] + alpha_d[dst], SLOPE)
            m = jax.ops.segment_max(e, dst, num_segments=n)
            w = jnp.exp(e - m[dst])
            z = jax.ops.segment_sum(w, dst, num_segments=n)
            alpha = w / z[dst]
            out = jax.ops.segment_sum(xW[src] * alpha[:, :, None], dst, num_segments=n)
            return out.reshape(n, heads * out_ch) + bias
        loop = jnp.arange(N)
        src = jnp.concatenate([edge_index[0], loop])
        dst = jnp.concatenate([edge_index[1], loop])
        h = jax.nn.elu(gat_layer(x, src, dst, W1, a_src1, a_dst1, b1, H, C))
        return gat_layer(h, src, dst, W2, a_src2, a_dst2, b2, 1, F_DIM)

    def _L0_ffn_ref(x, Wr, br, W1, b1, g1, be1, m1, v1, W2, b2, g2, be2, m2, v2, Wo, bo):
        import jax, jax.numpy as jnp
        import numpy as np
        BN_EPS = 0.001

        def _bn(h, g, b, m, v):
            return g * (h - m) * jax.lax.rsqrt(v + BN_EPS) + b
        feat = jnp.mean(x, axis=0)
        w = jax.nn.softmax(feat @ Wr + br, axis=-1)
        h = jnp.einsum('bfd,edh->bfeh', x, W1) + b1
        h = jax.nn.relu(_bn(h, g1, be1, m1, v1))
        h = jnp.einsum('bfeh,ehk->bfek', h, W2) + b2
        h = jax.nn.relu(_bn(h, g2, be2, m2, v2))
        y = jnp.einsum('bfeh,ehd->bfed', h, Wo) + bo
        return jnp.einsum('bfed,fe->bfd', y, w)
    edge_index = jnp.stack([src, dst])
    x = x + _L0_gnn_ref(_layernorm(x, axis=-1), edge_index, L0_gnn_W1, L0_gnn_a_src1, L0_gnn_a_dst1, L0_gnn_b1, L0_gnn_W2, L0_gnn_a_src2, L0_gnn_a_dst2, L0_gnn_b2)
    x = x + _L0_ffn_ref(_layernorm(x, axis=-1)[None], L0_ffn_Wr, L0_ffn_br, L0_ffn_W1, L0_ffn_b1, L0_ffn_g1, L0_ffn_be1, L0_ffn_m1, L0_ffn_v1, L0_ffn_W2, L0_ffn_b2, L0_ffn_g2, L0_ffn_be2, L0_ffn_m2, L0_ffn_v2, L0_ffn_Wo, L0_ffn_bo)[0]
    return x

_drawn_inputs = setup_inputs


def setup_inputs(seed=0):
    import zlib

    import numpy as np

    out = dict(_drawn_inputs(seed))
    spreads = {'L0_gnn_b1': (0.0, 0.1),
     'L0_gnn_b2': (0.0, 0.1),
     'L0_ffn_br': (0.0, 0.1),
     'L0_ffn_b1': (0.0, 0.324),
     'L0_ffn_g1': (1.0, 0.2),
     'L0_ffn_be1': (0.0, 0.333),
     'L0_ffn_m1': (0.0, 0.321),
     'L0_ffn_v1': (1.0, 0.6),
     'L0_ffn_b2': (0.0, 0.1),
     'L0_ffn_g2': (1.0, 0.2),
     'L0_ffn_be2': (0.0, 0.1),
     'L0_ffn_m2': (0.0, 0.1),
     'L0_ffn_v2': (1.0, 0.558),
     'L0_ffn_bo': (0.0, 0.1)}
    factors = {'L0_gnn_a_src1': 3.208,
     'L0_gnn_a_dst1': 8.0,
     'L0_gnn_a_src2': 8.0,
     'L0_gnn_a_dst2': 31.658}
    for name, (base, spread) in spreads.items():
        noise = np.random.default_rng([zlib.crc32(name.encode()), seed]).standard_normal(out[name].shape)
        drawn = base * np.exp(spread * noise) if base else spread * noise
        out[name] = jnp.asarray(drawn.astype(out[name].dtype))
    for name, factor in factors.items():
        out[name] = (out[name] * factor).astype(out[name].dtype)
    return out
```

```python
from contextlib import ExitStack

import numpy as np

import concourse.bass as bass
from concourse import mybir

F32 = mybir.dt.float32
F32R = mybir.dt.float32r
BF16 = mybir.dt.bfloat16
I32 = mybir.dt.int32
ALU = mybir.AluOpType
ACT = mybir.ActivationFunctionType
AX = mybir.AxisListType

P = 128
LN_EPS = 1e-5
BN_EPS = 1e-3
SLOPE = 0.2

BATCH = 8
BODY = 80
RING = 40
ACC_BANKS = 4


def build_program(nc, x, src, dst, gnn, ffn, out):
    N, F = x.shape
    E = src.shape[0]
    NT = -(-N // P)
    LAST = N - (NT - 1) * P
    ET = -(-E // P)
    EG = -(-ET // P)
    STEPS = -(-(ET + NT - 1) // BODY) * BODY
    ITERS = STEPS // BODY
    NB = BODY // BATCH
    RB = RING // BATCH
    KC = F // P
    HEADS = [gnn[0]["a_src"].shape[0], gnn[1]["a_src"].shape[0]]
    HMAX = max(HEADS)
    ROW = F + 2 * HMAX
    X = ffn["Wr"].shape[1]
    TB = 7
    assert NT % TB == 0 and N == (NT - 1) * P + LAST and KC == 2
    SC = STEPS // 2
    SG = -(-STEPS // P)

    rows_dram = [nc.dram_tensor(f"node_rows_{l}", [NT * P, ROW], F32, kind="Internal").ap() for l in (0, 1)]
    place_dram = nc.dram_tensor("edge_places", [STEPS, P], BF16, kind="Internal").ap()

    root = ExitStack()
    with root:
        def scope_tools(ctx):
            def sb(name, shape, dt=F32):
                return ctx.enter_context(nc.sbuf_tensor(name, shape, dt))

            def sem(name):
                return ctx.enter_context(nc.semaphore(name))

            return sb, sem

        sb, sem = scope_tools(root)
        ps = root.enter_context(nc.psum_tensor("ps", [P, 8, 512], F32))
        ident = sb("ident", [P, P])
        acc = sb("acc", [P, NT, ROW])
        bias_rows = sb("bias_rows", [P, 2, F])

        edges = ExitStack()
        with edges:
            esb, _ = scope_tools(edges)
            step_iota = esb("step_iota", [P, STEPS])
            part_iota = esb("part_iota", [P, 1])
            edge_src = esb("edge_src", [P, STEPS])
            edge_place = esb("edge_place", [P, STEPS])
            step_node = esb("step_node", [1, STEPS], I32)
            w_aug = esb("w_aug", [P, 2, KC, F + 2 * HMAX])
            scores = esb("scores", [P, NT, 2 * HMAX])

            prepare(nc, locals())
            for layer in (0, 1):
                transform(nc, locals(), layer)
                edge_sums(nc, locals(), layer)
        mixture(nc, locals())


def prepare(nc, g):
    P_, E, ET, EG, STEPS, SC, SG, NT, F, KC, HMAX, HEADS = (
        P, g["E"], g["ET"], g["EG"], g["STEPS"], g["SC"], g["SG"], g["NT"], g["F"], g["KC"], g["HMAX"], g["HEADS"])
    ps, ident, acc, bias_rows = g["ps"], g["ident"], g["acc"], g["bias_rows"]
    step_iota, part_iota, w_aug = g["step_iota"], g["part_iota"], g["w_aug"]
    full = ET - (EG - 1) * P - 1
    tail = E - (ET - 1) * P
    pad_node = g["N"]
    assert NT * P > pad_node and full < P
    with ExitStack() as ctx:
        def sb(name, shape, dt=F32):
            return ctx.enter_context(nc.sbuf_tensor(name, shape, dt))

        def sem(name):
            return ctx.enter_context(nc.semaphore(name))

        dst_i = sb("dst_i", [P, EG, P], I32)
        src_i = sb("src_i", [P, EG, P], I32)
        dst_f = sb("dst_f", [P, EG, P])
        src_f = sb("src_f", [P, EG, P])
        ends_i = sb("ends_i", [P, 2, EG], I32)
        ends = sb("ends", [P, 2, EG])
        tile_id = sb("tile_id", [P, EG])
        valid = sb("valid", [P, EG])
        count = sb("count", [P, EG])
        totals = sb("totals", [P, EG])
        before = sb("before", [P, EG])
        base = sb("base", [P, EG])
        limit = sb("limit", [P, EG])
        shift = sb("shift", [P, EG])
        shift128 = sb("shift128", [P, EG])
        node_off = sb("node_off", [P, EG])
        ones_g = sb("ones_g", [P, EG])
        below = sb("below", [P, STEPS])
        sel = sb("sel", [P, EG, STEPS])
        tri = sb("tri", [P, P])
        ones = sb("ones", [P, P])
        block_id = sb("block_id", [P, SG])
        places = sb("places", [P, SG, P], BF16)
        n_sum = sb("n_sum", [1, STEPS])
        n_used = sb("n_used", [1, STEPS])
        a_rows = sb("a_rows", [P, 4, F])
        prod = sb("prod", [P, F])

        s_zero, s_edges, s_w, s_a, s_const, s_pool = (
            sem("blank_tiles"), sem("edges_landed"), sem("weights_landed"), sem("attention_rows_landed"),
            sem("constants_ready"), sem("pool_chain"))
        s_v, s_prefix, s_dve_mid, s_pe, s_places, s_bias = (
            sem("dve_chain"), sem("prefix_ready"), sem("dve_tables"), sem("pe_tables"), sem("places_stored"),
            sem("bias_landed"))
        block = ctx.enter_context(nc.Block())

        @block.sync
        def _(sp):
            sp.wait_ge(s_zero, 2)
            for dram, tile in ((g["dst"], dst_i), (g["src"], src_i)):
                whole = (EG - 1) * P * P
                sp.dma_start(tile[:, 0:EG - 1, :],
                             dram[0:whole].rearrange("(g q p) -> q g p", q=P, p=P)).then_inc(s_edges, 16)
                sp.dma_start(tile[0:full, EG - 1, :],
                             dram[whole:whole + full * P].rearrange("(q p) -> q p", p=P)).then_inc(s_edges, 16)
                sp.dma_start(tile[full:full + 1, EG - 1, 0:tail],
                             dram[whole + full * P:E].rearrange("(a p) -> a p", a=1)).then_inc(s_edges, 16)
            for l in (0, 1):
                sp.dma_start(w_aug[:, l, :, 0:F],
                             g["gnn"][l]["W"].rearrange("(k p) n -> p k n", p=P)).then_inc(s_w, 16)
                for n, name in enumerate(("a_src", "a_dst")):
                    sp.dma_start(a_rows[:, 2 * l + n, :],
                                 g["gnn"][l][name].rearrange("h c -> (h c)").partition_broadcast(P)
                                 ).then_inc(s_a, 16)
                sp.dma_start(bias_rows[:, l, :], g["gnn"][l]["b"].partition_broadcast(P)).then_inc(s_bias, 16)
            sp.wait_ge(s_bias, 32)
            sp.wait_ge(s_dve_mid, 4)
            rest = STEPS - (SG - 1) * P
            sp.dma_start(g["place_dram"][0:(SG - 1) * P, :].rearrange("(g q) p -> q g p", q=P),
                         places[:, 0:SG - 1, :]).then_inc(s_places, 16)
            sp.dma_start(g["place_dram"][(SG - 1) * P:STEPS, :], places[0:rest, SG - 1, :]).then_inc(s_places, 16)
            sp.wait_ge(s_places, 32)

        @block.gpsimd
        def _(pool):
            pool.memset(dst_i[:, EG - 1, :], pad_node).then_inc(s_zero, 1)
            pool.memset(src_i[:, EG - 1, :], 0).then_inc(s_zero, 1)
            pool.memset(ident[:, :], 0.0).then_inc(s_pool, 1)
            pool.memset(ones[:, :], 1.0).then_inc(s_pool, 1)
            pool.wait_ge(s_pool, 2)
            pool.affine_select(out=ident[:, :], in_=ident[:, :], compare_op=ALU.not_equal, fill=1.0, base=0,
                               pattern=[[-1, P]], channel_multiplier=1).then_inc(s_const, 1)
            pool.affine_select(out=tri[:, :], in_=ones[:, :], compare_op=ALU.is_gt, fill=0.0, base=0,
                               pattern=[[1, P]], channel_multiplier=-1).then_inc(s_const, 1)
            pool.iota(step_iota[:, :], [[1, STEPS]], base=0, channel_multiplier=0,
                      allow_small_or_imprecise_dtypes=True).then_inc(s_const, 1)
            pool.iota(part_iota[:, :], [[1, 1]], base=0, channel_multiplier=1,
                      allow_small_or_imprecise_dtypes=True).then_inc(s_const, 1)
            pool.iota(tile_id[:, :], [[P, EG]], base=0, channel_multiplier=1,
                      allow_small_or_imprecise_dtypes=True).then_inc(s_const, 1)
            pool.iota(block_id[:, :], [[P, SG]], base=0, channel_multiplier=1,
                      allow_small_or_imprecise_dtypes=True).then_inc(s_const, 1)

        @block.vector
        def _(dve):
            done = [0]

            def then(ins):
                done[0] += 1
                ins.then_inc(s_v, 1)
                dve.wait_ge(s_v, done[0])

            then(nc.vector.memset(acc[:, :, :], 1.0))
            then(nc.vector.memset(ones_g[:, :], 1.0))
            dve.wait_ge(s_edges, 96)
            dve.wait_ge(s_const, 6)
            then(nc.vector.tensor_copy(dst_f[:, :, :], dst_i[:, :, :]))
            nc.vector.tensor_copy(src_f[:, :, :], src_i[:, :, :])
            shift_bits = int(np.log2(P))
            nc.vector.tensor_scalar(ends_i[:, 0, :], dst_i[:, :, 0], shift_bits, None, ALU.logical_shift_right)
            then(nc.vector.tensor_scalar(ends_i[:, 1, :], dst_i[:, :, P - 1], shift_bits, None,
                                         ALU.logical_shift_right))
            then(nc.vector.tensor_copy(ends[:, :, :], ends_i[:, :, :]))
            then(nc.vector.tensor_scalar(valid[:, :], tile_id[:, :], float(ET), None, ALU.is_lt))
            then(nc.vector.tensor_tensor(count[:, :], ends[:, 1, :], ends[:, 0, :], ALU.subtract))
            nc.vector.scalar_tensor_tensor(count[:, :], count[:, :], 1.0, valid[:, :], ALU.add, ALU.mult
                                           ).then_inc(s_dve_mid, 1)
            dve.wait_ge(s_dve_mid, 1)
            dve.wait_ge(s_prefix, 1)
            then(nc.vector.tensor_copy(totals[:, :], ps[:, 1, 0:EG]))
            then(nc.vector.tensor_tensor_scan(before[:, :], ones_g[:, :], totals[:, :], 0.0, ALU.mult, ALU.add))
            then(nc.vector.tensor_tensor(before[:, :], before[:, :], totals[:, :], ALU.subtract))
            then(nc.vector.tensor_tensor(base[:, :], ps[:, 0, 0:EG], before[:, :], ALU.add))
            then(nc.vector.tensor_tensor(limit[:, :], base[:, :], count[:, :], ALU.add))
            then(nc.vector.tensor_tensor(shift[:, :], ends[:, 0, :], base[:, :], ALU.subtract))
            then(nc.vector.tensor_scalar(shift128[:, :], shift[:, :], float(P), None, ALU.mult))
            then(nc.vector.tensor_scalar(node_off[:, :], shift[:, :], float(NT - 1), None, ALU.subtract))
            for e in range(EG):
                then(nc.vector.tensor_scalar(dst_f[:, e, :], dst_f[:, e, :], shift128[:, e:e + 1], None,
                                             ALU.subtract))
                then(nc.vector.tensor_scalar(below[:, :], step_iota[:, :], base[:, e:e + 1], None, ALU.is_ge))
                then(nc.vector.scalar_tensor_tensor(sel[:, e, :], step_iota[:, :], limit[:, e:e + 1],
                                                    below[:, :], ALU.is_lt, ALU.mult))
            dve.sem_inc(s_dve_mid, 1)
            dve.wait_ge(s_w, 32)
            dve.wait_ge(s_a, 64)
            for l, H in enumerate(HEADS):
                for k in range(KC):
                    for n in (0, 1):
                        then(nc.vector.tensor_tensor(prod[:, :], w_aug[:, l, k, 0:F], a_rows[:, 2 * l + n, :],
                                                     ALU.mult))
                        then(nc.vector.tensor_reduce(w_aug[:, l, k, F + n * H:F + (n + 1) * H],
                                                     prod[:, :].rearrange("p (h c) -> p h c", h=H), AX.X, ALU.add))
            dve.wait_ge(s_pe, 1)
            for c in (0, 1):
                cols = slice(c * SC, (c + 1) * SC)
                nc.vector.tensor_copy(g["edge_src"][:, cols], ps[:, c, 0:SC])
                nc.vector.scalar_tensor_tensor(g["edge_place"][:, cols], step_iota[:, cols], -float(P),
                                               ps[:, 2 + c, 0:SC], ALU.mult, ALU.add)
                nc.vector.tensor_copy(n_sum[:, cols], ps[0:1, 4 + c, 0:SC])
                then(nc.vector.tensor_copy(n_used[:, cols], ps[0:1, 6 + c, 0:SC]))
            then(nc.vector.tensor_tensor(n_used[:, :], n_used[:, :], step_iota[0:1, :], ALU.mult))
            then(nc.vector.tensor_tensor(n_sum[:, :], n_sum[:, :], n_used[:, :], ALU.add))
            nc.vector.tensor_scalar(g["step_node"][:, :], n_sum[:, :], float(NT - 1), None, ALU.add)
            then(nc.vector.tensor_scalar(block_id[:, :], block_id[:, :], float(P), None, ALU.mult))
            dve.sem_inc(s_dve_mid, 1)
            dve.wait_ge(s_pe, 2)
            for q in range(SG):
                rows = min(P, STEPS - q * P)
                last = nc.vector.tensor_scalar(places[0:rows, q, :], ps[0:rows, q // 4, (q % 4) * P:(q % 4 + 1) * P],
                                               block_id[0:rows, q:q + 1], None, ALU.subtract)
            last.then_inc(s_dve_mid, 1)

        @block.tensor
        def _(pe):
            pe.wait_ge(s_const, 6)
            pe.wait_ge(s_dve_mid, 1)
            nc.tensor.matmul(ps[:, 0, 0:EG], tri[:, :], count[:, :], start=True, stop=True)
            nc.tensor.matmul(ps[:, 1, 0:EG], ones[:, :], count[:, :], start=True, stop=True).then_inc(s_prefix, 1)
            pe.wait_ge(s_dve_mid, 2)
            for c in (0, 1):
                for e in range(EG):
                    first, last = e == 0, e == EG - 1
                    pick = sel[:, e, c * SC:(c + 1) * SC]
                    nc.tensor.matmul(ps[:, c, 0:SC], src_f[:, e, :], pick, start=first, stop=last)
                    nc.tensor.matmul(ps[:, 2 + c, 0:SC], dst_f[:, e, :], pick, start=first, stop=last)
                    nc.tensor.matmul(ps[0:1, 4 + c, 0:SC], node_off[:, e:e + 1], pick, start=first, stop=last)
                    mm = nc.tensor.matmul(ps[0:1, 6 + c, 0:SC], ones_g[:, 0:1], pick, start=first, stop=last)
            mm.then_inc(s_pe, 1)
            pe.wait_ge(s_dve_mid, 3)
            for q in range(SG):
                rows = min(P, STEPS - q * P)
                for e in range(EG):
                    mm = nc.tensor.matmul(ps[0:rows, q // 4, (q % 4) * P:(q % 4 + 1) * P],
                                          sel[:, e, q * P:q * P + rows], dst_f[:, e, :],
                                          start=e == 0, stop=e == EG - 1)
            mm.then_inc(s_pe, 1)


def transform(nc, g, layer):
    N, F, NT, LAST, KC, ROW, TB, HMAX = (g[k] for k in ("N", "F", "NT", "LAST", "KC", "ROW", "TB", "HMAX"))
    H = g["HEADS"][layer]
    C = F // H
    ps, ident, acc, bias_rows, w_aug, scores = (g[k] for k in ("ps", "ident", "acc", "bias_rows", "w_aug", "scores"))
    x, rows_dram = g["x"], g["rows_dram"][layer]
    with ExitStack() as ctx:
        def sb(name, shape, dt=F32):
            return ctx.enter_context(nc.sbuf_tensor(f"{name}{layer}", shape, dt))

        def sem(name):
            return ctx.enter_context(nc.semaphore(f"{name}{layer}"))

        inp = sb("t_in", [P, TB, F])
        xn = sb("t_norm", [P, TB, F])
        neg = sb("t_neg", [P, TB, F])
        pos = sb("t_pos", [P, TB, F])
        stats = sb("t_stats", [P, TB, 6])
        mv = sb("t_mv", [P, TB, 2])
        rstd = sb("t_rstd", [P, TB, 1])
        eps = sb("t_eps", [P, 1])
        ones_col = sb("t_ones", [P, 1])
        xT = sb("t_xT", [P, 2, KC, P])
        zinv = sb("t_zinv", [P, TB, HMAX])

        s_in = [sem(f"t_landed{j}_") for j in range(TB)]
        s_eps = sem("t_eps_set")
        s_turn = sem("t_turn")
        s_var = sem("t_var_ready")
        s_std = sem("t_std_ready")
        s_c = sem("t_dve_chain")
        s_act = sem("t_act_done")
        s_pool = sem("t_pool_done")
        s_xn = sem("t_norm_ready")
        s_tr = sem("t_transposed")
        s_xT = sem("t_xT_ready")
        s_mm = sem("t_product_ready")
        s_row = sem("t_row_copied")
        s_sco = sem("t_scores_copied")
        s_asco = sem("t_row_scores")
        s_store = sem("t_rows_stored")
        block = ctx.enter_context(nc.Block())
        R = NT // TB
        tail_rows = LAST

        @block.sync
        def _(sp):
            if layer == 0:
                def load(i, last=False):
                    for j in range(TB):
                        sp.wait_ge(s_xn, i * TB + j + 1)
                        if last and j == TB - 1:
                            sp.dma_start(inp[0:tail_rows, j, :], x[(NT - 1) * P:N, :]).then_inc(s_in[j], 16)
                        else:
                            sp.dma_start(inp[:, j, :], x[bass.ds((i * TB + j) * P, P), :]).then_inc(s_in[j], 16)

                with sp.Fori(0, R - 1) as i:
                    load(i)
                load(R - 1, last=True)

        @block.gpsimd
        def _(pool):
            def store(i):
                pool.wait_ge(s_row, (i + 1) * TB)
                pool.wait_ge(s_sco, (i + 1) * TB)
                nc.gpsimd.tensor_copy(acc[:, bass.ds(i * TB, TB), F + H:F + 2 * H],
                                      scores[:, bass.ds(i * TB, TB), 0:H]).then_inc(s_asco, 1)
                pool.wait_ge(s_asco, i + 1)
                pool.dma_start(rows_dram.rearrange("(n p) c -> p n c", p=P)[:, bass.ds(i * TB, TB), :],
                               acc[:, bass.ds(i * TB, TB), :]).then_inc(s_store, 16)

            with pool.Fori(0, R) as i:
                if layer == 1:
                    pool.wait_ge(s_c, i * 3 + 2)
                    nc.gpsimd.tensor_tensor(pos[:, :, :], inp[:, :, :],
                                            bias_rows[:, 0, :].unsqueeze(1).to_broadcast([P, TB, F]),
                                            ALU.add).then_inc(s_pool, 1)
                store(i)
            pool.wait_ge(s_store, 16 * R)

        @block.scalar
        def _(act):
            with act.Fori(0, R) as i:
                if layer == 0:
                    act.wait_ge(s_eps, 1)
                    act.wait_ge(s_var, i + 1)
                    nc.scalar.activation(rstd[:, :, :], mv[:, :, 1:2], ACT.Sqrt, bias=eps[:, 0:1]).then_inc(s_std, 1)
                else:
                    act.wait_ge(s_c, i * 3 + 3)
                    nc.scalar.activation(neg[:, :, :], neg[:, :, :], ACT.Exp).then_inc(s_act, 1)
                for j in range(TB):
                    act.wait_ge(s_mm, i * TB + j + 1)
                    nc.scalar.activation(
                        acc[:, bass.ds(i * TB + j, 1), 0:F + H].rearrange("p a (h c) -> p (a h) c", h=H)[:, :, 0:C],
                        ps[:, 2 + j % 2, 0:F].rearrange("p (h c) -> p h c", h=H), ACT.Copy).then_inc(s_row, 1)

        @block.vector
        def _(dve):
            if layer == 0:
                nc.vector.memset(eps[:, :], LN_EPS).then_inc(s_eps, 1)
            else:
                nc.vector.memset(ones_col[:, :], 1.0).then_inc(s_eps, 1)
                dve.wait_ge(s_eps, 1)

            dve.sem_inc(s_xn, TB)

            def tile_products(i, j):
                n = i * TB + j
                dve.wait_ge(s_tr, n + 1)
                nc.vector.tensor_copy(xT[:, j % 2, :, :],
                                      ps[:, j % 2, 0:KC * P].rearrange("p (k q) -> p k q", k=KC)).then_inc(s_xT, 1)
                dve.wait_ge(s_mm, n + 1)
                nc.vector.tensor_copy(scores[:, bass.ds(n, 1), 0:2 * H],
                                      ps[:, 4 + j % 2, 0:2 * H].unsqueeze(1)).then_inc(s_sco, 1)

            def body(i, last=False):
                if layer == 0:
                    for j in range(TB):
                        dve.wait_ge(s_in[j], i * 16 + 16)
                        dve.sem_inc(s_turn, 1)
                        nc.vector.bn_stats(stats[:, j, :], inp[:, j, :]).then_inc(s_c, 1)
                    for j in range(TB):
                        dve.wait_ge(s_c, i * (TB + 1) + j + 1)
                        dve.sem_inc(s_turn, 1)
                        ins = nc.vector.bn_aggr(mv[:, j, :], stats[:, j, :])
                    ins.then_inc(s_var, 1)
                    dve.wait_ge(s_std, i + 1)
                    nc.vector.reciprocal(rstd[:, :, :], rstd[:, :, :]).then_inc(s_c, 1)
                    dve.wait_ge(s_c, (i + 1) * (TB + 1))
                    for j in range(TB):
                        nc.vector.tensor_scalar(xn[:, j, :], inp[:, j, :], mv[:, j, 0:1], rstd[:, j, :],
                                                ALU.subtract, ALU.mult).then_inc(s_xn, 1)
                else:
                    H0 = g["HEADS"][0]
                    C0 = F // H0
                    sums = acc[:, bass.ds(i * TB, TB), 0:F + H0].rearrange("p n (h c) -> p n h c", h=H0)
                    nc.vector.reciprocal(zinv[:, :, 0:H0], sums[:, :, :, C0]).then_inc(s_c, 1)
                    dve.wait_ge(s_c, i * 3 + 1)
                    for j in range(TB):
                        one = acc[:, bass.ds(i * TB + j, 1), 0:F + H0].rearrange("p a (h c) -> p (a h) c", h=H0)
                        ins = nc.vector.tensor_tensor(
                            inp[:, j, :].rearrange("p (h c) -> p h c", h=H0), one[:, :, 0:C0],
                            zinv[:, j, 0:H0].unsqueeze(2).to_broadcast([P, H0, C0]), ALU.mult)
                    ins.then_inc(s_c, 1)
                    dve.wait_ge(s_pool, i + 1)
                    nc.vector.tensor_scalar(neg[:, :, :], pos[:, :, :], 0.0, None, ALU.min).then_inc(s_c, 1)
                    dve.wait_ge(s_act, i + 1)
                    nc.vector.tensor_scalar(pos[:, :, :], pos[:, :, :], 0.0, -1.0, ALU.max, ALU.add
                                            ).then_inc(s_std, 1)
                    dve.wait_ge(s_std, i + 1)
                    nc.vector.tensor_copy(acc[:, bass.ds(i * TB, TB), F:F + 1],
                                          ones_col[:, :].unsqueeze(1).to_broadcast([P, TB, 1]))
                    for j in range(TB):
                        nc.vector.tensor_tensor(xn[:, j, :], neg[:, j, :], pos[:, j, :], ALU.add).then_inc(s_xn, 1)
                for j in range(TB):
                    tile_products(i, j)

            if layer == 0:
                with dve.Fori(0, R - 1) as i:
                    body(i)
                body(R - 1, last=True)
            else:
                with dve.Fori(0, R) as i:
                    body(i)

        @block.tensor
        def _(pe):
            def transposes(i, j):
                pe.wait_ge(s_xn, TB + i * TB + j + 1)
                for k in range(KC):
                    mm = nc.tensor.transpose(ps[:, j % 2, k * P:(k + 1) * P], xn[:, j, k * P:(k + 1) * P], ident[:, :])
                mm.then_inc(s_tr, 1)

            def product(i, j):
                pe.wait_ge(s_xT, i * TB + j + 1)
                for k in range(KC):
                    nc.tensor.matmul(ps[:, 2 + j % 2, 0:F], xT[:, j % 2, k, :],
                                     w_aug[:, layer, k, 0:F], start=k == 0, stop=k == KC - 1)
                for k in range(KC):
                    mm = nc.tensor.matmul(ps[:, 4 + j % 2, 0:2 * H], xT[:, j % 2, k, :],
                                          w_aug[:, layer, k, F:F + 2 * H], start=k == 0, stop=k == KC - 1)
                mm.then_inc(s_mm, 1)

            with pe.Fori(0, R) as i:
                for j in range(TB):
                    if j >= 2:
                        pe.wait_ge(s_row, i * TB + j - 1)
                    transposes(i, j)
                    product(i, j)


def edge_sums(nc, g, layer):
    F, NT, ROW, STEPS, ITERS, NB, RB, HMAX = (g[k] for k in ("F", "NT", "ROW", "STEPS", "ITERS", "NB", "RB", "HMAX"))
    H = g["HEADS"][layer]
    C = F // H
    W = F + H
    ps, acc, scores = g["ps"], g["acc"], g["scores"]
    edge_src, edge_place, step_node = g["edge_src"], g["edge_place"], g["step_node"]
    step_iota, part_iota = g["step_iota"], g["part_iota"]
    rows_dram = g["rows_dram"][layer]
    PARTS = 3
    M = 2 * H
    GROUP = RING
    GB = GROUP // BATCH
    with ExitStack() as ctx:
        def sb(name, shape, dt=F32):
            return ctx.enter_context(nc.sbuf_tensor(f"{name}{layer}", shape, dt))

        def sem(name):
            return ctx.enter_context(nc.semaphore(f"{name}{layer}"))

        ring = sb("gathered_rows", [P, RING, ROW])
        idx = sb("gather_index", [P, 2, GROUP], I32)
        place_rows = sb("place_rows", [P, 2, BATCH * P], BF16)
        onehot_t = sb("onehot_t", [P, 2, BATCH * P], BF16)
        onehot = sb("onehot", [P, 2, BATCH, P])
        table = sb("node_table", [P, NT, M * PARTS], BF16)
        node_dm = sb("node_dm", [P, NT, M])
        rest1 = sb("rest1", [P, NT, M])
        rest2 = sb("rest2", [P, NT, M])
        self_w = sb("self_w", [P, NT, H])
        self_e = sb("self_e", [P, NT, H])
        top_p = sb("top_p", [P, H])
        top = sb("top", [P, H])
        adm = sb("adm", [P, 2, BATCH, M])
        e_sum = sb("e_sum", [P, 2, BATCH, H])
        e_leaky = sb("e_leaky", [P, 2, BATCH, H])
        e_less = sb("e_less", [P, 2, BATCH, H])
        weight = sb("weight", [P, 2, BATCH, H])

        s_top_p, s_top, s_c, s_self, s_selfw, s_table = (
            sem("top_by_partition"), sem("top_ready"), sem("scalar_chain"), sem("self_scores"), sem("self_weights"),
            sem("table_ready"))
        s_prow = [sem(f"place_rows_landed{n}_") for n in (0, 1)]
        s_idx = sem("index_ready")
        s_turn = sem("gather_turn")
        s_gath = [sem(f"gathered{n}_") for n in range(RB)]
        s_oht = sem("onehot_t_ready")
        s_admp = sem("adm_product_ready")
        s_adm = sem("adm_summed")
        s_e = sem("score_chain")
        s_scores = sem("scores_ready")
        s_w = sem("weights_ready")
        s_oh = sem("onehot_ready")
        s_wt = sem("weighted")
        s_prod = sem("products_ready")
        s_acc = sem("sums_added")
        s_rows_free = sem("place_rows_free")
        block = ctx.enter_context(nc.Block())

        def loop(eng, body):
            with eng.Fori(0, ITERS - 1) as i:
                body(i, False)
            body(ITERS - 1, True)

        @block.sync
        def _(sp):
            def body(i, last):
                for jb in range(NB):
                    b = i * NB + jb
                    sp.wait_ge(s_rows_free, b + 1)
                    rows = g["place_dram"][bass.ds(b * BATCH, BATCH), :].rearrange("s p -> (s p)")
                    sp.dma_start(place_rows[:, jb % 2, :], rows.partition_broadcast(P)).then_inc(s_prow[jb % 2], 16)

            loop(sp, body)

        @block.gpsimd
        def _(pool):
            pool.wait_ge(s_top_p, 1)
            nc.gpsimd.partition_all_reduce(top[:, :], top_p[:, :], P, bass.bass_isa.ReduceOp.max).then_inc(s_top, 1)

            def body(i, last):
                for jb in range(NB):
                    b = i * NB + jb
                    if jb % GB == 0:
                        pool.wait_ge(s_idx, i * (NB // GB) + jb // GB + 1)
                    pool.wait_ge(s_prod, (b + 1) * BATCH)
                    pool.sem_inc(s_turn, 1)
                    for j in range(BATCH):
                        step = jb * BATCH + j
                        nc.gpsimd.indirect_dma_start(
                            ring[:, step % RING, :], None, rows_dram,
                            bass.IndirectOffsetOnAxis(idx[:, step // GROUP % 2, step % GROUP:step % GROUP + 1], 0)
                        ).then_inc(s_gath[jb % RB], 16)

            loop(pool, body)

        @block.scalar
        def _(act):
            def lay_index(group):
                nc.scalar.activation(idx[:, group % 2 if isinstance(group, int) else 0, :],
                                     edge_src[:, bass.ds(group * GROUP, GROUP)], ACT.Copy).then_inc(s_idx, 1)

            nc.scalar.activation(idx[:, 0, :], edge_src[:, 0:GROUP], ACT.Copy).then_inc(s_idx, 1)
            act.wait_ge(s_self, 1)
            nc.scalar.activation(self_w[:, :, :], self_e[:, :, :], ACT.Exp).then_inc(s_selfw, 1)

            def exp(b, jb):
                act.wait_ge(s_scores, b + 1)
                nc.scalar.activation(weight[:, jb % 2, :, :], e_less[:, jb % 2, :, :], ACT.Exp).then_inc(s_w, 1)

            def body(i, last):
                for jb in range(NB):
                    b = i * NB + jb
                    exp(b, jb)
                    if jb % GB == 0:
                        half = jb // GB + 1
                        if not (last and half == NB // GB):
                            group = i * (NB // GB) + half
                            act.wait_ge(s_prod, group * GROUP)
                            nc.scalar.activation(idx[:, half % 2, :], edge_src[:, bass.ds(group * GROUP, GROUP)],
                                                 ACT.Copy).then_inc(s_idx, 1)

            loop(act, body)

        @block.vector
        def _(dve):
            done = [0]

            def then(ins):
                done[0] += 1
                ins.then_inc(s_c, 1)
                dve.wait_ge(s_c, done[0])

            dve.sem_inc(s_acc, ACC_BANKS)
            dve.sem_inc(s_rows_free, 2)
            nc.vector.tensor_reduce(top_p[:, :], scores[:, :, 0:H].rearrange("p n h -> p h n"), AX.X, ALU.max
                                    ).then_inc(s_top_p, 1)
            dve.wait_ge(s_top, 1)
            then(nc.vector.tensor_tensor(rest1[:, :, 0:H], scores[:, :, H:M],
                                         top[:, :].unsqueeze(1).to_broadcast([P, NT, H]), ALU.add))
            nc.vector.tensor_copy(node_dm[:, :, 0:H], scores[:, :, H:M])
            then(nc.vector.scalar_tensor_tensor(node_dm[:, :, H:M], rest1[:, :, 0:H], SLOPE, rest1[:, :, 0:H],
                                                ALU.mult, ALU.max))
            then(nc.vector.tensor_tensor(self_e[:, :, :], scores[:, :, 0:H], scores[:, :, H:M], ALU.add))
            then(nc.vector.scalar_tensor_tensor(self_e[:, :, :], self_e[:, :, :], SLOPE, self_e[:, :, :],
                                                ALU.mult, ALU.max))
            nc.vector.tensor_tensor(self_e[:, :, :], self_e[:, :, :], node_dm[:, :, H:M], ALU.subtract
                                    ).then_inc(s_self, 1)
            parts = table[:, :, :].rearrange("p n (m q) -> p n m q", q=PARTS)
            then(nc.vector.tensor_copy(parts[:, :, :, 0], node_dm[:, :, :]))
            then(nc.vector.tensor_tensor(rest1[:, :, :], node_dm[:, :, :], parts[:, :, :, 0], ALU.subtract))
            then(nc.vector.tensor_copy(parts[:, :, :, 1], rest1[:, :, :]))
            then(nc.vector.tensor_tensor(rest2[:, :, :], rest1[:, :, :], parts[:, :, :, 1], ALU.subtract))
            nc.vector.tensor_copy(parts[:, :, :, 2], rest2[:, :, :]).then_inc(s_table, 1)
            dve.wait_ge(s_selfw, 1)
            loops = acc[:, :, 0:W].rearrange("p n (h c) -> p n h c", h=H)
            if H == 1:
                then(nc.vector.tensor_tensor(acc[:, :, 0:W], acc[:, :, 0:W],
                                             self_w[:, :, :].to_broadcast([P, NT, W]), ALU.mult))
            else:
                then(nc.vector.tensor_tensor(loops, loops, self_w[:, :, :].unsqueeze(3).to_broadcast(
                    [P, NT, H, W // H]), ALU.mult))

            def slots(jb):
                first = jb % RB * BATCH
                return ring[:, first:first + BATCH, :]

            def prep(b, jb, piece, i=None):
                h = jb % 2
                if piece == 0:
                    dve.wait_ge(s_prow[h], (b * 8 + 16 if isinstance(b, int) and b % 2 == 0 else None) or
                                (b // 2 + 1) * 16 if isinstance(b, int) else (i * (NB // 2) + jb // 2 + 1) * 16)
                    nc.vector.tensor_scalar(onehot_t[:, h, :], place_rows[:, h, :], part_iota[:, 0:1], None,
                                            ALU.is_equal).then_inc(s_oht, 1)
                if piece == 1:
                    places = edge_place[:, bass.ds(b * BATCH, BATCH)]
                    nc.vector.tensor_tensor(onehot[:, h, :, :],
                                            step_iota[:, 0:P].unsqueeze(1).to_broadcast([P, BATCH, P]),
                                            places.unsqueeze(2).to_broadcast([P, BATCH, P]), ALU.is_equal
                                            ).then_inc(s_oh, 1)
                    dve.wait_ge(s_oht, b + 1)
                    dve.sem_inc(s_rows_free, 1)
                if piece == 2:
                    dve.wait_ge(s_admp, b + 1)
                    nc.vector.tensor_reduce(
                        adm[:, h, :, :], ps[:, 4 + h, 0:BATCH * M * PARTS].rearrange("p (s m q) -> p s m q", s=BATCH, q=PARTS),
                        AX.X, ALU.add).then_inc(s_adm, 1)
                if piece == 3:
                    dve.wait_ge(s_gath[jb % RB], (b // RB + 1) * 16 * BATCH if isinstance(b, int)
                                else (i * (NB // RB) + jb // RB + 1) * 16 * BATCH)
                    dve.wait_ge(s_adm, b + 1)
                    nc.vector.tensor_tensor(e_sum[:, h, :, :], slots(jb)[:, :, F + H:F + 2 * H], adm[:, h, :, 0:H],
                                            ALU.add).then_inc(s_e, 1)
                if piece == 4:
                    dve.wait_ge(s_e, 2 * b + 1)
                    nc.vector.scalar_tensor_tensor(e_leaky[:, h, :, :], e_sum[:, h, :, :], SLOPE, e_sum[:, h, :, :],
                                                   ALU.mult, ALU.max).then_inc(s_e, 1)
                if piece == 5:
                    dve.wait_ge(s_e, 2 * b + 2)
                    nc.vector.tensor_tensor(e_less[:, h, :, :], e_leaky[:, h, :, :], adm[:, h, :, H:M], ALU.subtract
                                            ).then_inc(s_scores, 1)
                if piece == 7:
                    dve.wait_ge(s_w, b + 1)
                    if H == 1:
                        dve.wait_ge(s_oh, b + 1)
                        nc.vector.tensor_tensor(onehot[:, h, :, :], onehot[:, h, :, :],
                                                weight[:, h, :, :].to_broadcast([P, BATCH, P]), ALU.mult
                                                ).then_inc(s_wt, 1)
                    else:
                        rows = slots(jb)[:, :, 0:W].rearrange("p s (h c) -> p s h c", h=H)
                        nc.vector.tensor_tensor(rows, rows, weight[:, h, :, :].unsqueeze(3).to_broadcast(
                            [P, BATCH, H, W // H]), ALU.mult).then_inc(s_wt, 1)

            for piece in range(BATCH):
                prep(0, 0, piece)

            def body(i, last):
                for jb in range(NB):
                    b = i * NB + jb
                    _, nodes = nc.values_load_multi_w_load_instructions(
                        step_node[0:1, bass.ds(b * BATCH, BATCH)], engines=[dve.engine], min_val=0, max_val=NT - 1,
                        skip_runtime_bounds_check_because="prepare() keeps it to the node tiles")
                    for j in range(BATCH):
                        if not (last and jb == NB - 1):
                            nj = jb + 1
                            ni = i if nj < NB else i + 1
                            prep(b + 1, nj % NB, j, ni)
                        s = b * BATCH + j
                        sums = acc[:, bass.ds(nodes[j], 1), 0:W].rearrange("p a c -> p (a c)")
                        dve.wait_ge(s_prod, RING + s + 1)
                        dve.wait_ge(s_acc, ACC_BANKS + s)
                        nc.vector.tensor_tensor(sums, ps[:, j % ACC_BANKS, 0:W], sums, ALU.add).then_inc(s_acc, 1)

            loop(dve, body)

        @block.tensor
        def _(pe):
            pe.sem_inc(s_prod, RING)
            pe.wait_ge(s_table, 1)

            def adm_products(b, jb):
                _, nodes = nc.values_load_multi_w_load_instructions(
                    step_node[0:1, bass.ds(b * BATCH, BATCH)], engines=[pe.engine], min_val=0, max_val=NT - 1,
                    skip_runtime_bounds_check_because="prepare() keeps it to the node tiles")
                pe.wait_ge(s_oht, b + 1)
                for j in range(BATCH):
                    mm = nc.tensor.matmul(ps[:, 4 + jb % 2, j * M * PARTS:(j + 1) * M * PARTS],
                                          onehot_t[:, jb % 2, j * P:(j + 1) * P],
                                          table[:, bass.ds(nodes[j], 1), 0:M * PARTS].rearrange("p a c -> p (a c)"),
                                          start=True, stop=True)
                mm.then_inc(s_admp, 1)

            adm_products(0, 0)

            def body(i, last):
                for jb in range(NB):
                    b = i * NB + jb
                    for j in range(BATCH):
                        s = b * BATCH + j
                        if j == 0:
                            pe.wait_ge(s_wt, b + 1)
                            pe.wait_ge(s_oh, b + 1)
                        pe.wait_ge(s_acc, s + 1)
                        nc.tensor.matmul(ps[:, j % ACC_BANKS, 0:W], onehot[:, jb % 2, j, :],
                                         ring[:, (jb * BATCH + j) % RING, 0:W], start=True, stop=True
                                         ).then_inc(s_prod, 1)
                        if j == 1 and not (last and jb == NB - 1):
                            adm_products(b + 1, (jb + 1) % NB)

            loop(pe, body)


def mixture(nc, g):
    N, F, NT, LAST, KC, ROW, X = (g[k] for k in ("N", "F", "NT", "LAST", "KC", "ROW", "X"))
    ps, ident, acc, bias_rows = g["ps"], g["ident"], g["acc"], g["bias_rows"]
    ffn, x, out = g["ffn"], g["x"], g["out"]
    GT = 4
    TOK = GT * P
    GROUPS = (NT - 1) // GT
    assert NT - 1 == GROUPS * GT
    with ExitStack() as ctx:
        def sb(name, shape, dt=F32):
            return ctx.enter_context(nc.sbuf_tensor(f"m_{name}", shape, dt))

        def sem(name):
            return ctx.enter_context(nc.semaphore(f"m_{name}"))

        w_hi = sb("w_hi", [P, 3, X, KC, F], F32R)
        w_lo = sb("w_lo", [P, 3, X, KC, F], F32R)
        h_hi = sb("h_hi", [P, 2, 2, KC, TOK], F32R)
        h_lo = sb("h_lo", [P, 2, 2, KC, TOK], F32R)
        h_f = sb("h_f", [P, 2, TOK])
        x_hi = sb("x_hi", [P, KC, TOK], F32R)
        x_lo = sb("x_lo", [P, KC, TOK], F32R)
        xn = sb("xn", [P, GT, F])
        bn = sb("bn", [P, 2, 5, KC, X])
        bn_s = sb("bn_s", [P, 2, KC, X])
        bn_t = sb("bn_t", [P, 2, KC, X])
        wr = sb("wr", [P, KC, X])
        br = sb("br", [P, X])
        bo = sb("bo", [X, F])
        stats = sb("stats", [P, GT, 6])
        mv = sb("mv", [P, GT, 2])
        rstd = sb("rstd", [P, GT, 1])
        eps = sb("eps", [P, 2])
        zinv = sb("zinv", [P, GT, 1])
        logit = sb("logit", [P, GT, X])
        lmax = sb("lmax", [P, GT, 1])
        lsum = sb("lsum", [P, GT, 1])
        prob = sb("prob", [P, GT, X])
        probT = sb("probT", [X, GT, P])
        w_raw = sb("w_raw", [P, 2, KC, F])
        x_in = xn

        s_turn = sem("turn")
        s_small, s_eps, s_bnc, s_bnq = sem("small_landed"), sem("eps_set"), sem("bn_chain"), sem("bn_sqrt")
        s_raw = [sem("raw_landed0"), sem("raw_landed1")]
        s_whi, s_wlo = sem("w_hi_ready"), sem("w_lo_ready")
        s_x = sem("x_landed")
        s_c, s_sq, s_xn, s_tr = sem("dve_chain"), sem("std_ready"), sem("norm_ready"), sem("transposed")
        s_xhi, s_xlo, s_xf = sem("x_hi_ready"), sem("x_lo_ready"), sem("xT_ready")
        s_log, s_lm, s_ex, s_pr, s_pt, s_ptc, s_bop, s_yin = (
            sem("logits_ready"), sem("logits_less_max"), sem("router_exp"), sem("prob_ready"), sem("prob_transposed"),
            sem("probT_ready"), sem("bias_product"), sem("bias_added"))
        s_h, s_hf, s_hhi, s_hlo = sem("hidden_product"), sem("hidden_ready"), sem("hidden_hi"), sem("hidden_lo")
        s_y, s_ya, s_out = sem("y_product"), sem("y_added"), sem("stored")
        block = ctx.enter_context(nc.Block())
        names = (("b1", "g1", "be1", "m1", "v1"), ("b2", "g2", "be2", "m2", "v2"))
        CH = 2 * KC * X
        NSM = 2 * 5 * KC * X + 3 + KC - 1

        def group_loop(eng, body):
            with eng.Fori(0, GROUPS) as i:
                body(i, GT)
            body(GROUPS, 1)

        order = []
        for t in range(X + 2):
            for m, e in ((0, t), (1, t - 1), (2, t - 2)):
                if 0 <= e < X:
                    order.append((m, e))
        hidden = [(m, e, c) for m, e in order if m < 2 for c in range(KC)]
        rank = {k: n for n, k in enumerate(hidden)}

        @block.sync
        def _(sp):
            for l in (0, 1):
                for n, name in enumerate(names[l]):
                    for k in range(KC):
                        for e in range(X):
                            sp.dma_start(bn[:, l, n, k, e:e + 1],
                                         ffn[name][e, k * P:(k + 1) * P].rearrange("(p a) -> p a", a=1)
                                         ).then_inc(s_small, 16)
            for k in range(KC):
                sp.dma_start(wr[:, k, :], ffn["Wr"][k * P:(k + 1) * P, :]).then_inc(s_small, 16)
            sp.dma_start(br[:, :], ffn["br"].partition_broadcast(P)).then_inc(s_small, 16)
            sp.dma_start(bo[:, :], ffn["bo"]).then_inc(s_small, 16)

            def body(i, tiles):
                if tiles == 1:
                    sp.wait_ge(s_tr, (GROUPS + 1) * KC)
                    sp.dma_start(x_in[0:LAST, 0, :], x[(NT - 1) * P:N, :]).then_inc(s_x, 16)
                else:
                    sp.wait_ge(s_tr, (i + 1) * KC)
                    sp.dma_start(x_in[:, :, :], x[bass.ds(i * TOK, TOK), :].rearrange("(n p) f -> p n f", p=P)
                                 ).then_inc(s_x, 16)
                sp.wait_ge(s_ya, i * GT * X + tiles * X)
                if tiles == 1:
                    sp.dma_start(out[(NT - 1) * P:N, :], acc[0:LAST, NT - 1, 0:F]).then_inc(s_out, 16)
                else:
                    sp.dma_start(out[bass.ds(i * TOK, TOK), :].rearrange("(n p) f -> p n f", p=P),
                                 acc[:, bass.ds(i * GT, GT), 0:F]).then_inc(s_out, 16)

            group_loop(sp, body)
            sp.wait_ge(s_out, 16 * (GROUPS + 1))

        @block.gpsimd
        def _(pool):
            n = 0
            for m, name in enumerate(("W1", "W2", "Wo")):
                for e in range(X):
                    if n >= 2:
                        pool.wait_ge(s_wlo, n - 1)
                    pool.dma_start(w_raw[:, n % 2, :, :], ffn[name][e].rearrange("(k p) n -> p k n", p=P)
                                   ).then_inc(s_raw[n % 2], 16)
                    n += 1

        @block.scalar
        def _(act):
            n = 0
            act.wait_ge(s_eps, 1)
            act.wait_ge(s_small, 16 * NSM)
            nc.scalar.activation(bn[:, :, 4, :, :], bn[:, :, 4, :, :], ACT.Sqrt, bias=eps[:, 1:2]).then_inc(s_bnq, 1)
            for m in range(3):
                for e in range(X):
                    act.wait_ge(s_raw[n % 2], 16 * (n // 2 + 1))
                    nc.scalar.activation(w_hi[:, m, e, :, :], w_raw[:, n % 2, :, :], ACT.Copy).then_inc(s_whi, 1)
                    n += 1

            def body(i, tiles):
                T = tiles * P
                act.wait_ge(s_c, i * 3 + 3 if isinstance(i, int) else i * 3 + 3)
                nc.scalar.activation(rstd[:, 0:tiles, :], mv[:, 0:tiles, 1:2], ACT.Sqrt, bias=eps[:, 0:1]
                                     ).then_inc(s_sq, 1)
                for k in range(KC):
                    act.wait_ge(s_tr, KC + i * KC + k + 1)
                    nc.scalar.activation(h_f[:, k, 0:T], ps[:, k, 0:T], ACT.Copy).then_inc(s_xf, 1)
                    nc.scalar.activation(x_hi[:, k, 0:T], ps[:, k, 0:T], ACT.Copy).then_inc(s_xhi, 1)
                act.wait_ge(s_lm, i + 1)
                nc.scalar.activation(prob[:, 0:tiles, :], logit[:, 0:tiles, :], ACT.Exp).then_inc(s_ex, 1)
                act.wait_ge(s_log, i + 1)
                act.wait_ge(s_xlo, i * KC + KC)
                for r, (m, e, c) in enumerate(hidden):
                    act.wait_ge(s_h, i * CH + r + 1)
                    if r >= 2:
                        act.wait_ge(s_hlo, i * CH + r - 1)
                    bank = ps[:, 2 + r % 2, 0:T]
                    scale, shift = bn_s[:, m, c, e:e + 1], bn_t[:, m, c, e:e + 1]
                    nc.scalar.activation(h_f[:, r % 2, 0:T], bank, ACT.Relu, bias=shift, scale=scale).then_inc(s_hf, 1)
                    nc.scalar.activation(h_hi[:, m, e % 2, c, 0:T], bank, ACT.Relu, bias=shift, scale=scale
                                         ).then_inc(s_hhi, 1)

            group_loop(act, body)

        @block.vector
        def _(dve):
            done = [0]

            def then(ins):
                done[0] += 1
                ins.then_inc(s_bnc, 1)
                dve.wait_ge(s_bnc, done[0])

            nc.vector.memset(eps[:, 0:1], LN_EPS)
            nc.vector.memset(eps[:, 1:2], BN_EPS).then_inc(s_eps, 1)
            dve.wait_ge(s_small, 16 * NSM)
            dve.wait_ge(s_bnq, 1)
            then(nc.vector.reciprocal(bn[:, :, 4, :, :], bn[:, :, 4, :, :]))
            then(nc.vector.tensor_tensor(bn_s[:, :, :, :], bn[:, :, 4, :, :], bn[:, :, 1, :, :], ALU.mult))
            then(nc.vector.tensor_tensor(bn_t[:, :, :, :], bn[:, :, 0, :, :], bn[:, :, 3, :, :], ALU.subtract))
            then(nc.vector.tensor_tensor(bn_t[:, :, :, :], bn_t[:, :, :, :], bn_s[:, :, :, :], ALU.mult))
            then(nc.vector.tensor_tensor(bn_t[:, :, :, :], bn_t[:, :, :, :], bn[:, :, 2, :, :], ALU.add))
            n = 0
            for m in range(3):
                for e in range(X):
                    dve.wait_ge(s_whi, n + 1)
                    nc.vector.tensor_tensor(w_lo[:, m, e, :, :], w_raw[:, n % 2, :, :], w_hi[:, m, e, :, :].bitcast(F32),
                                            ALU.subtract).then_inc(s_wlo, 1)
                    n += 1
            dve.wait_ge(s_bnc, done[0])

            def body(i, tiles):
                T = tiles * P
                rows = acc[:, bass.ds(i * GT, tiles), :]
                n0 = i * GT
                nc.vector.reciprocal(zinv[:, 0:tiles, :], rows[:, :, F:F + 1]).then_inc(s_c, 1)
                dve.wait_ge(s_x, 16 * i + 16)
                dve.wait_ge(s_c, i * 3 + 1)
                bias = bias_rows[:, 1, :].unsqueeze(1).to_broadcast([P, tiles, F])
                nc.vector.tensor_tensor(rows[:, :, 0:F], rows[:, :, 0:F],
                                        zinv[:, 0:tiles, :].to_broadcast([P, tiles, F]), ALU.mult).then_inc(s_bnc, 1)
                dve.wait_ge(s_bnc, done[0] + i * 8 + 1)
                nc.vector.tensor_tensor(rows[:, :, 0:F], rows[:, :, 0:F], bias, ALU.add).then_inc(s_bnc, 1)
                dve.wait_ge(s_bnc, done[0] + i * 8 + 2)
                nc.vector.tensor_tensor(rows[:, :, 0:F], rows[:, :, 0:F], x_in[:, 0:tiles, :], ALU.add
                                        ).then_inc(s_bnc, 1)
                dve.wait_ge(s_bnc, done[0] + i * 8 + 3)
                dve.sem_inc(s_turn, 1)
                for q in range(tiles):
                    ins = nc.vector.bn_stats(stats[:, q, :], acc[:, bass.ds(i * GT + q, 1), 0:F].rearrange(
                        "p a f -> p (a f)"))
                ins.then_inc(s_c, 1)
                dve.wait_ge(s_c, i * 3 + 2)
                dve.sem_inc(s_turn, 1)
                for q in range(tiles):
                    ins = nc.vector.bn_aggr(mv[:, q, :], stats[:, q, :])
                ins.then_inc(s_c, 1)
                dve.wait_ge(s_sq, i + 1)
                nc.vector.reciprocal(rstd[:, 0:tiles, :], rstd[:, 0:tiles, :]).then_inc(s_bnc, 1)
                dve.wait_ge(s_bnc, done[0] + i * 8 + 4)
                for q in range(tiles):
                    nc.vector.tensor_scalar(xn[:, q, :], acc[:, bass.ds(i * GT + q, 1), 0:F].rearrange(
                        "p a f -> p (a f)"), mv[:, q, 0:1], rstd[:, q, :], ALU.subtract, ALU.mult).then_inc(s_xn, 1)
                for k in range(KC):
                    dve.wait_ge(s_xhi, i * KC + k + 1)
                    nc.vector.tensor_tensor(x_lo[:, k, 0:T], h_f[:, k, 0:T], x_hi[:, k, 0:T].bitcast(F32),
                                            ALU.subtract).then_inc(s_xlo, 1)
                dve.wait_ge(s_log, i + 1)
                nc.vector.tensor_tensor(logit[:, 0:tiles, :], ps[:, 4, 0:tiles * X].rearrange(
                    "p (n e) -> p n e", e=X), br[:, :].unsqueeze(1).to_broadcast([P, tiles, X]), ALU.add
                ).then_inc(s_bnc, 1)
                dve.wait_ge(s_bnc, done[0] + i * 8 + 5)
                nc.vector.tensor_reduce(lmax[:, 0:tiles, :], logit[:, 0:tiles, :], AX.X, ALU.max).then_inc(s_bnc, 1)
                dve.wait_ge(s_bnc, done[0] + i * 8 + 6)
                nc.vector.tensor_tensor(logit[:, 0:tiles, :], logit[:, 0:tiles, :],
                                        lmax[:, 0:tiles, :].to_broadcast([P, tiles, X]), ALU.subtract
                                        ).then_inc(s_lm, 1)
                dve.wait_ge(s_ex, i + 1)
                nc.vector.tensor_reduce(lsum[:, 0:tiles, :], prob[:, 0:tiles, :], AX.X, ALU.add).then_inc(s_bnc, 1)
                dve.wait_ge(s_bnc, done[0] + i * 8 + 7)
                nc.vector.reciprocal(lsum[:, 0:tiles, :], lsum[:, 0:tiles, :]).then_inc(s_bnc, 1)
                dve.wait_ge(s_bnc, done[0] + i * 8 + 8)
                nc.vector.tensor_tensor(prob[:, 0:tiles, :], prob[:, 0:tiles, :],
                                        lsum[:, 0:tiles, :].to_broadcast([P, tiles, X]), ALU.mult
                                        ).then_inc(s_pr, 1)
                dve.wait_ge(s_pt, i + 1)
                nc.vector.tensor_copy(probT[:, 0:tiles, :], ps[0:X, 5, 0:T].rearrange("e (n p) -> e n p", p=P)
                                      ).then_inc(s_ptc, 1)

                def add_bias(q):
                    dve.wait_ge(s_bop, n0 + q + 1)
                    row = acc[:, bass.ds(i * GT + q, 1), 0:F].rearrange("p a f -> p (a f)")
                    nc.vector.tensor_tensor(row, ps[:, 6 + q % 2, 0:F], row, ALU.add).then_inc(s_yin, 1)

                def add_y(e, q, first):
                    k = i * GT * X + e * tiles + q
                    row = acc[:, bass.ds(i * GT + q, 1), 0:F].rearrange("p a f -> p (a f)")
                    dve.wait_ge(s_y, k + 1)
                    if e == 0:
                        dve.wait_ge(s_yin, n0 + q + 1)
                    else:
                        dve.wait_ge(s_ya, i * GT * X + (e - 1) * tiles + q + 1)
                    nc.vector.scalar_tensor_tensor(row, ps[:, 6 + (e * tiles + q) % 2, 0:F], prob[:, q, e:e + 1], row,
                                                   ALU.mult, ALU.add).then_inc(s_ya, 1)

                for q in range(tiles):
                    add_bias(q)
                r = 0
                for m, e in order:
                    if m < 2:
                        for c in range(KC):
                            dve.wait_ge(s_hhi, i * CH + r + 1)
                            nc.vector.tensor_tensor(h_lo[:, m, e % 2, c, 0:T], h_f[:, r % 2, 0:T],
                                                    h_hi[:, m, e % 2, c, 0:T].bitcast(F32), ALU.subtract
                                                    ).then_inc(s_hlo, 1)
                            r += 1
                    else:
                        for q in range(tiles):
                            add_y(e, q, e == 0)

            group_loop(dve, body)

        @block.tensor
        def _(pe):
            pe.sem_inc(s_tr, KC)
            pe.wait_ge(s_small, 16 * NSM)
            pe.wait_ge(s_wlo, 3 * X)

            def split_product(bank, a_hi, a_lo, b_hi, b_lo):
                pairs = [(a_hi[k], b_hi[k]) for k in range(KC)] + [(a_lo[k], b_hi[k]) for k in range(KC)] + \
                    [(a_hi[k], b_lo[k]) for k in range(KC)]
                for n, (a, b) in enumerate(pairs):
                    mm = nc.tensor.matmul(bank, a, b, start=n == 0, stop=n == len(pairs) - 1)
                return mm

            def body(i, tiles):
                T = tiles * P
                n0 = i * GT
                pe.wait_ge(s_xn, n0 + tiles)
                for k in range(KC):
                    for q in range(tiles):
                        mm = nc.tensor.transpose(ps[:, k, q * P:(q + 1) * P], xn[:, q, k * P:(k + 1) * P], ident[:, :])
                    mm.then_inc(s_tr, 1)
                pe.wait_ge(s_xf, i * KC + KC)
                for q in range(tiles):
                    for k in range(KC):
                        mm = nc.tensor.matmul(ps[:, 4, q * X:(q + 1) * X], h_f[:, k, q * P:(q + 1) * P], wr[:, k, :],
                                              start=k == 0, stop=k == KC - 1)
                mm.then_inc(s_log, 1)
                pe.wait_ge(s_pr, i + 1)
                for q in range(tiles):
                    mm = nc.tensor.transpose(ps[0:X, 5, q * P:(q + 1) * P], prob[:, q, :], ident[:, :])
                mm.then_inc(s_pt, 1)
                pe.wait_ge(s_ptc, i + 1)
                for q in range(tiles):
                    if q >= 2:
                        pe.wait_ge(s_yin, n0 + q - 1)
                    nc.tensor.matmul(ps[:, 6 + q % 2, 0:F], probT[:, q, :], bo[:, :], start=True, stop=True
                                     ).then_inc(s_bop, 1)
                pe.wait_ge(s_xlo, i * KC + KC)
                r = 0
                for m, e in order:
                    if m < 2:
                        for c in range(KC):
                            cols = slice(c * P, (c + 1) * P)
                            if m == 1:
                                pe.wait_ge(s_hlo, i * CH + rank[(0, e, KC - 1)] + 1)
                            if r >= 2:
                                pe.wait_ge(s_hhi, i * CH + r - 1)
                            a_hi = [w_hi[:, m, e, k, cols] for k in range(KC)]
                            a_lo = [w_lo[:, m, e, k, cols] for k in range(KC)]
                            if m == 0:
                                b_hi, b_lo = [x_hi[:, k, 0:T] for k in range(KC)], [x_lo[:, k, 0:T] for k in range(KC)]
                            else:
                                b_hi = [h_hi[:, 0, e % 2, k, 0:T] for k in range(KC)]
                                b_lo = [h_lo[:, 0, e % 2, k, 0:T] for k in range(KC)]
                            split_product(ps[:, 2 + r % 2, 0:T], a_hi, a_lo, b_hi, b_lo).then_inc(s_h, 1)
                            r += 1
                    else:
                        pe.wait_ge(s_hlo, i * CH + rank[(1, e, KC - 1)] + 1)
                        for q in range(tiles):
                            k1 = e * tiles + q
                            if k1 >= 2:
                                pe.wait_ge(s_ya, i * GT * X + k1 - 1)
                            else:
                                pe.wait_ge(s_yin, n0 + tiles)
                            toks = slice(q * P, (q + 1) * P)
                            split_product(ps[:, 6 + k1 % 2, 0:F],
                                          [h_hi[:, 1, e % 2, k, toks] for k in range(KC)],
                                          [h_lo[:, 1, e % 2, k, toks] for k in range(KC)],
                                          [w_hi[:, 2, e, k, :] for k in range(KC)],
                                          [w_lo[:, 2, e, k, :] for k in range(KC)]).then_inc(s_y, 1)
                pe.wait_ge(s_ya, i * GT * X + tiles * X)

            group_loop(pe, body)


_GNN = ("W", "a_src", "a_dst", "b")
_FFN = ("Wr", "br", "W1", "b1", "g1", "be1", "m1", "v1", "W2", "b2", "g2", "be2", "m2", "v2", "Wo", "bo")
_INS = ["x", "src", "dst"] + [f"L0_gnn_{n}{l}" for l in (1, 2) for n in _GNN] + [f"L0_ffn_{n}" for n in _FFN]


def kernel(**inputs):
    import numpy as _np
    import concourse.bacc as _bacc
    from concourse import mybir as _mybir
    from concourse.bass_utils import run_bass_kernel_spmd as _run

    nc = _bacc.Bacc("TRN2", target_bir_lowering=False, num_devices=1)
    arrays, aps = {}, {}
    for name in _INS:
        a = _np.ascontiguousarray(inputs[name])
        arrays[f"in_{name}_dram"] = a
        aps[name] = nc.dram_tensor(f"in_{name}_dram", a.shape, _mybir.dt.from_np(a.dtype), kind="ExternalInput").ap()
    shape = arrays["in_x_dram"].shape
    out = nc.dram_tensor("out_0_dram", shape, _mybir.dt.float32, kind="ExternalOutput").ap()
    gnn = [{n: aps[f"L0_gnn_{n}{l}"] for n in _GNN} for l in (1, 2)]
    ffn = {n: aps[f"L0_ffn_{n}"] for n in _FFN}
    build_program(nc, aps["x"], aps["src"], aps["dst"], gnn, ffn, out)
    r = _run(nc, [arrays], core_ids=[0])
    return r.results[0]["out_0_dram"]
```

```python
from contextlib import ExitStack, contextmanager

import numpy as np

import concourse.bass as bass
from concourse import mybir

F32 = mybir.dt.float32
F32R = mybir.dt.float32r
BF16 = mybir.dt.bfloat16
I32 = mybir.dt.int32
ALU = mybir.AluOpType
ACT = mybir.ActivationFunctionType
AX = mybir.AxisListType

P = 128
LN_EPS = 1e-5
BN_EPS = 1e-3
SLOPE = 0.2

BATCH = 8
UNIT = 4
BODY = 80
RING = 40
RING2 = 20
PARTS = 3
GT = 4
SUM_TILES = 16
MAX_SPREAD = 60.0
FAR = 1e30


def build_program(nc, x, src, dst, gnn, ffn, out):
    N, F = x.shape
    E = src.shape[0]
    NT = -(-N // P)
    LAST = N - (NT - 1) * P
    ET = -(-E // P)
    EG = -(-ET // P)
    STEPS = -(-(ET + NT - 1) // BODY) * BODY
    ITERS = STEPS // BODY
    NB = BODY // BATCH
    RB = RING // BATCH
    KC = F // P
    HEADS = [gnn[0]["a_src"].shape[0], gnn[1]["a_src"].shape[0]]
    HMAX = max(HEADS)
    ROW = F + 2 * HMAX
    X = ffn["Wr"].shape[1]
    TB = 7
    assert NT % TB == 0 and N == (NT - 1) * P + LAST and KC == 2
    SC = STEPS // 2
    SG = -(-STEPS // P)

    rows_dram = [nc.dram_tensor(f"node_rows_{l}", [NT * P, F + 2 * H], F32, kind="Internal").ap()
                 for l, H in enumerate(HEADS)]
    scores_dram = [nc.dram_tensor(f"node_scores_{l}", [NT * P, 2 * H], F32, kind="Internal").ap()
                   for l, H in enumerate(HEADS)]
    totals_dram = [nc.dram_tensor(f"node_totals_{l}", [NT * P, F + H], F32, kind="Internal").ap()
                   for l, H in enumerate(HEADS)]
    place_dram = nc.dram_tensor("edge_places", [STEPS, P], BF16, kind="Internal").ap()

    with ExitStack() as whole:
        def sb(name, shape, dt=F32):
            return whole.enter_context(nc.sbuf_tensor(name, shape, dt))

        ps = whole.enter_context(nc.psum_tensor("ps", [P, 8, 512], F32))
        ident = sb("ident", [P, P])
        lane = sb("lane", [P, P])
        part_iota = sb("part_iota", [P, 1])
        bias_rows = sb("bias_rows", [P, 2, F])
        edge_src = sb("edge_src", [P, STEPS])
        edge_place = sb("edge_place", [P, STEPS])
        scores = sb("scores", [P, NT, 2 * HMAX])
        step_tables = sb("step_tables", [P, STEPS], I32)
        step_node = step_tables[0:1, :]
        step_bank = step_tables[32:33, :]
        batch_nodes = {"all": step_tables[64:65, 0:2 * STEPS // BATCH],
                       "ring": step_tables[96:97, 0:2 * STEPS // BATCH]}

        disorder = sb("disorder", [1, 1])
        by_list = sb("by_list", [P, 2], I32)
        top = sb("top", [P, 2, 2 * HMAX])

        def for_pool(name, count):
            return [whole.enter_context(nc.semaphore(f"{name}{n}_")) for n in range(count)]

        stored = for_pool("rows_stored", 2)
        gathered = [for_pool("gathered_1_", RING // UNIT), for_pool("gathered_2_", RING2 // UNIT)]
        listed_rows = [for_pool("listed_1_", 3), for_pool("listed_2_", 3)]

        with ExitStack() as first:
            acc = first.enter_context(nc.sbuf_tensor("acc", [P, NT, ROW], F32))
            w_aug = first.enter_context(nc.sbuf_tensor("w_aug", [P, 2, KC, F + 2 * HMAX], F32))
            with semaphores(nc, "_p") as sem:
                prepare(nc, locals())
            with semaphores(nc, "_t0") as sem:
                transform(nc, locals(), 0)
            with semaphores(nc, "_e0") as sem:
                first_edges(nc, locals())
            with semaphores(nc, "_g0") as sem:
                general_edges(nc, locals(), 0)
            with semaphores(nc, "_t1") as sem:
                transform(nc, locals(), 1)
            with semaphores(nc, "_g1") as sem:
                general_edges(nc, locals(), 1)
        with semaphores(nc, "_m") as sem:
            edges_and_mixture(nc, locals())


@contextmanager
def semaphores(nc, suffix):
    with ExitStack() as held:
        named = []

        def sem(name):
            named.append(held.enter_context(nc.semaphore(name + suffix)))
            return named[-1]

        yield sem
        with nc.Block() as block:
            @block.sync
            def _(sp):
                for s in named:
                    sp.sem_clear(s)


def prepare(nc, g):
    P_, E, ET, EG, STEPS, SC, SG, NT, F, KC, HMAX, HEADS = (
        P, g["E"], g["ET"], g["EG"], g["STEPS"], g["SC"], g["SG"], g["NT"], g["F"], g["KC"], g["HMAX"], g["HEADS"])
    ps, ident, acc, bias_rows = g["ps"], g["ident"], g["acc"], g["bias_rows"]
    lane, part_iota, w_aug = g["lane"], g["part_iota"], g["w_aug"]
    TABLE = 2 * STEPS // BATCH
    ITERS = g["ITERS"]
    full = ET - (EG - 1) * P - 1
    tail = E - (ET - 1) * P
    pad_node = g["N"]
    assert NT * P > pad_node and full < P
    with ExitStack() as ctx:
        def sb(name, shape, dt=F32):
            return ctx.enter_context(nc.sbuf_tensor(name, shape, dt))

        sem = g["sem"]
        dst_i = sb("dst_i", [P, EG, P], I32)
        src_i = sb("src_i", [P, EG, P], I32)
        dst_f = sb("dst_f", [P, EG, P])
        src_f = sb("src_f", [P, EG, P])
        ends_i = sb("ends_i", [P, 2, EG], I32)
        ends = sb("ends", [P, 2, EG])
        tile_id = sb("tile_id", [P, EG])
        valid = sb("valid", [P, EG])
        count = sb("count", [P, EG])
        totals = sb("totals", [P, EG])
        before = sb("before", [P, EG])
        base = sb("base", [P, EG])
        limit = sb("limit", [P, EG])
        shift = sb("shift", [P, EG])
        shift128 = sb("shift128", [P, EG])
        node_off = sb("node_off", [P, EG])
        ones_g = sb("ones_g", [P, EG])
        below = sb("below", [P, STEPS])
        sel = sb("sel", [P, EG, STEPS])
        tri = sb("tri", [P, P])
        ones = sb("ones", [P, P])
        block_id = sb("block_id", [P, SG])
        places = sb("places", [P, SG, P], BF16)
        n_sum = sb("n_sum", [1, STEPS])
        n_used = sb("n_used", [1, STEPS])
        n_ends = sb("n_ends", [1, STEPS // BATCH, 2])
        n_ring = sb("n_ring", [1, TABLE], I32)
        next_i = sb("next_i", [P, EG, P], I32)
        next_f = sb("next_f", [P, EG, P])
        falls = sb("falls", [P, EG, P])
        faults_p = sb("faults_p", [P, 1])
        faults = sb("faults", [P, 1])
        other = sb("other", [1, STEPS])
        fault = sb("fault", [1, 4])
        marks = sb("marks", [1, ITERS])
        late = sb("late", [1, ITERS])
        n_all = sb("n_all", [1, TABLE], I32)
        step_iota = sb("step_iota", [P, STEPS])
        a_rows = sb("a_rows", [P, 4, F])
        prod = sb("prod", [P, F])

        s_zero, s_edges, s_w, s_a, s_const, s_pool = (
            sem("blank_tiles"), sem("edges_landed"), sem("weights_landed"), sem("attention_rows_landed"),
            sem("constants_ready"), sem("pool_chain"))
        s_falls = sem("falls_found")
        s_v, s_prefix, s_dve_mid, s_pe, s_places, s_bias = (
            sem("dve_chain"), sem("prefix_ready"), sem("dve_tables"), sem("pe_tables"), sem("places_stored"),
            sem("bias_landed"))
        block = ctx.enter_context(nc.Block())

        @block.sync
        def _(sp):
            sp.wait_ge(s_zero, 3)
            for dram, tile in ((g["dst"], dst_i), (g["src"], src_i)):
                whole = (EG - 1) * P * P
                sp.dma_start(tile[:, 0:EG - 1, :],
                             dram[0:whole].rearrange("(g q p) -> q g p", q=P, p=P)).then_inc(s_edges, 16)
                sp.dma_start(tile[0:full, EG - 1, :],
                             dram[whole:whole + full * P].rearrange("(q p) -> q p", p=P)).then_inc(s_edges, 16)
                sp.dma_start(tile[full:full + 1, EG - 1, 0:tail],
                             dram[whole + full * P:E].rearrange("(a p) -> a p", a=1)).then_inc(s_edges, 16)
            whole = (EG - 1) * P * P
            sp.dma_start(next_i[:, 0:EG - 1, :],
                         g["dst"][1:whole + 1].rearrange("(g q p) -> q g p", q=P, p=P)).then_inc(s_edges, 16)
            sp.dma_start(next_i[0:full, EG - 1, :],
                         g["dst"][whole + 1:whole + full * P + 1].rearrange("(q p) -> q p", p=P)).then_inc(s_edges, 16)
            sp.dma_start(next_i[full:full + 1, EG - 1, 0:tail - 1],
                         g["dst"][whole + full * P + 1:E].rearrange("(a p) -> a p", a=1)).then_inc(s_edges, 16)
            for l in (0, 1):
                sp.dma_start(w_aug[:, l, :, 0:F],
                             g["gnn"][l]["W"].rearrange("(k p) n -> p k n", p=P)).then_inc(s_w, 16)
                for n, name in enumerate(("a_src", "a_dst")):
                    sp.dma_start(a_rows[:, 2 * l + n, :],
                                 g["gnn"][l][name].rearrange("h c -> (h c)").partition_broadcast(P)
                                 ).then_inc(s_a, 16)
                sp.dma_start(bias_rows[:, l, :], g["gnn"][l]["b"].partition_broadcast(P)).then_inc(s_bias, 16)
            sp.wait_ge(s_bias, 32)
            sp.wait_ge(s_dve_mid, 4)
            rest = STEPS - (SG - 1) * P
            sp.dma_start(g["place_dram"][0:(SG - 1) * P, :].rearrange("(g q) p -> q g p", q=P),
                         places[:, 0:SG - 1, :]).then_inc(s_places, 16)
            sp.dma_start(g["place_dram"][(SG - 1) * P:STEPS, :], places[0:rest, SG - 1, :]).then_inc(s_places, 16)
            sp.wait_ge(s_places, 32)

        @block.gpsimd
        def _(pool):
            pool.memset(dst_i[:, EG - 1, :], pad_node).then_inc(s_zero, 1)
            pool.memset(src_i[:, EG - 1, :], 0).then_inc(s_zero, 1)
            pool.memset(next_i[:, EG - 1, :], pad_node).then_inc(s_zero, 1)
            pool.memset(ident[:, :], 0.0).then_inc(s_pool, 1)
            pool.memset(ones[:, :], 1.0).then_inc(s_pool, 1)
            pool.wait_ge(s_pool, 2)
            pool.affine_select(out=ident[:, :], in_=ident[:, :], compare_op=ALU.not_equal, fill=1.0, base=0,
                               pattern=[[-1, P]], channel_multiplier=1).then_inc(s_const, 1)
            pool.affine_select(out=tri[:, :], in_=ones[:, :], compare_op=ALU.is_gt, fill=0.0, base=0,
                               pattern=[[1, P]], channel_multiplier=-1).then_inc(s_const, 1)
            pool.iota(step_iota[:, :], [[1, STEPS]], base=0, channel_multiplier=0,
                      allow_small_or_imprecise_dtypes=True).then_inc(s_const, 1)
            pool.iota(part_iota[:, :], [[1, 1]], base=0, channel_multiplier=1,
                      allow_small_or_imprecise_dtypes=True).then_inc(s_const, 1)
            pool.iota(tile_id[:, :], [[P, EG]], base=0, channel_multiplier=1,
                      allow_small_or_imprecise_dtypes=True).then_inc(s_const, 1)
            pool.iota(block_id[:, :], [[P, SG]], base=0, channel_multiplier=1,
                      allow_small_or_imprecise_dtypes=True).then_inc(s_const, 1)
            pool.wait_ge(s_falls, 1)
            nc.gpsimd.partition_all_reduce(faults[:, :], faults_p[:, :], P, bass.bass_isa.ReduceOp.max
                                           ).then_inc(s_falls, 1)

        @block.vector
        def _(dve):
            done = [0]

            def then(ins):
                done[0] += 1
                ins.then_inc(s_v, 1)
                dve.wait_ge(s_v, done[0])

            then(nc.vector.memset(acc[:, :, :], 1.0))
            then(nc.vector.memset(ones_g[:, :], 1.0))
            dve.wait_ge(s_edges, 144)
            dve.wait_ge(s_const, 6)
            then(nc.vector.tensor_copy(dst_f[:, :, :], dst_i[:, :, :]))
            nc.vector.tensor_copy(src_f[:, :, :], src_i[:, :, :])
            shift_bits = int(np.log2(P))
            nc.vector.tensor_scalar(ends_i[:, 0, :], dst_i[:, :, 0], shift_bits, None, ALU.logical_shift_right)
            then(nc.vector.tensor_scalar(ends_i[:, 1, :], dst_i[:, :, P - 1], shift_bits, None,
                                         ALU.logical_shift_right))
            then(nc.vector.tensor_copy(ends[:, :, :], ends_i[:, :, :]))
            then(nc.vector.tensor_scalar(valid[:, :], tile_id[:, :], float(ET), None, ALU.is_lt))
            then(nc.vector.tensor_tensor(count[:, :], ends[:, 1, :], ends[:, 0, :], ALU.subtract))
            nc.vector.scalar_tensor_tensor(count[:, :], count[:, :], 1.0, valid[:, :], ALU.add, ALU.mult
                                           ).then_inc(s_dve_mid, 1)
            dve.wait_ge(s_dve_mid, 1)
            dve.wait_ge(s_prefix, 1)
            then(nc.vector.tensor_copy(totals[:, :], ps[:, 1, 0:EG]))
            then(nc.vector.tensor_tensor_scan(before[:, :], ones_g[:, :], totals[:, :], 0.0, ALU.mult, ALU.add))
            then(nc.vector.tensor_tensor(before[:, :], before[:, :], totals[:, :], ALU.subtract))
            then(nc.vector.tensor_tensor(base[:, :], ps[:, 0, 0:EG], before[:, :], ALU.add))
            then(nc.vector.tensor_tensor(limit[:, :], base[:, :], count[:, :], ALU.add))
            then(nc.vector.tensor_tensor(shift[:, :], ends[:, 0, :], base[:, :], ALU.subtract))
            then(nc.vector.tensor_scalar(shift128[:, :], shift[:, :], float(P), None, ALU.mult))
            then(nc.vector.tensor_scalar(node_off[:, :], shift[:, :], float(NT - 1), None, ALU.subtract))
            for e in range(EG):
                then(nc.vector.tensor_scalar(dst_f[:, e, :], dst_f[:, e, :], shift128[:, e:e + 1], None,
                                             ALU.subtract))
                then(nc.vector.tensor_scalar(below[:, :], step_iota[:, :], base[:, e:e + 1], None, ALU.is_ge))
                then(nc.vector.scalar_tensor_tensor(sel[:, e, :], step_iota[:, :], limit[:, e:e + 1],
                                                    below[:, :], ALU.is_lt, ALU.mult))
            dve.sem_inc(s_dve_mid, 1)
            then(nc.vector.tensor_copy(next_f[:, :, :], next_i[:, :, :]))
            then(nc.vector.tensor_copy(falls[:, :, :], dst_i[:, :, :]))
            then(nc.vector.tensor_tensor(falls[:, :, :], falls[:, :, :], next_f[:, :, :], ALU.is_gt))
            nc.vector.tensor_reduce(faults_p[:, :], falls[:, :, :].rearrange("p a b -> p (a b)"), AX.X, ALU.max
                                    ).then_inc(s_falls, 1)
            dve.wait_ge(s_w, 32)
            dve.wait_ge(s_a, 64)
            for l, H in enumerate(HEADS):
                for k in range(KC):
                    for n in (0, 1):
                        then(nc.vector.tensor_tensor(prod[:, :], w_aug[:, l, k, 0:F], a_rows[:, 2 * l + n, :],
                                                     ALU.mult))
                        then(nc.vector.tensor_reduce(w_aug[:, l, k, F + n * H:F + (n + 1) * H],
                                                     prod[:, :].rearrange("p (h c) -> p h c", h=H), AX.X, ALU.add))
            dve.wait_ge(s_pe, 1)
            for c in (0, 1):
                cols = slice(c * SC, (c + 1) * SC)
                nc.vector.tensor_copy(g["edge_src"][:, cols], ps[:, c, 0:SC])
                nc.vector.scalar_tensor_tensor(g["edge_place"][:, cols], step_iota[:, cols], -float(P),
                                               ps[:, 2 + c, 0:SC], ALU.mult, ALU.add)
                nc.vector.tensor_copy(n_sum[:, cols], ps[0:1, 4 + c, 0:SC])
                then(nc.vector.tensor_copy(n_used[:, cols], ps[0:1, 6 + c, 0:SC]))
            then(nc.vector.tensor_tensor(n_used[:, :], n_used[:, :], step_iota[0:1, :], ALU.mult))
            then(nc.vector.tensor_tensor(n_sum[:, :], n_sum[:, :], n_used[:, :], ALU.add))
            then(nc.vector.tensor_scalar(n_sum[:, :], n_sum[:, :], float(NT - 1), None, ALU.add))
            by_batch = n_sum[:, :].rearrange("a (b s) -> a b s", s=BATCH)
            nc.vector.tensor_copy(g["step_node"][:, :], n_sum[:, :])
            nc.vector.tensor_copy(lane[:, :], step_iota[:, 0:P])
            nc.vector.tensor_copy(n_ends[:, :, 0:1], by_batch[:, :, 0:1])
            then(nc.vector.tensor_copy(n_ends[:, :, 1:2], by_batch[:, :, BATCH - 1:BATCH]))
            then(nc.vector.tensor_copy(n_all[:, :], n_ends[:, :, :].rearrange("a b e -> a (b e)")))
            then(nc.vector.tensor_scalar(n_ring[:, :], n_all[:, :], SUM_TILES - 1, None, ALU.bitwise_and))
            then(nc.vector.tensor_tensor(n_used[:, :].rearrange("a (b s) -> a b s", s=BATCH), by_batch,
                                         n_ends[:, :, 0:1].to_broadcast([1, STEPS // BATCH, BATCH]), ALU.not_equal))
            nc.vector.tensor_copy(g["batch_nodes"]["all"][:, :], n_all[:, :])
            nc.vector.tensor_copy(g["batch_nodes"]["ring"][:, :], n_ring[:, :])
            then(nc.vector.tensor_copy(g["step_bank"][:, :], n_used[:, :]))
            then(nc.vector.tensor_tensor(other[:, :].rearrange("a (b s) -> a b s", s=BATCH), by_batch,
                                         n_ends[:, :, 1:2].to_broadcast([1, STEPS // BATCH, BATCH]), ALU.not_equal))
            then(nc.vector.tensor_tensor(other[:, :], other[:, :], n_used[:, :], ALU.mult))
            then(nc.vector.tensor_reduce(fault[:, 0:1], other[:, :], AX.X, ALU.max))
            by_iter = n_sum[:, :].rearrange("a (i s) -> a i s", s=BODY)
            then(nc.vector.tensor_scalar(marks[:, :], step_iota[0:1, 0:ITERS], float(GT), None, ALU.mult))
            then(nc.vector.tensor_tensor(late[:, 1:ITERS], by_iter[:, 1:ITERS, 0], marks[:, 1:ITERS], ALU.is_lt))
            then(nc.vector.tensor_reduce(fault[:, 1:2], late[:, 1:ITERS], AX.X, ALU.max))
            then(nc.vector.tensor_scalar(marks[:, :], marks[:, :], float(SUM_TILES - GT), None, ALU.add))
            then(nc.vector.tensor_tensor(late[:, :], by_iter[:, :, BODY - 1], marks[:, :], ALU.is_ge))
            then(nc.vector.tensor_reduce(fault[:, 2:3], late[:, :], AX.X, ALU.max))
            dve.wait_ge(s_falls, 2)
            then(nc.vector.tensor_copy(fault[:, 3:4], faults[0:1, :]))
            then(nc.vector.tensor_reduce(g["disorder"][:, :], fault[:, :], AX.X, ALU.max))
            then(nc.vector.tensor_scalar(block_id[:, :], block_id[:, :], float(P), None, ALU.mult))
            dve.sem_inc(s_dve_mid, 1)
            dve.wait_ge(s_pe, 2)
            for q in range(SG):
                rows = min(P, STEPS - q * P)
                last = nc.vector.tensor_scalar(places[0:rows, q, :], ps[0:rows, q // 4, (q % 4) * P:(q % 4 + 1) * P],
                                               block_id[0:rows, q:q + 1], None, ALU.subtract)
            last.then_inc(s_dve_mid, 1)

        @block.tensor
        def _(pe):
            pe.wait_ge(s_const, 6)
            pe.wait_ge(s_dve_mid, 1)
            nc.tensor.matmul(ps[:, 0, 0:EG], tri[:, :], count[:, :], start=True, stop=True)
            nc.tensor.matmul(ps[:, 1, 0:EG], ones[:, :], count[:, :], start=True, stop=True).then_inc(s_prefix, 1)
            pe.wait_ge(s_dve_mid, 2)
            for c in (0, 1):
                for e in range(EG):
                    first, last = e == 0, e == EG - 1
                    pick = sel[:, e, c * SC:(c + 1) * SC]
                    nc.tensor.matmul(ps[:, c, 0:SC], src_f[:, e, :], pick, start=first, stop=last)
                    nc.tensor.matmul(ps[:, 2 + c, 0:SC], dst_f[:, e, :], pick, start=first, stop=last)
                    nc.tensor.matmul(ps[0:1, 4 + c, 0:SC], node_off[:, e:e + 1], pick, start=first, stop=last)
                    mm = nc.tensor.matmul(ps[0:1, 6 + c, 0:SC], ones_g[:, 0:1], pick, start=first, stop=last)
            mm.then_inc(s_pe, 1)
            pe.wait_ge(s_dve_mid, 3)
            for q in range(SG):
                rows = min(P, STEPS - q * P)
                for e in range(EG):
                    mm = nc.tensor.matmul(ps[0:rows, q // 4, (q % 4) * P:(q % 4 + 1) * P],
                                          sel[:, e, q * P:q * P + rows], dst_f[:, e, :],
                                          start=e == 0, stop=e == EG - 1)
            mm.then_inc(s_pe, 1)


def transform(nc, g, layer):
    N, F, NT, LAST, KC, ROW, TB, HMAX = (g[k] for k in ("N", "F", "NT", "LAST", "KC", "ROW", "TB", "HMAX"))
    H = g["HEADS"][layer]
    C = F // H
    ps, ident, acc, bias_rows, w_aug, scores = (g[k] for k in ("ps", "ident", "acc", "bias_rows", "w_aug", "scores"))
    x, rows_dram, top = g["x"], g["rows_dram"][layer], g["top"]
    with ExitStack() as ctx:
        def sb(name, shape, dt=F32):
            return ctx.enter_context(nc.sbuf_tensor(f"{name}{layer}", shape, dt))

        sem = g["sem"]
        inp = sb("t_in", [P, TB, F])
        xn = sb("t_norm", [P, TB, F])
        neg = sb("t_neg", [P, TB, F])
        pos = sb("t_pos", [P, TB, F])
        stats = sb("t_stats", [P, TB, 6])
        mv = sb("t_mv", [P, TB, 2])
        rstd = sb("t_rstd", [P, TB, 1])
        eps = sb("t_eps", [P, 1])
        ones_col = sb("t_ones", [P, 1])
        xT = sb("t_xT", [P, 2, KC, P])
        zinv = sb("t_zinv", [P, TB, HMAX])

        s_in = [sem(f"t_landed{j}_") for j in range(TB)]
        s_eps = sem("t_eps_set")
        s_turn = sem("t_turn")
        s_var = sem("t_var_ready")
        s_std = sem("t_std_ready")
        s_c = sem("t_dve_chain")
        s_act = sem("t_act_done")
        s_pool = sem("t_pool_done")
        s_xn = sem("t_norm_ready")
        s_tr = sem("t_transposed")
        s_xT = sem("t_xT_ready")
        s_mm = sem("t_product_ready")
        s_row = sem("t_row_copied")
        s_sco = sem("t_scores_copied")
        s_asco = sem("t_row_scores")
        s_store = g["stored"][layer]
        top_p = sb("t_top_p", [P, 2 * H])
        spread = sb("t_spread", [1, H])
        widest = sb("t_widest", [1, 1])
        neg_scores = sb("t_neg_scores", [P, NT, H])
        s_top, s_end = sem("t_top"), sem("t_end_chain")
        block = ctx.enter_context(nc.Block())
        R = NT // TB
        tail_rows = LAST

        @block.sync
        def _(sp):
            if layer == 0:
                def load(i, last=False):
                    for j in range(TB):
                        sp.wait_ge(s_xn, i * TB + j + 1)
                        if last and j == TB - 1:
                            sp.dma_start(inp[0:tail_rows, j, :], x[(NT - 1) * P:N, :]).then_inc(s_in[j], 16)
                        else:
                            sp.dma_start(inp[:, j, :], x[bass.ds((i * TB + j) * P, P), :]).then_inc(s_in[j], 16)

                with sp.Fori(0, R - 1) as i:
                    load(i)
                load(R - 1, last=True)

        @block.gpsimd
        def _(pool):
            def store(i):
                pool.wait_ge(s_row, (i + 1) * TB)
                pool.wait_ge(s_sco, (i + 1) * TB)
                nc.gpsimd.tensor_copy(acc[:, bass.ds(i * TB, TB), F + H:F + 2 * H],
                                      scores[:, bass.ds(i * TB, TB), 0:H]).then_inc(s_asco, 1)
                pool.wait_ge(s_asco, i + 1)
                pool.dma_start(rows_dram.rearrange("(n p) c -> p n c", p=P)[:, bass.ds(i * TB, TB), :],
                               acc[:, bass.ds(i * TB, TB), 0:F + 2 * H]).then_inc(s_store, 16)

            with pool.Fori(0, R) as i:
                if layer == 1:
                    pool.wait_ge(s_c, i * 3 + 2)
                    nc.gpsimd.tensor_tensor(pos[:, :, :], inp[:, :, :],
                                            bias_rows[:, 0, :].unsqueeze(1).to_broadcast([P, TB, F]),
                                            ALU.add).then_inc(s_pool, 1)
                store(i)
            pool.wait_ge(s_top, 1)
            nc.gpsimd.partition_all_reduce(top[:, layer, 0:2 * H], top_p[:, :], P, bass.bass_isa.ReduceOp.max
                                           ).then_inc(s_top, 1)
            pool.wait_ge(s_store, 16 * R)

        @block.scalar
        def _(act):
            with act.Fori(0, R) as i:
                if layer == 0:
                    act.wait_ge(s_eps, 1)
                    act.wait_ge(s_var, i + 1)
                    nc.scalar.activation(rstd[:, :, :], mv[:, :, 1:2], ACT.Sqrt, bias=eps[:, 0:1]).then_inc(s_std, 1)
                else:
                    act.wait_ge(s_c, i * 3 + 3)
                    nc.scalar.activation(neg[:, :, :], neg[:, :, :], ACT.Exp).then_inc(s_act, 1)
                for j in range(TB):
                    act.wait_ge(s_mm, i * TB + j + 1)
                    nc.scalar.activation(
                        acc[:, bass.ds(i * TB + j, 1), 0:F + H].rearrange("p a (h c) -> p (a h) c", h=H)[:, :, 0:C],
                        ps[:, 2 + j % 2, 0:F].rearrange("p (h c) -> p h c", h=H), ACT.Copy).then_inc(s_row, 1)

        @block.vector
        def _(dve):
            if layer == 0:
                nc.vector.memset(eps[:, :], LN_EPS).then_inc(s_eps, 1)
            else:
                nc.vector.memset(ones_col[:, :], 1.0).then_inc(s_eps, 1)
                dve.wait_ge(s_eps, 1)

            dve.sem_inc(s_xn, TB)

            def tile_products(i, j):
                n = i * TB + j
                dve.wait_ge(s_tr, n + 1)
                nc.vector.tensor_copy(xT[:, j % 2, :, :],
                                      ps[:, j % 2, 0:KC * P].rearrange("p (k q) -> p k q", k=KC)).then_inc(s_xT, 1)
                dve.wait_ge(s_mm, n + 1)
                nc.vector.tensor_copy(scores[:, bass.ds(n, 1), 0:2 * H],
                                      ps[:, 4 + j % 2, 0:2 * H].unsqueeze(1)).then_inc(s_sco, 1)

            def body(i, last=False):
                if layer == 0:
                    for j in range(TB):
                        dve.wait_ge(s_in[j], i * 16 + 16)
                        dve.sem_inc(s_turn, 1)
                        nc.vector.bn_stats(stats[:, j, :], inp[:, j, :]).then_inc(s_c, 1)
                    for j in range(TB):
                        dve.wait_ge(s_c, i * (TB + 1) + j + 1)
                        dve.sem_inc(s_turn, 1)
                        ins = nc.vector.bn_aggr(mv[:, j, :], stats[:, j, :])
                    ins.then_inc(s_var, 1)
                    dve.wait_ge(s_std, i + 1)
                    nc.vector.reciprocal(rstd[:, :, :], rstd[:, :, :]).then_inc(s_c, 1)
                    dve.wait_ge(s_c, (i + 1) * (TB + 1))
                    for j in range(TB):
                        nc.vector.tensor_scalar(xn[:, j, :], inp[:, j, :], mv[:, j, 0:1], rstd[:, j, :],
                                                ALU.subtract, ALU.mult).then_inc(s_xn, 1)
                else:
                    H0 = g["HEADS"][0]
                    C0 = F // H0
                    sums = acc[:, bass.ds(i * TB, TB), 0:F + H0].rearrange("p n (h c) -> p n h c", h=H0)
                    nc.vector.reciprocal(zinv[:, :, 0:H0], sums[:, :, :, C0]).then_inc(s_c, 1)
                    dve.wait_ge(s_c, i * 3 + 1)
                    for j in range(TB):
                        one = acc[:, bass.ds(i * TB + j, 1), 0:F + H0].rearrange("p a (h c) -> p (a h) c", h=H0)
                        ins = nc.vector.tensor_tensor(
                            inp[:, j, :].rearrange("p (h c) -> p h c", h=H0), one[:, :, 0:C0],
                            zinv[:, j, 0:H0].unsqueeze(2).to_broadcast([P, H0, C0]), ALU.mult)
                    ins.then_inc(s_c, 1)
                    dve.wait_ge(s_pool, i + 1)
                    nc.vector.tensor_scalar(neg[:, :, :], pos[:, :, :], 0.0, None, ALU.min).then_inc(s_c, 1)
                    dve.wait_ge(s_act, i + 1)
                    nc.vector.tensor_scalar(pos[:, :, :], pos[:, :, :], 0.0, -1.0, ALU.max, ALU.add
                                            ).then_inc(s_std, 1)
                    dve.wait_ge(s_std, i + 1)
                    nc.vector.tensor_copy(acc[:, bass.ds(i * TB, TB), F:F + 1],
                                          ones_col[:, :].unsqueeze(1).to_broadcast([P, TB, 1]))
                    for j in range(TB):
                        nc.vector.tensor_tensor(xn[:, j, :], neg[:, j, :], pos[:, j, :], ALU.add).then_inc(s_xn, 1)
                for j in range(TB):
                    tile_products(i, j)

            if layer == 0:
                with dve.Fori(0, R - 1) as i:
                    body(i)
                body(R - 1, last=True)
            else:
                with dve.Fori(0, R) as i:
                    body(i)
            done = [0]

            def then(ins):
                done[0] += 1
                ins.then_inc(s_end, 1)
                dve.wait_ge(s_end, done[0])

            dve.wait_ge(s_sco, NT)
            nc.vector.tensor_scalar(neg_scores[:, :, :], scores[:, :, 0:H], -1.0, None, ALU.mult).then_inc(s_end, 1)
            done[0] += 1
            then(nc.vector.tensor_reduce(top_p[:, 0:H], scores[:, :, 0:H].rearrange("p n h -> p h n"), AX.X, ALU.max))
            nc.vector.tensor_reduce(top_p[:, H:2 * H], neg_scores[:, :, :].rearrange("p n h -> p h n"), AX.X, ALU.max
                                    ).then_inc(s_top, 1)
            dve.wait_ge(s_top, 2)
            then(nc.vector.tensor_tensor(spread[:, :], top[0:1, layer, 0:H], top[0:1, layer, H:2 * H], ALU.add))
            then(nc.vector.tensor_scalar(spread[:, :], spread[:, :], MAX_SPREAD, None, ALU.is_gt))
            then(nc.vector.tensor_reduce(widest[:, :], spread[:, :], AX.X, ALU.max))
            then(nc.vector.tensor_tensor(widest[:, :], widest[:, :], g["disorder"][:, :], ALU.max))
            then(nc.vector.tensor_copy(g["by_list"][0:1, layer:layer + 1], widest[:, :]))

        @block.tensor
        def _(pe):
            def transposes(i, j):
                pe.wait_ge(s_xn, TB + i * TB + j + 1)
                for k in range(KC):
                    mm = nc.tensor.transpose(ps[:, j % 2, k * P:(k + 1) * P], xn[:, j, k * P:(k + 1) * P], ident[:, :])
                mm.then_inc(s_tr, 1)

            def product(i, j):
                pe.wait_ge(s_xT, i * TB + j + 1)
                for k in range(KC):
                    nc.tensor.matmul(ps[:, 2 + j % 2, 0:F], xT[:, j % 2, k, :],
                                     w_aug[:, layer, k, 0:F], start=k == 0, stop=k == KC - 1)
                for k in range(KC):
                    mm = nc.tensor.matmul(ps[:, 4 + j % 2, 0:2 * H], xT[:, j % 2, k, :],
                                          w_aug[:, layer, k, F:F + 2 * H], start=k == 0, stop=k == KC - 1)
                mm.then_inc(s_mm, 1)

            with pe.Fori(0, R) as i:
                for j in range(TB):
                    if j >= 2:
                        pe.wait_ge(s_row, i * TB + j - 1)
                    transposes(i, j)
                    product(i, j)


def guards(nc, g, layer, sb, sem):
    NT, HMAX = g["NT"], g["HMAX"]
    H = g["HEADS"][layer]
    M = 2 * H
    scores = g["scores"]
    table = sb("node_table", [P, NT, M * PARTS], BF16)
    node_dm = sb("node_dm", [P, NT, M])
    rest1 = sb("rest1", [P, NT, M])
    rest2 = sb("rest2", [P, NT, M])
    self_w = sb("self_w", [P, NT, H])
    self_e = sb("self_e", [P, NT, H])
    top = g["top"]
    s_c, s_self, s_selfw, s_table = (
        sem("scalar_chain"), sem("self_scores"), sem("self_weights"),
        sem("table_ready"))

    def on_scalar(act):
        act.wait_ge(s_self, 1)
        nc.scalar.activation(self_w[:, :, :], self_e[:, :, :], ACT.Exp).then_inc(s_selfw, 1)

    def on_vector(dve):
        done = [0]

        def then(ins):
            done[0] += 1
            ins.then_inc(s_c, 1)
            dve.wait_ge(s_c, done[0])

        then(nc.vector.tensor_tensor(rest1[:, :, 0:H], scores[:, :, H:M],
                                     top[:, layer, 0:H].unsqueeze(1).to_broadcast([P, NT, H]), ALU.add))
        nc.vector.tensor_copy(node_dm[:, :, 0:H], scores[:, :, H:M])
        then(nc.vector.scalar_tensor_tensor(node_dm[:, :, H:M], rest1[:, :, 0:H], SLOPE, rest1[:, :, 0:H],
                                            ALU.mult, ALU.max))
        then(nc.vector.tensor_tensor(self_e[:, :, :], scores[:, :, 0:H], scores[:, :, H:M], ALU.add))
        then(nc.vector.scalar_tensor_tensor(self_e[:, :, :], self_e[:, :, :], SLOPE, self_e[:, :, :],
                                            ALU.mult, ALU.max))
        nc.vector.tensor_tensor(self_e[:, :, :], self_e[:, :, :], node_dm[:, :, H:M], ALU.subtract
                                ).then_inc(s_self, 1)
        parts = table[:, :, :].rearrange("p n (m q) -> p n m q", q=PARTS)
        then(nc.vector.tensor_copy(parts[:, :, :, 0], node_dm[:, :, :]))
        then(nc.vector.tensor_tensor(rest1[:, :, :], node_dm[:, :, :], parts[:, :, :, 0], ALU.subtract))
        then(nc.vector.tensor_copy(parts[:, :, :, 1], rest1[:, :, :]))
        then(nc.vector.tensor_tensor(rest2[:, :, :], rest1[:, :, :], parts[:, :, :, 1], ALU.subtract))
        nc.vector.tensor_copy(parts[:, :, :, 2], rest2[:, :, :]).then_inc(s_table, 1)
        dve.wait_ge(s_selfw, 1)

    return table, self_w, s_table, on_scalar, on_vector


def edge_parts(nc, g, layer, sb, sem, table, s_table, sums, ring_slots, node_of):
    F, NT, ITERS = g["F"], g["NT"], g["ITERS"]
    H = g["HEADS"][layer]
    W = F + H
    ROW = F + 2 * H
    M = 2 * H
    NB = BODY // BATCH
    RU = ring_slots // UNIT
    NU = BODY // UNIT
    BU = BATCH // UNIT
    GROUP = BODY // 2
    GB = GROUP // BATCH
    assert NU % RU == 0
    ps = g["ps"]
    edge_src, edge_place, step_node, step_bank = g["edge_src"], g["edge_place"], g["step_node"], g["step_bank"]
    batch_nodes = g["batch_nodes"][node_of]
    rows_dram = g["rows_dram"][layer]
    LASTB = ITERS * NB - 1

    ring = sb("gathered_rows", [P, ring_slots, ROW])
    idx = sb("gather_index", [P, 2, GROUP], I32)
    onehot_t = sb("onehot_t", [P, 2, BATCH * P], BF16)
    onehot = sb("onehot", [P, 2, BATCH, P])
    place_now = sb("place_now", [P, 2, BATCH])
    adm = sb("adm", [P, 2, BATCH, M])
    e_sum = sb("e_sum", [P, 2, BATCH, H])
    e_leaky = sb("e_leaky", [P, 2, BATCH, H])
    e_less = sb("e_less", [P, 2, BATCH, H])
    weight = sb("weight", [P, 2, BATCH, H])
    zero_w = sb("zero_w", [P, P], BF16)
    zero_r = sb("zero_r", [P, W + W % 2], BF16)

    s_prow = [sem(f"place_rows_landed{n}_") for n in (0, 1)]
    s_idx = sem("index_ready")
    s_turn = sem("gather_turn")
    s_sp_turn = sem("load_turn")
    s_gath = g["gathered"][layer]
    s_oht = sem("onehot_t_ready")
    s_admp = sem("adm_product_ready")
    s_adm = sem("adm_summed")
    s_e = sem("score_chain")
    s_scores = sem("scores_ready")
    s_w = sem("weights_ready")
    s_oh = sem("onehot_ready")
    s_wt = sem("weighted")
    s_prod = sem("products_ready")
    s_add = sem("sums_added")
    s_rows_free = sem("place_rows_free")
    s_zero = sem("zeros_set")

    def slots_of(unit):
        return ring[:, unit % RU * UNIT:(unit % RU + 1) * UNIT, :]

    class Parts:
        sums_added = s_add

        @staticmethod
        def sync_batch(sp, i, jb):
            b = i * NB + jb
            sp.wait_ge(s_rows_free, b + 1)
            sp.sem_inc(s_sp_turn, 1)
            rows = g["place_dram"][bass.ds(b * BATCH, BATCH), :].rearrange("s p -> (s p)")
            sp.dma_start(onehot_t[:, jb % 2, :], rows.partition_broadcast(P)).then_inc(s_prow[jb % 2], 16)

        @staticmethod
        def gpsimd_batch(pool, i, jb):
            b = i * NB + jb
            if jb % GB == 0:
                pool.wait_ge(s_idx, i * (NB // GB) + jb // GB + 1)
            for j in range(BATCH):
                step = jb * BATCH + j
                if j % UNIT == 0:
                    pool.wait_ge(s_prod, i * NU + step // UNIT + 1)
                    pool.sem_inc(s_turn, 1)
                nc.gpsimd.indirect_dma_start(
                    ring[:, step % ring_slots, :], None, rows_dram,
                    bass.IndirectOffsetOnAxis(idx[:, step // GROUP % 2, step % GROUP:step % GROUP + 1], 0)
                ).then_inc(s_gath[step // UNIT % RU], 16)

        @staticmethod
        def scalar_start(act):
            nc.scalar.activation(idx[:, 0, :], edge_src[:, 0:GROUP], ACT.Copy).then_inc(s_idx, 1)

        @staticmethod
        def scalar_batch(act, i, jb):
            nj = (jb + 1) % NB
            b1 = i * NB + jb + 1
            if H == 1:
                nc.scalar.activation(place_now[:, nj % 2, :], edge_place[:, bass.ds(b1 * BATCH, BATCH)], ACT.Copy)
            act.wait_ge(s_scores, b1 + 1)
            nc.scalar.activation(weight[:, nj % 2, :, :], e_less[:, nj % 2, :, :], ACT.Exp).then_inc(s_w, 1)

        @staticmethod
        def scalar_index(act, i, jb, last):
            if jb % GB == 0 and not (last and jb + GB == NB):
                half = jb // GB + 1
                group = i * (NB // GB) + half
                act.wait_ge(s_prod, (group - 1) * (GROUP // UNIT) + RU)
                nc.scalar.activation(idx[:, half % 2, :], edge_src[:, bass.ds(group * GROUP, GROUP)],
                                     ACT.Copy).then_inc(s_idx, 1)

        @staticmethod
        def scalar_first(act):
            if H == 1:
                nc.scalar.activation(place_now[:, 0, :], edge_place[:, 0:BATCH], ACT.Copy)
            act.wait_ge(s_scores, 1)
            nc.scalar.activation(weight[:, 0, :, :], e_less[:, 0, :, :], ACT.Exp).then_inc(s_w, 1)

        @staticmethod
        def vector_start(dve):
            nc.vector.memset(zero_w[:, :], 0.0).then_inc(s_zero, 1)
            nc.vector.memset(zero_r[:, :], 0.0).then_inc(s_zero, 1)
            dve.sem_inc(s_rows_free, 2)

        @staticmethod
        def scores_of(dve, i, jb, stage):
            b = i * NB + jb
            h = jb % 2
            if stage == "node one-hot":
                dve.wait_ge(s_prow[h], (i * (NB // 2) + jb // 2 + 1) * 16)
                nc.vector.tensor_scalar(onehot_t[:, h, :], onehot_t[:, h, :], g["part_iota"][:, 0:1], None,
                                        ALU.is_equal).then_inc(s_oht, 1)
            if stage == "sum":
                dve.wait_ge(s_admp, b + 1)
                dve.sem_inc(s_rows_free, 1)
                nc.vector.tensor_reduce(
                    adm[:, h, :, :],
                    ps[:, 4, 0:BATCH * M * PARTS].rearrange("p (s m q) -> p s m q", s=BATCH, q=PARTS),
                    AX.X, ALU.add).then_inc(s_adm, 1)
                dve.wait_ge(s_adm, b + 1)
                for u in range(BU):
                    unit = jb * BU + u
                    dve.wait_ge(s_gath[unit % RU], (i * (NU // RU) + unit // RU + 1) * 16 * UNIT)
                    ins = nc.vector.tensor_tensor(
                        e_sum[:, h, u * UNIT:(u + 1) * UNIT, :], slots_of(unit)[:, :, F + H:F + 2 * H],
                        adm[:, h, u * UNIT:(u + 1) * UNIT, 0:H], ALU.add)
                ins.then_inc(s_e, 1)
            if stage == "leaky":
                dve.wait_ge(s_e, 2 * b + 1)
                nc.vector.scalar_tensor_tensor(e_leaky[:, h, :, :], e_sum[:, h, :, :], SLOPE, e_sum[:, h, :, :],
                                               ALU.mult, ALU.max).then_inc(s_e, 1)
            if stage == "less guard":
                dve.wait_ge(s_e, 2 * b + 2)
                nc.vector.tensor_tensor(e_less[:, h, :, :], e_leaky[:, h, :, :], adm[:, h, :, H:M], ALU.subtract
                                        ).then_inc(s_scores, 1)

        @staticmethod
        def weigh(dve, i, jb, u):
            b = i * NB + jb
            h = jb % 2
            if u == 0:
                if H > 1:
                    places = edge_place[:, bass.ds(b * BATCH, BATCH)]
                    nc.vector.tensor_tensor(onehot[:, h, :, :],
                                            g["lane"][:, :].unsqueeze(1).to_broadcast([P, BATCH, P]),
                                            places.unsqueeze(2).to_broadcast([P, BATCH, P]), ALU.is_equal
                                            ).then_inc(s_oh, 1)
                dve.wait_ge(s_w, b + 1)
            if H == 1:
                for j in range(u * UNIT, (u + 1) * UNIT):
                    ins = nc.vector.tensor_scalar(onehot[:, h, j, :], g["lane"][:, :],
                                                  place_now[:, h, j:j + 1], weight[:, h, j, :],
                                                  ALU.is_equal, ALU.mult)
            else:
                w_rows = slots_of(jb * BU + u)[:, :, 0:W].rearrange("p s (h c) -> p s h c", h=H)
                ins = nc.vector.tensor_tensor(
                    w_rows, w_rows, weight[:, h, u * UNIT:(u + 1) * UNIT, :].unsqueeze(3).to_broadcast(
                        [P, UNIT, H, W // H]), ALU.mult)
            ins.then_inc(s_wt, 1)

        @staticmethod
        def add_batch(dve, i, jb, which, state):
            b = i * NB + jb
            if which == 0:
                _, state["nodes"] = nc.values_load_multi_w_load_instructions(
                    batch_nodes[:, bass.ds(b * 2, 2)], engines=[dve.engine], min_val=0,
                    max_val=sums.shape[1] - 1,
                    skip_runtime_bounds_check_because="prepare() keeps it to the node tiles")
                dve.wait_ge(s_prod, (b + 1) * BU + RU)
            if not (isinstance(i, int) and b == 0 and which == 0):
                dve.wait_ge(s_add, 2 * b + which)
            tile = sums[:, bass.ds(state["nodes"][which], 1), 0:W].rearrange("p a c -> p (a c)")
            nc.vector.tensor_tensor(tile, ps[:, 2 * (jb % 2) + which, 0:W], tile, ALU.add).then_inc(s_add, 1)

        @staticmethod
        def vector_first(dve):
            for stage in ("node one-hot", "sum", "leaky", "less guard"):
                Parts.scores_of(dve, 0, 0, stage)
            for u in range(BU):
                Parts.weigh(dve, 0, 0, u)
            Parts.scores_of(dve, 0, 1, "node one-hot")

        @staticmethod
        def vector_piece(dve, i, j, last, state):
            jb, piece = j // BATCH, j % BATCH
            if piece in (2, 3) and not (isinstance(i, int) and i == 0 and jb == 0):
                Parts.add_batch(dve, i if jb else i - 1, (jb - 1) % NB, piece - 2, state)
            i1, jb1 = i + (jb + 1) // NB, (jb + 1) % NB
            if not (last and jb == NB - 1):
                if piece == 0:
                    Parts.scores_of(dve, i1, jb1, "sum")
                if piece == 1:
                    Parts.scores_of(dve, i1, jb1, "leaky")
                    Parts.scores_of(dve, i1, jb1, "less guard")
                if piece in (3, 5):
                    Parts.weigh(dve, i1, jb1, piece // 4)
            if piece == 4 and not (last and jb >= NB - 2):
                Parts.scores_of(dve, i + (jb + 2) // NB, (jb + 2) % NB, "node one-hot")

        @staticmethod
        def vector_last(dve, state):
            for which in (0, 1):
                Parts.add_batch(dve, ITERS - 1, NB - 1, which, state)

        @staticmethod
        def tensor_start(pe):
            pe.sem_inc(s_prod, RU)
            pe.wait_ge(s_table, 1)
            pe.wait_ge(s_zero, 2)

        @staticmethod
        def node_products(pe, i, jb):
            b = i * NB + jb
            _, nodes = nc.values_load_multi_w_load_instructions(
                step_node[0:1, bass.ds(b * BATCH, BATCH)], engines=[pe.engine], min_val=0, max_val=NT - 1,
                skip_runtime_bounds_check_because="prepare() keeps it to the node tiles")
            pe.wait_ge(s_oht, b + 1)
            if not isinstance(i, int) or b >= 1:
                pe.wait_ge(s_adm, b)
            for j in range(BATCH):
                mm = nc.tensor.matmul(ps[:, 4, j * M * PARTS:(j + 1) * M * PARTS],
                                      onehot_t[:, jb % 2, j * P:(j + 1) * P],
                                      table[:, bass.ds(nodes[j], 1), 0:M * PARTS].rearrange("p a c -> p (a c)"),
                                      start=True, stop=True)
            mm.then_inc(s_admp, 1)

        @staticmethod
        def tensor_step(pe, i, j, last, state):
            jb, q = j // BATCH, j % BATCH
            b = i * NB + jb
            first_bank = 2 * (jb % 2)
            if q == 0:
                _, state["banks"] = nc.values_load_multi_w_load_instructions(
                    step_bank[0:1, bass.ds(b * BATCH, BATCH)], engines=[pe.engine], min_val=0, max_val=1,
                    skip_runtime_bounds_check_because="a comparison's outcome")
                if not isinstance(i, int) or b >= 2:
                    pe.wait_ge(s_add, 2 * b - 2)
                nc.tensor.matmul(ps[:, first_bank + 1, 0:W], zero_w[:, :], zero_r[:, 0:W], start=True, stop=False,
                                 skip_group_check=True)
                if H > 1:
                    pe.wait_ge(s_oh, b + 1)
                pe.wait_ge(s_wt, (b + 1) * BU)
            bank = ps[:, first_bank, 0:W] if q == 0 else \
                ps[:, bass.ds(state["banks"][q] + first_bank, 1), 0:W].rearrange("p a c -> p (a c)")
            mm = nc.tensor.matmul(bank, onehot[:, jb % 2, q, :], ring[:, (jb * BATCH + q) % ring_slots, 0:W],
                                  start=q == 0, stop=q == BATCH - 1, skip_group_check=True)
            if q % UNIT == UNIT - 1:
                mm.then_inc(s_prod, 1)
            if q == BATCH - 1 and not (last and jb >= NB - 2):
                Parts.node_products(pe, i + (jb + 2) // NB, (jb + 2) % NB)

    return Parts


def first_edges(nc, g):
    F, NT, ITERS, HEADS = g["F"], g["NT"], g["ITERS"], g["HEADS"]
    H = HEADS[0]
    W = F + H
    acc = g["acc"]
    NB = BODY // BATCH
    with ExitStack() as ctx:
        def sb(name, shape, dt=F32):
            return ctx.enter_context(nc.sbuf_tensor(f"{name}0", shape, dt))

        sem = g["sem"]
        table, self_w, s_table, guard_act, guard_dve = guards(nc, g, 0, sb, sem)
        parts = edge_parts(nc, g, 0, sb, sem, table, s_table, acc, RING, "all")
        s_loops = sem("loops_weighted")
        block = ctx.enter_context(nc.Block())

        def loop(eng, body):
            body(0, False)
            with eng.Fori(1, ITERS - 1) as i:
                body(i, False)
            body(ITERS - 1, True)

        @block.sync
        def _(sp):
            with sp.If(listed(nc, sp, g, 0) == 0):
                def body(i, last):
                    for jb in range(NB):
                        parts.sync_batch(sp, i, jb)

                loop(sp, body)

        @block.gpsimd
        def _(pool):
            with pool.If(listed(nc, pool, g, 0) == 0):

                def body(i, last):
                    for jb in range(NB):
                        parts.gpsimd_batch(pool, i, jb)

                loop(pool, body)

        @block.scalar
        def _(act):
            with act.If(listed(nc, act, g, 0) == 0):
                parts.scalar_start(act)
                guard_act(act)
                parts.scalar_first(act)

                def body(i, last):
                    for jb in range(NB):
                        if not (last and jb == NB - 1):
                            parts.scalar_batch(act, i, jb)
                        parts.scalar_index(act, i, jb, last)

                loop(act, body)

        @block.vector
        def _(dve):
            with dve.If(listed(nc, dve, g, 0) == 0):
                state = {}
                guard_dve(dve)
                parts.vector_start(dve)
                loops = acc[:, :, 0:W].rearrange("p n (h c) -> p n h c", h=H)
                nc.vector.tensor_tensor(loops, loops, self_w[:, :, :].unsqueeze(3).to_broadcast(
                    [P, NT, H, W // H]), ALU.mult).then_inc(s_loops, 1)
                parts.vector_first(dve)
                dve.wait_ge(s_loops, 1)

                def body(i, last):
                    for j in range(BODY):
                        parts.vector_piece(dve, i, j, last, state)

                loop(dve, body)
                parts.vector_last(dve, state)

        @block.tensor
        def _(pe):
            with pe.If(listed(nc, pe, g, 0) == 0):
                state = {}
                parts.tensor_start(pe)
                parts.node_products(pe, 0, 0)
                parts.node_products(pe, 0, 1)

                def body(i, last):
                    for j in range(BODY):
                        parts.tensor_step(pe, i, j, last, state)

                loop(pe, body)


def listed(nc, eng, g, layer):
    _, values = nc.values_load_multi_w_load_instructions(
        g["by_list"][0:1, layer:layer + 1], engines=[eng.engine], min_val=0, max_val=1,
        skip_runtime_bounds_check_because="a comparison's outcome")
    return values[0]


def general_edges(nc, g, layer):
    E, ET, F, NT, N = g["E"], g["ET"], g["F"], g["NT"], g["N"]
    H = g["HEADS"][layer]
    W = F + H
    ps, ident, acc, scores = g["ps"], g["ident"], g["acc"], g["scores"]
    rows_dram, scores_dram, totals_dram = g["rows_dram"][layer], g["scores_dram"][layer], g["totals_dram"][layer]
    tail = E - (ET - 1) * P
    with ExitStack() as ctx:
        def sb(name, shape, dt=F32):
            return ctx.enter_context(nc.sbuf_tensor(f"g_{name}{layer}", shape, dt))

        sem = g["sem"]
        state = sb("state", [P, NT, 2 * H])
        src_of = {False: sb("src_of", [P, 1], I32), True: sb("src_of_last", [P, 1], I32)}
        dst_of = {False: sb("dst_of", [P, 1], I32), True: sb("dst_of_last", [P, 1], I32)}
        dst_f = sb("dst_f", [P, 1])
        rows = sb("rows", [P, F + 2 * H])
        node = sb("node", [P, 2 * H])
        total = sb("total", [P, W])
        diag = sb("diag", [P, 1 + H, P])
        ones = sb("ones", [P, P])
        same = sb("same", [P, P])
        out_of = sb("out_of", [P, P])
        held = sb("held", [P, H, P])
        best = sb("best", [P, H])
        e_sum = sb("e_sum", [P, H])
        guard = sb("guard", [P, H])
        weight = sb("weight", [P, H])
        node_sum = sb("node_sum", [P, NT, H])
        node_guard = sb("node_guard", [P, NT, H])
        node_w = sb("node_w", [P, NT, H])
        sums = sb("sums", [P, 7, W])

        s_set, s_init, s_turn = sem("state_set"), sem("state_stored"), sem("turn")
        s_list, s_free = sem("list_landed"), sem("list_used")
        s_got, s_node, s_put = g["listed_rows"][layer]
        s_diag, s_bc = sem("diagonals_ready"), sem("rows_broadcast")
        s_new = sem("new_state_ready")
        s_score, s_exp, s_prod = sem("scores_ready"), sem("weights_ready"), sem("sums_ready")
        s_c, s_back, s_taken, s_final = sem("dve_chain"), sem("totals_back"), sem("totals_used"), sem("rows_stored")
        block = ctx.enter_context(nc.Block())
        R = NT // 7

        def tiles(eng, step, passes=(0, ET)):
            for base in passes:
                with eng.Fori(0, ET - 1) as e:
                    step(e, e + base, base > 0, False)
                step(ET - 1, base + ET - 1, base > 0, True)

        def by_tile(dram, first, tiles_):
            return dram.rearrange("(n p) c -> p n c", p=P)[:, bass.ds(first, tiles_), :]

        @block.sync
        def _(sp):
            with sp.If(listed(nc, sp, g, layer) == 1):
                sp.wait_ge(s_set, 1)
                sp.dma_start(by_tile(scores_dram, 0, NT), state[:, :, :]).then_inc(s_init, 16)
                for r in range(R):
                    sp.dma_start(by_tile(totals_dram, r * 7, 7), sums[:, :, :]).then_inc(s_init, 16)

                def step(e, n, second, last):
                    sp.wait_ge(s_free, n + 1)
                    sp.sem_inc(s_turn, 1)
                    if last:
                        sp.dma_start(src_of[True][0:tail, :], g["src"][(ET - 1) * P:E].rearrange("(p a) -> p a", a=1)
                                     ).then_inc(s_list, 16)
                        sp.dma_start(dst_of[True][0:tail, :], g["dst"][(ET - 1) * P:E].rearrange("(p a) -> p a", a=1)
                                     ).then_inc(s_list, 16)
                    else:
                        sp.dma_start(src_of[False][:, :], g["src"][bass.ds(e * P, P)].rearrange("(p a) -> p a", a=1)
                                     ).then_inc(s_list, 16)
                        sp.dma_start(dst_of[False][:, :], g["dst"][bass.ds(e * P, P)].rearrange("(p a) -> p a", a=1)
                                     ).then_inc(s_list, 16)

                tiles(sp, step)
                sp.wait_ge(s_put, 16 * 2 * ET)
                sp.dma_start(state[:, :, :], by_tile(scores_dram, 0, NT)).then_inc(s_back, 16)
                for r in range(R):
                    if r:
                        sp.wait_ge(s_taken, r)
                    sp.dma_start(sums[:, :, :], by_tile(totals_dram, r * 7, 7)).then_inc(s_back, 16)
                sp.wait_ge(s_taken, R)
                if layer == 1:
                    sp.dma_start(by_tile(rows_dram, 0, NT), acc[:, :, 0:F + 2 * H]).then_inc(s_final, 16)
                    sp.wait_ge(s_final, 16)

        @block.gpsimd
        def _(pool):
            with pool.If(listed(nc, pool, g, layer) == 1):
                pool.wait_ge(s_init, 16 * (R + 1))

                def step(e, n, second, last):
                    pool.wait_ge(s_list, n * 32 + 32)
                    pool.sem_inc(s_turn, 1)
                    nc.gpsimd.indirect_dma_start(rows[:, :], None, rows_dram,
                                                 bass.IndirectOffsetOnAxis(src_of[last][:, 0:1], 0)).then_inc(s_got, 16)
                    nc.gpsimd.indirect_dma_start(node[:, :], None, scores_dram,
                                                 bass.IndirectOffsetOnAxis(dst_of[last][:, 0:1], 0)).then_inc(s_node, 16)
                    if second:
                        nc.gpsimd.indirect_dma_start(total[:, :], None, totals_dram,
                                                     bass.IndirectOffsetOnAxis(dst_of[last][:, 0:1], 0)).then_inc(s_node, 16)
                    pool.wait_ge(s_new, n + 1)
                    pool.sem_inc(s_turn, 1)
                    if second:
                        nc.gpsimd.indirect_dma_start(totals_dram, bass.IndirectOffsetOnAxis(dst_of[last][:, 0:1], 0),
                                                     total[:, :], None).then_inc(s_put, 16)
                    else:
                        nc.gpsimd.indirect_dma_start(scores_dram, bass.IndirectOffsetOnAxis(dst_of[last][:, 0:1], 0),
                                                     node[:, :], None).then_inc(s_put, 16)
                    pool.wait_ge(s_put, n * 16 + 16)
                    pool.sem_inc(s_free, 1)

                tiles(pool, step)

        @block.scalar
        def _(act):
            with act.If(listed(nc, act, g, layer) == 1):
                def step(e, n, second, last):
                    act.wait_ge(s_score, n - (ET - 1))
                    nc.scalar.activation(weight[:, :], e_sum[:, :], ACT.Exp).then_inc(s_exp, 1)

                tiles(act, step, passes=(ET,))
                act.wait_ge(s_score, ET + 1)
                nc.scalar.activation(node_w[:, :, :], node_sum[:, :, :], ACT.Exp).then_inc(s_exp, 1)

        @block.tensor
        def _(pe):
            with pe.If(listed(nc, pe, g, layer) == 1):
                def step(e, n, second, last):
                    pe.wait_ge(s_diag, n + 1)
                    for m in range(1 if second else 1 + H):
                        mm = nc.tensor.matmul(ps[:, m, 0:P], ones[:, :], diag[:, m, :], start=True, stop=True)
                    mm.then_inc(s_bc, 1)
                    if second:
                        pe.wait_ge(s_prod, n - (ET - 1))
                        nc.tensor.matmul(ps[:, 6, 0:W], same[:, :], rows[:, 0:W], start=True, stop=True
                                         ).then_inc(s_bc, 1)

                tiles(pe, step)

        @block.vector
        def _(dve):
            with dve.If(listed(nc, dve, g, layer) == 1):
                CHAIN = {False: 3 + 2 * H, True: 7}

                nc.vector.memset(src_of[True][:, :], 0).then_inc(s_c, 1)
                nc.vector.memset(dst_of[True][:, :], N).then_inc(s_c, 1)
                nc.vector.memset(ones[:, :], 1.0).then_inc(s_c, 1)
                nc.vector.tensor_copy(state[:, :, 0:H], scores[:, :, H:2 * H]).then_inc(s_c, 1)
                nc.vector.tensor_copy(state[:, :, H:2 * H], scores[:, :, 0:H]).then_inc(s_c, 1)
                nc.vector.memset(sums[:, :, :], 0.0).then_inc(s_c, 1)
                dve.wait_ge(s_c, 6)
                dve.sem_inc(s_set, 1)
                dve.sem_inc(s_free, 1)

                def step(e, n, second, last):
                    if not second:
                        links = 6 + n * CHAIN[False]
                    else:
                        links = 6 + ET * CHAIN[False] + (n - ET) * CHAIN[True]
                    done = [0]

                    def then(ins):
                        done[0] += 1
                        ins.then_inc(s_c, 1)
                        dve.wait_ge(s_c, links + done[0])

                    dve.wait_ge(s_list, n * 32 + 32)
                    then(nc.vector.tensor_copy(dst_f[:, :], dst_of[last][:, :]))
                    if second:
                        dve.wait_ge(s_got, n * 16 + 16)
                        nc.vector.tensor_scalar(diag[:, 0, :], ident[:, :], dst_f[:, 0:1], None, ALU.mult
                                                ).then_inc(s_diag, 1)
                    else:
                        nc.vector.tensor_scalar(diag[:, 0, :], ident[:, :], dst_f[:, 0:1], None, ALU.mult)
                        dve.wait_ge(s_got, n * 16 + 16)
                        for h in range(H):
                            ins = nc.vector.tensor_scalar(diag[:, 1 + h, :], ident[:, :],
                                                          rows[:, F + H + h:F + H + h + 1], None, ALU.mult)
                        ins.then_inc(s_diag, 1)
                    if second:
                        dve.wait_ge(s_bc, ET + (n - ET) * 2 + 1)
                        then(nc.vector.tensor_scalar(same[:, :], ps[:, 0, 0:P], dst_f[:, 0:1], None, ALU.is_equal))
                        dve.wait_ge(s_node, ET * 16 + (n - ET) * 32 + 32)
                        then(nc.vector.tensor_tensor(guard[:, :], node[:, 0:H], node[:, H:2 * H], ALU.add))
                        then(nc.vector.scalar_tensor_tensor(guard[:, :], guard[:, :], SLOPE, guard[:, :],
                                                            ALU.mult, ALU.max))
                        then(nc.vector.tensor_tensor(e_sum[:, :], node[:, 0:H], rows[:, F + H:F + 2 * H], ALU.add))
                        then(nc.vector.scalar_tensor_tensor(e_sum[:, :], e_sum[:, :], SLOPE, e_sum[:, :],
                                                            ALU.mult, ALU.max))
                        nc.vector.tensor_tensor(e_sum[:, :], e_sum[:, :], guard[:, :], ALU.subtract
                                                ).then_inc(s_score, 1)
                        dve.wait_ge(s_exp, n - (ET - 1))
                        w_rows = rows[:, 0:W].rearrange("p (h c) -> p h c", h=H)
                        nc.vector.tensor_tensor(w_rows, w_rows, weight[:, :].unsqueeze(2).to_broadcast(
                            [P, H, W // H]), ALU.mult).then_inc(s_prod, 1)
                        dve.wait_ge(s_bc, ET + (n - ET) * 2 + 2)
                        then(nc.vector.tensor_tensor(total[:, :], ps[:, 6, 0:W], total[:, :], ALU.add))
                        assert done[0] == CHAIN[True]
                        dve.sem_inc(s_new, 1)
                    else:
                        dve.wait_ge(s_bc, n + 1)
                        then(nc.vector.tensor_scalar(same[:, :], ps[:, 0, 0:P], dst_f[:, 0:1], None, ALU.is_equal))
                        then(nc.vector.tensor_scalar(out_of[:, :], same[:, :], -1.0, FAR, ALU.add, ALU.mult))
                        for h in range(H):
                            then(nc.vector.tensor_tensor(held[:, h, :], ps[:, 1 + h, 0:P], out_of[:, :], ALU.add))
                            then(nc.vector.tensor_reduce(best[:, h:h + 1], held[:, h, :], AX.X, ALU.max))
                        assert done[0] == CHAIN[False]
                        dve.wait_ge(s_node, n * 16 + 16)
                        nc.vector.tensor_tensor(node[:, H:2 * H], node[:, H:2 * H], best[:, :], ALU.max
                                                ).then_inc(s_new, 1)

                tiles(dve, step)
                done = [6 + ET * (CHAIN[False] + CHAIN[True])]

                def then(ins):
                    done[0] += 1
                    ins.then_inc(s_c, 1)
                    dve.wait_ge(s_c, done[0])

                dve.wait_ge(s_back, 32)
                then(nc.vector.tensor_tensor(node_guard[:, :, :], state[:, :, 0:H], state[:, :, H:2 * H], ALU.add))
                then(nc.vector.scalar_tensor_tensor(node_guard[:, :, :], node_guard[:, :, :], SLOPE,
                                                    node_guard[:, :, :], ALU.mult, ALU.max))
                then(nc.vector.tensor_tensor(node_sum[:, :, :], scores[:, :, 0:H], scores[:, :, H:2 * H], ALU.add))
                then(nc.vector.scalar_tensor_tensor(node_sum[:, :, :], node_sum[:, :, :], SLOPE,
                                                    node_sum[:, :, :], ALU.mult, ALU.max))
                nc.vector.tensor_tensor(node_sum[:, :, :], node_sum[:, :, :], node_guard[:, :, :], ALU.subtract
                                        ).then_inc(s_score, 1)
                dve.wait_ge(s_exp, ET + 1)
                own = acc[:, :, 0:W].rearrange("p n (h c) -> p n h c", h=H)
                then(nc.vector.tensor_tensor(own, own, node_w[:, :, :].unsqueeze(3).to_broadcast(
                    [P, NT, H, W // H]), ALU.mult))
                for r in range(R):
                    dve.wait_ge(s_back, (r + 2) * 16)
                    nc.vector.tensor_tensor(acc[:, r * 7:(r + 1) * 7, 0:W], acc[:, r * 7:(r + 1) * 7, 0:W],
                                            sums[:, :, :], ALU.add).then_inc(s_taken, 1)


def edges_and_mixture(nc, g):
    N, F, NT, LAST, KC, X, ITERS = (g[k] for k in ("N", "F", "NT", "LAST", "KC", "X", "ITERS"))
    ps, ident, bias_rows = g["ps"], g["ident"], g["bias_rows"]
    ffn, x, out = g["ffn"], g["x"], g["out"]
    rows_dram = g["rows_dram"][1]
    W = F + 1
    NB = BODY // BATCH
    TOK = GT * P
    GROUPS = (NT - 1) // GT
    assert NT - 1 == GROUPS * GT and GROUPS + 1 >= ITERS
    PRE_STEPS = (0, 4, 7, 10, 13, 16, 19, 22, 24)
    PRE = len(PRE_STEPS) - 1
    with ExitStack() as ctx:
        def sb(name, shape, dt=F32):
            return ctx.enter_context(nc.sbuf_tensor(f"m_{name}", shape, dt))

        sem = g["sem"]
        w_hi = sb("w_hi", [P, 3, X, KC, F], F32R)
        w_lo = sb("w_lo", [P, 3, X, KC, F], F32R)
        h_hi = sb("h_hi", [P, 2, KC, TOK], F32R)
        h_lo = sb("h_lo", [P, 2, KC, TOK], F32R)
        h_f = sb("h_f", [P, 2, TOK])
        x_hi = sb("x_hi", [P, KC, TOK], F32R)
        x_lo = sb("x_lo", [P, KC, TOK], F32R)
        xr = sb("xr", [P, 2, GT, F])
        own = sb("own", [P, GT, F + 2])
        xn = own
        bn = sb("bn", [P, 2, 5, KC, X])
        bn_s = sb("bn_s", [P, 2, KC, X])
        bn_t = sb("bn_t", [P, 2, KC, X])
        wr = sb("wr", [P, KC, X])
        br = sb("br", [P, X])
        bo = sb("bo", [X, F])
        stats = sb("stats", [P, GT, 6])
        mv = sb("mv", [P, GT, 2])
        rstd = sb("rstd", [P, GT, 1])
        eps = sb("eps", [P, 3])
        zinv = sb("zinv", [P, GT, 1])
        logit = sb("logit", [P, GT, X])
        lmax = sb("lmax", [P, GT, 1])
        lsum = sb("lsum", [P, GT, 1])
        prob = sb("prob", [P, GT, X])
        probT = sb("probT", [X, GT, P])
        sums = sb("sums", [P, SUM_TILES, W])
        w_raw = h_f

        def xr_half(half, tiles):
            return xr[:, bass.ds(half, 1), 0:tiles, :].rearrange("p a n f -> p (a n) f")

        assert TOK == KC * F

        table, self_w, s_table, guard_act, guard_dve = guards(nc, g, 1, sb, sem)
        parts = edge_parts(nc, g, 1, sb, sem, table, s_table, sums, RING2, "ring")

        s_small, s_eps, s_bnc, s_bnq, s_turn = (
            sem("small_landed"), sem("eps_set"), sem("bn_chain"), sem("bn_sqrt"), sem("turn"))
        s_sp_turn = sem("load_turn_m")
        s_raw = [sem("raw_landed0"), sem("raw_landed1")]
        s_whi, s_wlo = sem("w_hi_ready"), sem("w_lo_ready")
        s_x, s_own, s_own_free = sem("x_landed"), sem("own_rows_landed"), sem("own_rows_used")
        s_zer = sem("sums_zeroed")
        s_c, s_sq, s_xn, s_tr = sem("norm_chain"), sem("std_ready"), sem("norm_ready"), sem("transposed")
        s_st = sem("stats_ready")
        s_r = sem("router_chain")
        s_xhi, s_xlo, s_xf = sem("x_hi_ready"), sem("x_lo_ready"), sem("xT_ready")
        s_log, s_lm, s_ex, s_pr, s_pt, s_ptc, s_bop, s_yin = (
            sem("logits_ready"), sem("logits_less_max"), sem("router_exp"), sem("prob_ready"), sem("prob_transposed"),
            sem("probT_ready"), sem("bias_product"), sem("bias_added"))
        s_h, s_hf, s_hhi, s_hlo = sem("hidden_product"), sem("hidden_ready"), sem("hidden_hi"), sem("hidden_lo")
        s_y, s_ya, s_out = sem("y_product"), sem("y_added"), sem("stored")
        block = ctx.enter_context(nc.Block())
        names = (("b1", "g1", "be1", "m1", "v1"), ("b2", "g2", "be2", "m2", "v2"))
        CH = 2 * KC * X
        NSM = 2 * 5 * KC * X + 3 + KC - 1
        NW = 3 * X

        def products_of(tiles):
            yield "hidden", 0, 0, 0, 7
            yield "hidden", 0, 0, 1, 5
            for e in range(X):
                yield "hidden", 1, e, 0, 5
                yield "hidden", 1, e, 1, 6
                if e + 1 < X:
                    yield "hidden", 0, e + 1, 0, 7
                    yield "hidden", 0, e + 1, 1, 5
                yield "output", 2, e, 0, 6
                if tiles > 2:
                    yield "output", 2, e, 1, 7

        slots = list(products_of(GT))
        SLOTS = len(slots)
        hidden = [(m, e, c) for kind, m, e, c, _ in slots if kind == "hidden"]
        rank = {k: n for n, k in enumerate(hidden)}

        def step_of(k):
            if k < 0:
                return PRE_STEPS[k + PRE]
            return PRE_STEPS[-1] + (BODY - PRE_STEPS[-1]) * k // SLOTS

        def outputs_before(grp, tiles, e, c):
            return grp * 2 * X + e * (2 if tiles > 2 else 1) + c

        def slots_of_group(tiles):
            return len(list(products_of(tiles)))

        def schedule(eng, ordered, edge, ffn_part):
            def iteration(i, edges, group, tiles, last=False):
                edges = edges and ordered
                for k in range(-PRE, SLOTS if tiles != 1 else slots_of_group(1)):
                    ffn_part(i, group, tiles, k)
                    if edges:
                        for j in range(step_of(k), step_of(k + 1)):
                            edge(i, j, last)

            iteration(0, True, None, 0)
            with eng.Fori(1, ITERS - 1) as i:
                iteration(i, True, i - 1, GT)
            iteration(ITERS - 1, True, ITERS - 2, GT, last=True)
            for group in range(ITERS - 1, GROUPS):
                iteration(group + 1, False, group, GT)
            iteration(GROUPS + 1, False, GROUPS, 1)

        @block.sync
        def _(sp):
            def program(ordered):
                for l in (0, 1):
                    for n, name in enumerate(names[l]):
                        for k in range(KC):
                            for e in range(X):
                                sp.dma_start(bn[:, l, n, k, e:e + 1],
                                             ffn[name][e, k * P:(k + 1) * P].rearrange("(p a) -> p a", a=1)
                                             ).then_inc(s_small, 16)
                for k in range(KC):
                    sp.dma_start(wr[:, k, :], ffn["Wr"][k * P:(k + 1) * P, :]).then_inc(s_small, 16)
                sp.dma_start(br[:, :], ffn["br"].partition_broadcast(P)).then_inc(s_small, 16)
                sp.dma_start(bo[:, :], ffn["bo"]).then_inc(s_small, 16)

                if ordered:
                    for jb in range(2):
                        parts.sync_batch(sp, 0, jb)

                def edge(i, j, last):
                    jb = j // BATCH + 2
                    if j % BATCH == 0 and not (last and jb >= NB):
                        parts.sync_batch(sp, i + jb // NB, jb % NB)

                def load_group(grp, tiles):
                    if tiles == 1:
                        sp.dma_start(xr[0:LAST, GROUPS % 2, 0, :], x[(NT - 1) * P:N, :]).then_inc(s_x, 16)
                        sp.dma_start(own[:, 0:1, :], rows_dram[(NT - 1) * P:NT * P, :].rearrange(
                            "(n p) c -> p n c", p=P)).then_inc(s_own, 16)
                    else:
                        sp.dma_start(xr_half(grp % 2, GT), x[bass.ds(grp * TOK, TOK), :].rearrange(
                            "(n p) f -> p n f", p=P)).then_inc(s_x, 16)
                        sp.dma_start(own[:, :, :], rows_dram[bass.ds(grp * TOK, TOK), :].rearrange(
                            "(n p) c -> p n c", p=P)).then_inc(s_own, 16)

                sp.wait_ge(s_eps, 4)
                load_group(0, GT)
                sp.sem_inc(s_out, 16)

                def part(i, grp, tiles, k):
                    if grp is None:
                        if k >= 0:
                            n = k // 2
                            if k % 2 or n >= NW:
                                return
                            if n >= 2:
                                sp.wait_ge(s_wlo, n - 1)
                            sp.dma_start(w_raw[:, n % 2, :].rearrange("p (k n) -> p k n", n=F),
                                         ffn[("W1", "W2", "Wo")[n // X]][n % X].rearrange("(k p) n -> p k n", p=P)
                                         ).then_inc(s_raw[n % 2], 16)
                        return
                    if k == -PRE:
                        pass
                    half = grp % 2
                    if k == 4:
                        nxt = grp + 1
                        if tiles == GT:
                            sp.wait_ge(s_tr, KC * nxt)
                            sp.sem_inc(s_sp_turn, 1)
                            sp.wait_ge(s_out, 16 * nxt)
                            sp.sem_inc(s_sp_turn, 1)
                            load_group(nxt, GT if not isinstance(nxt, int) or nxt < GROUPS else 1)
                    if k == slots_of_group(tiles) - 1:
                        sp.wait_ge(s_ya, 1 + grp * GT * X + tiles * X)
                        sp.sem_inc(s_sp_turn, 1)
                        if tiles == 1:
                            sp.dma_start(out[(NT - 1) * P:N, :], xr[0:LAST, GROUPS % 2, 0, :]).then_inc(s_out, 16)
                        else:
                            sp.dma_start(out[bass.ds(grp * TOK, TOK), :].rearrange("(n p) f -> p n f", p=P),
                                         xr_half(half, GT)).then_inc(s_out, 16)

                schedule(sp, ordered, edge, part)
                sp.wait_ge(s_out, 16 * (GROUPS + 2))

            with sp.If(listed(nc, sp, g, 1) == 0):
                program(True)
            with sp.If(listed(nc, sp, g, 1) == 1):
                program(False)

        @block.gpsimd
        def _(pool):
            def program(ordered):

                if ordered:
                    with pool.Fori(0, ITERS) as i:
                        for jb in range(NB):
                            parts.gpsimd_batch(pool, i, jb)

            with pool.If(listed(nc, pool, g, 1) == 0):
                program(True)

        @block.scalar
        def _(act):
            def program(ordered):
                if ordered:
                    parts.scalar_start(act)
                    guard_act(act)
                act.wait_ge(s_eps, 3)
                act.wait_ge(s_small, 16 * NSM)
                nc.scalar.activation(bn[:, :, 4, :, :], bn[:, :, 4, :, :], ACT.Sqrt, bias=eps[:, 1:2]).then_inc(s_bnq, 1)
                if ordered:
                    parts.scalar_first(act)

                def edge(i, j, last):
                    jb, q = j // BATCH, j % BATCH
                    if q == 1 and not (last and jb == NB - 1):
                        parts.scalar_batch(act, i, jb)
                    if q == 7:
                        parts.scalar_index(act, i, jb, last)

                def part(i, grp, tiles, k):
                    if grp is None:
                        if k >= 0:
                            n = k // 2
                            if k % 2 or n >= NW:
                                return
                            act.wait_ge(s_raw[n % 2], 16 * (n // 2 + 1))
                            nc.scalar.activation(w_hi[:, n // X, n % X, :, :].rearrange("p k n -> p (k n)"),
                                                 w_raw[:, n % 2, :], ACT.Copy).then_inc(s_whi, 1)
                        return
                    T = tiles * P
                    if k == -PRE + 2:
                        act.wait_ge(s_st, grp + 1)
                        nc.scalar.activation(rstd[:, 0:tiles, :], mv[:, 0:tiles, 1:2], ACT.Sqrt, bias=eps[:, 0:1]
                                             ).then_inc(s_sq, 1)
                    if k == -PRE + 1:
                        act.wait_ge(s_own_free, grp + 1)
                        if tiles == GT:
                            nc.scalar.activation(sums[:, bass.ds((grp % (SUM_TILES // GT)) * GT, GT), :],
                                                 eps[:, 2:3].unsqueeze(1).to_broadcast([P, GT, W]), ACT.Copy
                                                 ).then_inc(s_zer, 1)
                    if k == -PRE + 3:
                        for c in range(KC):
                            act.wait_ge(s_tr, grp * KC + c + 1)
                            nc.scalar.activation(h_f[:, c, 0:T], ps[:, 5 + c, 0:T], ACT.Copy).then_inc(s_xf, 1)
                            nc.scalar.activation(x_hi[:, c, 0:T], ps[:, 5 + c, 0:T], ACT.Copy).then_inc(s_xhi, 1)
                    if k == -PRE + 4:
                        act.wait_ge(s_lm, grp + 1)
                        nc.scalar.activation(prob[:, 0:tiles, :], logit[:, 0:tiles, :], ACT.Exp).then_inc(s_ex, 1)
                    if k >= 0:
                        kind, m, e, c, bank = list(products_of(tiles))[k]
                        if kind == "output":
                            return
                        r = rank[(m, e, c)]
                        if r < 2:
                            act.wait_ge(s_log, grp + 1)
                            act.wait_ge(s_xlo, grp * KC + KC)
                        else:
                            act.wait_ge(s_hlo, grp * CH + r - 1)
                        act.wait_ge(s_h, grp * CH + r + 1)
                        product = ps[:, bank, 0:T]
                        scale, shift = bn_s[:, m, c, e:e + 1], bn_t[:, m, c, e:e + 1]
                        nc.scalar.activation(h_f[:, r % 2, 0:T], product, ACT.Relu, bias=shift, scale=scale
                                             ).then_inc(s_hf, 1)
                        nc.scalar.activation(h_hi[:, m, c, 0:T], product, ACT.Relu, bias=shift, scale=scale
                                             ).then_inc(s_hhi, 1)

                schedule(act, ordered, edge, part)

            with act.If(listed(nc, act, g, 1) == 0):
                program(True)
            with act.If(listed(nc, act, g, 1) == 1):
                program(False)

        @block.vector
        def _(dve):
            def program(ordered):
                done = [0]
                state = {}

                def then(ins):
                    done[0] += 1
                    ins.then_inc(s_bnc, 1)
                    dve.wait_ge(s_bnc, done[0])

                nc.vector.memset(eps[:, 0:1], LN_EPS).then_inc(s_eps, 1)
                nc.vector.memset(eps[:, 1:2], BN_EPS).then_inc(s_eps, 1)
                nc.vector.memset(eps[:, 2:3], 0.0).then_inc(s_eps, 1)
                nc.vector.memset(sums[:, :, :], 0.0).then_inc(s_eps, 1)
                dve.wait_ge(s_eps, 4)
                if ordered:
                    guard_dve(dve)
                    parts.vector_start(dve)
                else:
                    nc.vector.memset(self_w[:, :, :], 1.0).then_inc(s_eps, 1)
                    dve.wait_ge(s_eps, 5)
                dve.wait_ge(s_small, 16 * NSM)
                dve.wait_ge(s_bnq, 1)
                then(nc.vector.reciprocal(bn[:, :, 4, :, :], bn[:, :, 4, :, :]))
                then(nc.vector.tensor_tensor(bn_s[:, :, :, :], bn[:, :, 4, :, :], bn[:, :, 1, :, :], ALU.mult))
                then(nc.vector.tensor_tensor(bn_t[:, :, :, :], bn[:, :, 0, :, :], bn[:, :, 3, :, :], ALU.subtract))
                then(nc.vector.tensor_tensor(bn_t[:, :, :, :], bn_t[:, :, :, :], bn_s[:, :, :, :], ALU.mult))
                then(nc.vector.tensor_tensor(bn_t[:, :, :, :], bn_t[:, :, :, :], bn[:, :, 2, :, :], ALU.add))
                dve.sem_inc(s_ya, 1)
                if ordered:
                    parts.vector_first(dve)

                def edge(i, j, last):
                    parts.vector_piece(dve, i, j, last, state)
                    if last and j == BODY - 1:
                        parts.vector_last(dve, state)

                def part(i, grp, tiles, k):
                    if grp is None:
                        if k >= 0:
                            n = k // 2
                            if k % 2 or n >= NW:
                                return
                            dve.wait_ge(s_whi, n + 1)
                            nc.vector.tensor_tensor(w_lo[:, n // X, n % X, :, :].rearrange("p k n -> p (k n)"),
                                                    w_raw[:, n % 2, :],
                                                    w_hi[:, n // X, n % X, :, :].rearrange("p k n -> p (k n)").bitcast(F32),
                                                    ALU.subtract).then_inc(s_wlo, 1)
                        return
                    T = tiles * P
                    half = grp % 2
                    mine = xr_half(half, tiles)

                    def my_tile(q):
                        return xr[:, bass.ds(half, 1), q, :].rearrange("p a f -> p (a f)")

                    if k == -PRE:
                        dve.wait_ge(s_x, 16 * grp + 16)
                        dve.wait_ge(s_own, 16 * grp + 16)
                        loop_w = self_w[:, bass.ds(grp * GT, tiles), :].to_broadcast([P, tiles, W])
                        nc.vector.tensor_tensor(own[:, 0:tiles, 0:W], own[:, 0:tiles, 0:W], loop_w, ALU.mult
                                                ).then_inc(s_c, 1)
                        nc.vector.tensor_tensor(mine, mine, bias_rows[:, 1, :].unsqueeze(1).to_broadcast([P, tiles, F]),
                                                ALU.add).then_inc(s_c, 1)
                    if k == -PRE + 1:
                        if not ordered:
                            pass
                        elif isinstance(grp, int) and grp >= ITERS - 1:
                            dve.wait_ge(parts.sums_added, 2 * NB * ITERS)
                        else:
                            dve.wait_ge(parts.sums_added, 2 * NB * (grp + 1))
                        dve.wait_ge(s_c, grp * 6 + 1)
                        nc.vector.tensor_tensor(own[:, 0:tiles, 0:W], own[:, 0:tiles, 0:W],
                                                sums[:, bass.ds((grp % (SUM_TILES // GT)) * GT, tiles), 0:W], ALU.add
                                                ).then_inc(s_own_free, 1)
                        dve.wait_ge(s_own_free, grp + 1)
                        nc.vector.reciprocal(zinv[:, 0:tiles, :], own[:, 0:tiles, F:F + 1]).then_inc(s_c, 1)
                        dve.wait_ge(s_c, grp * 6 + 3)
                        for q in range(tiles):
                            ins = nc.vector.scalar_tensor_tensor(my_tile(q), own[:, q, 0:F], zinv[:, q, :], my_tile(q),
                                                                 ALU.mult, ALU.add)
                        ins.then_inc(s_c, 1)
                        dve.wait_ge(s_c, grp * 6 + 4)
                        dve.sem_inc(s_turn, 1)
                        for q in range(tiles):
                            ins = nc.vector.bn_stats(stats[:, q, :], my_tile(q))
                        ins.then_inc(s_c, 1)
                        dve.wait_ge(s_c, grp * 6 + 5)
                        dve.sem_inc(s_turn, 1)
                        for q in range(tiles):
                            ins = nc.vector.bn_aggr(mv[:, q, :], stats[:, q, :])
                        ins.then_inc(s_st, 1)
                    if k == -PRE + 2:
                        if tiles == GT:
                            dve.wait_ge(s_zer, grp + 1)
                        dve.wait_ge(s_sq, grp + 1)
                        nc.vector.reciprocal(rstd[:, 0:tiles, :], rstd[:, 0:tiles, :]).then_inc(s_c, 1)
                        dve.wait_ge(s_c, grp * 6 + 6)
                        for q in range(tiles):
                            nc.vector.tensor_scalar(xn[:, q, 0:F], my_tile(q), mv[:, q, 0:1], rstd[:, q, :],
                                                    ALU.subtract, ALU.mult).then_inc(s_xn, 1)
                    if k == -PRE + 3:
                        for c in range(KC):
                            dve.wait_ge(s_xhi, grp * KC + c + 1)
                            nc.vector.tensor_tensor(x_lo[:, c, 0:T], h_f[:, c, 0:T], x_hi[:, c, 0:T].bitcast(F32),
                                                    ALU.subtract).then_inc(s_xlo, 1)
                    if k == -PRE + 4:
                        dve.wait_ge(s_log, grp + 1)
                        nc.vector.tensor_tensor(logit[:, 0:tiles, :], ps[:, 7, 0:tiles * X].rearrange("p (n e) -> p n e", e=X),
                                                br[:, :].unsqueeze(1).to_broadcast([P, tiles, X]), ALU.add
                                                ).then_inc(s_r, 1)
                        dve.wait_ge(s_r, grp * 4 + 1)
                        nc.vector.tensor_reduce(lmax[:, 0:tiles, :], logit[:, 0:tiles, :], AX.X, ALU.max).then_inc(s_r, 1)
                        dve.wait_ge(s_r, grp * 4 + 2)
                        nc.vector.tensor_tensor(logit[:, 0:tiles, :], logit[:, 0:tiles, :],
                                                lmax[:, 0:tiles, :].to_broadcast([P, tiles, X]), ALU.subtract
                                                ).then_inc(s_lm, 1)
                    if k == -PRE + 5:
                        dve.wait_ge(s_ex, grp + 1)
                        nc.vector.tensor_reduce(lsum[:, 0:tiles, :], prob[:, 0:tiles, :], AX.X, ALU.add).then_inc(s_r, 1)
                        dve.wait_ge(s_r, grp * 4 + 3)
                        nc.vector.reciprocal(lsum[:, 0:tiles, :], lsum[:, 0:tiles, :]).then_inc(s_r, 1)
                        dve.wait_ge(s_r, grp * 4 + 4)
                        nc.vector.tensor_tensor(prob[:, 0:tiles, :], prob[:, 0:tiles, :],
                                                lsum[:, 0:tiles, :].to_broadcast([P, tiles, X]), ALU.mult
                                                ).then_inc(s_pr, 1)
                    if k == -PRE + 6:
                        dve.wait_ge(s_pt, grp + 1)
                        nc.vector.tensor_copy(probT[:, 0:tiles, :], ps[0:X, 5, 0:T].rearrange("e (n p) -> e n p", p=P)
                                              ).then_inc(s_ptc, 1)
                    if k == -PRE + 7:
                        for q in range(tiles):
                            if q % 2 == 0:
                                dve.wait_ge(s_bop, grp * 2 + q // 2 + 1)
                            nc.vector.tensor_tensor(my_tile(q), ps[:, 7 - q // 2, (q % 2) * F:(q % 2 + 1) * F],
                                                    my_tile(q), ALU.add).then_inc(s_yin, 1)
                    if k >= 0:
                        kind, m, e, c, bank = list(products_of(tiles))[k]
                        if kind == "hidden":
                            r = rank[(m, e, c)]
                            dve.wait_ge(s_hhi, grp * CH + r + 1)
                            nc.vector.tensor_tensor(h_lo[:, m, c, 0:T], h_f[:, r % 2, 0:T],
                                                    h_hi[:, m, c, 0:T].bitcast(F32), ALU.subtract).then_inc(s_hlo, 1)
                        else:
                            for q in range(2 * c, min(2 * c + 2, tiles)):
                                n = e * tiles + q
                                if q % 2 == 0:
                                    dve.wait_ge(s_y, outputs_before(grp, tiles, e, c) + 1)
                                if e == 0:
                                    dve.wait_ge(s_yin, grp * GT + q + 1)
                                else:
                                    dve.wait_ge(s_ya, 1 + grp * GT * X + n - tiles + 1)
                                nc.vector.scalar_tensor_tensor(
                                    my_tile(q), ps[:, bank, (q % 2) * F:(q % 2 + 1) * F], prob[:, q, e:e + 1],
                                    my_tile(q), ALU.mult, ALU.add).then_inc(s_ya, 1)

                schedule(dve, ordered, edge, part)

            with dve.If(listed(nc, dve, g, 1) == 0):
                program(True)
            with dve.If(listed(nc, dve, g, 1) == 1):
                program(False)

        @block.tensor
        def _(pe):
            def program(ordered):
                state = {}
                if ordered:
                    parts.tensor_start(pe)
                    parts.node_products(pe, 0, 0)
                    parts.node_products(pe, 0, 1)

                def edge(i, j, last):
                    parts.tensor_step(pe, i, j, last, state)

                def split_product(bank, a_hi, a_lo, b_hi, b_lo):
                    pairs = [(a_hi[k], b_hi[k]) for k in range(KC)] + [(a_lo[k], b_hi[k]) for k in range(KC)] + \
                        [(a_hi[k], b_lo[k]) for k in range(KC)]
                    for n, (a, b) in enumerate(pairs):
                        mm = nc.tensor.matmul(bank, a, b, start=n == 0, stop=n == len(pairs) - 1)
                    return mm

                def part(i, grp, tiles, k):
                    if grp is None:
                        return
                    T = tiles * P
                    if k == -PRE + 3:
                        pe.wait_ge(s_ya, 1 + grp * GT * X)
                        pe.wait_ge(s_wlo, NW)
                        pe.wait_ge(s_xn, grp * GT + tiles)
                        for c in range(KC):
                            for q in range(tiles):
                                mm = nc.tensor.transpose(ps[:, 5 + c, q * P:(q + 1) * P], xn[:, q, c * P:(c + 1) * P],
                                                         ident[:, :])
                            mm.then_inc(s_tr, 1)
                    if k == -PRE + 4:
                        pe.wait_ge(s_xf, grp * KC + KC)
                        for q in range(tiles):
                            for c in range(KC):
                                mm = nc.tensor.matmul(ps[:, 7, q * X:(q + 1) * X], h_f[:, c, q * P:(q + 1) * P],
                                                      wr[:, c, :], start=c == 0, stop=c == KC - 1)
                        mm.then_inc(s_log, 1)
                    if k == -PRE + 5:
                        pe.wait_ge(s_xhi, grp * KC + KC)
                        pe.wait_ge(s_pr, grp + 1)
                        for q in range(tiles):
                            mm = nc.tensor.transpose(ps[0:X, 5, q * P:(q + 1) * P], prob[:, q, :], ident[:, :])
                        mm.then_inc(s_pt, 1)
                    if k == -PRE + 6:
                        pe.wait_ge(s_ptc, grp + 1)
                        for q in range(tiles):
                            mm = nc.tensor.matmul(ps[:, 7 - q // 2, (q % 2) * F:(q % 2 + 1) * F], probT[:, q, :],
                                                  bo[:, :], start=True, stop=True)
                            if q % 2 or q == tiles - 1:
                                mm.then_inc(s_bop, 1)
                    if k == 0:
                        pe.wait_ge(s_xlo, grp * KC + KC)
                        pe.wait_ge(s_yin, grp * GT + tiles)
                    if k < 0:
                        return
                    kind, m, e, c, bank = list(products_of(tiles))[k]
                    done_before = 1 + grp * GT * X
                    if kind == "hidden":
                        if m == 1 and c == 0:
                            pe.wait_ge(s_hlo, grp * CH + rank[(0, e, KC - 1)] + 1)
                        if bank == 6 and e >= 1:
                            pe.wait_ge(s_ya, done_before + (e - 1) * tiles + min(2, tiles))
                        if bank == 7 and e >= 2:
                            pe.wait_ge(s_ya, done_before + (e - 1) * tiles)
                        if m == 0 and c == 1 and e >= 1:
                            pe.wait_ge(s_hhi, grp * CH + rank[(1, e - 1, 0)] + 1)
                        cols = slice(c * P, (c + 1) * P)
                        a_hi = [w_hi[:, m, e, kc, cols] for kc in range(KC)]
                        a_lo = [w_lo[:, m, e, kc, cols] for kc in range(KC)]
                        if m == 0:
                            b_hi, b_lo = [x_hi[:, kc, 0:T] for kc in range(KC)], [x_lo[:, kc, 0:T] for kc in range(KC)]
                        else:
                            b_hi, b_lo = [h_hi[:, 0, kc, 0:T] for kc in range(KC)], [h_lo[:, 0, kc, 0:T] for kc in range(KC)]
                        split_product(ps[:, bank, 0:T], a_hi, a_lo, b_hi, b_lo).then_inc(s_h, 1)
                    else:
                        if c == 0:
                            pe.wait_ge(s_hlo, grp * CH + rank[(1, e, KC - 1)] + 1)
                        elif e + 1 < X:
                            pe.wait_ge(s_hhi, grp * CH + rank[(0, e + 1, 0)] + 1)
                        else:
                            pe.wait_ge(s_ya, done_before + e * tiles)
                        for q in range(2 * c, min(2 * c + 2, tiles)):
                            toks = slice(q * P, (q + 1) * P)
                            mm = split_product(ps[:, bank, (q % 2) * F:(q % 2 + 1) * F],
                                               [h_hi[:, 1, kc, toks] for kc in range(KC)],
                                               [h_lo[:, 1, kc, toks] for kc in range(KC)],
                                               [w_hi[:, 2, e, kc, :] for kc in range(KC)],
                                               [w_lo[:, 2, e, kc, :] for kc in range(KC)])
                        mm.then_inc(s_y, 1)

                schedule(pe, ordered, edge, part)

            with pe.If(listed(nc, pe, g, 1) == 0):
                program(True)
            with pe.If(listed(nc, pe, g, 1) == 1):
                program(False)


_GNN = ("W", "a_src", "a_dst", "b")
_FFN = ("Wr", "br", "W1", "b1", "g1", "be1", "m1", "v1", "W2", "b2", "g2", "be2", "m2", "v2", "Wo", "bo")
_INS = ["x", "src", "dst"] + [f"L0_gnn_{n}{l}" for l in (1, 2) for n in _GNN] + [f"L0_ffn_{n}" for n in _FFN]


def kernel(**inputs):
    import numpy as _np
    import concourse.bacc as _bacc
    from concourse import mybir as _mybir
    from concourse.bass_utils import run_bass_kernel_spmd as _run

    nc = _bacc.Bacc("TRN2", target_bir_lowering=False, num_devices=1)
    arrays, aps = {}, {}
    for name in _INS:
        a = _np.ascontiguousarray(inputs[name])
        arrays[f"in_{name}_dram"] = a
        aps[name] = nc.dram_tensor(f"in_{name}_dram", a.shape, _mybir.dt.from_np(a.dtype), kind="ExternalInput").ap()
    shape = arrays["in_x_dram"].shape
    out = nc.dram_tensor("out_0_dram", shape, _mybir.dt.float32, kind="ExternalOutput").ap()
    gnn = [{n: aps[f"L0_gnn_{n}{l}"] for n in _GNN} for l in (1, 2)]
    ffn = {n: aps[f"L0_ffn_{n}"] for n in _FFN}
    build_program(nc, aps["x"], aps["src"], aps["dst"], gnn, ffn, out)
    r = _run(nc, [arrays], core_ids=[0])
    return r.results[0]["out_0_dram"]
```

```python
from contextlib import ExitStack, contextmanager

import numpy as np

import concourse.bass as bass
from concourse import mybir

F32 = mybir.dt.float32
F32R = mybir.dt.float32r
BF16 = mybir.dt.bfloat16
I32 = mybir.dt.int32
ALU = mybir.AluOpType
ACT = mybir.ActivationFunctionType
AX = mybir.AxisListType

P = 128
LN_EPS = 1e-5
BN_EPS = 1e-3
SLOPE = 0.2

BATCH = 8
UNIT = 4
BODY = 80
RING = 40
RING2 = 20
PARTS = 3
GT = 4
SUM_TILES = 16
MAX_SPREAD = 60.0
FAR = 1e30


def build_program(nc, x, src, dst, gnn, ffn, out):
    N, F = x.shape
    E = src.shape[0]
    NT = -(-N // P)
    LAST = N - (NT - 1) * P
    ET = -(-E // P)
    EG = -(-ET // P)
    STEPS = -(-(ET + NT - 1) // BODY) * BODY
    ITERS = STEPS // BODY
    NB = BODY // BATCH
    RB = RING // BATCH
    KC = F // P
    HEADS = [gnn[0]["a_src"].shape[0], gnn[1]["a_src"].shape[0]]
    HMAX = max(HEADS)
    ROW = F + 2 * HMAX
    X = ffn["Wr"].shape[1]
    TB = 7
    assert NT % TB == 0 and N == (NT - 1) * P + LAST and KC == 2
    SC = STEPS // 2
    SG = -(-STEPS // P)

    rows_dram = [nc.dram_tensor(f"node_rows_{l}", [NT * P, F + 2 * H], F32, kind="Internal").ap()
                 for l, H in enumerate(HEADS)]
    scores_dram = [nc.dram_tensor(f"node_scores_{l}", [NT * P, 2 * H], F32, kind="Internal").ap()
                   for l, H in enumerate(HEADS)]
    totals_dram = [nc.dram_tensor(f"node_totals_{l}", [NT * P, F + H], F32, kind="Internal").ap()
                   for l, H in enumerate(HEADS)]
    place_dram = nc.dram_tensor("edge_places", [STEPS, P], BF16, kind="Internal").ap()

    with ExitStack() as whole:
        def sb(name, shape, dt=F32):
            return whole.enter_context(nc.sbuf_tensor(name, shape, dt))

        ps = whole.enter_context(nc.psum_tensor("ps", [P, 8, 512], F32))
        ident = sb("ident", [P, P])
        lane = sb("lane", [P, P])
        part_iota = sb("part_iota", [P, 1])
        bias_rows = sb("bias_rows", [P, 2, F])
        edge_src = sb("edge_src", [P, STEPS])
        edge_place = sb("edge_place", [P, STEPS])
        scores = sb("scores", [P, NT, 2 * HMAX])
        step_tables = sb("step_tables", [P, STEPS], I32)
        step_node = step_tables[0:1, :]
        step_bank = step_tables[32:33, :]
        batch_nodes = {"all": step_tables[64:65, 0:2 * STEPS // BATCH],
                       "ring": step_tables[96:97, 0:2 * STEPS // BATCH]}

        disorder = sb("disorder", [1, 1])
        by_list = sb("by_list", [P, 2], I32)
        top = sb("top", [P, 2, 2 * HMAX])

        def for_pool(name, count):
            return [whole.enter_context(nc.semaphore(f"{name}{n}_")) for n in range(count)]

        stored = for_pool("rows_stored", 2)
        gathered = [for_pool("gathered_1_", RING // UNIT), for_pool("gathered_2_", RING2 // UNIT)]
        listed_rows = [for_pool("listed_1_", 3), for_pool("listed_2_", 3)]

        with ExitStack() as first:
            acc = first.enter_context(nc.sbuf_tensor("acc", [P, NT, ROW], F32))
            w_aug = first.enter_context(nc.sbuf_tensor("w_aug", [P, 2, KC, F + 2 * HMAX], F32))
            with semaphores(nc, "_p") as sem:
                prepare(nc, locals())
            with semaphores(nc, "_t0") as sem:
                first_rows(nc, locals())
            with semaphores(nc, "_e0") as sem:
                first_edges(nc, locals())
            with semaphores(nc, "_g0") as sem:
                general_edges(nc, locals(), 0)
            with semaphores(nc, "_t1") as sem:
                transform(nc, locals(), 1)
            with semaphores(nc, "_g1") as sem:
                general_edges(nc, locals(), 1)
        with semaphores(nc, "_m") as sem:
            edges_and_mixture(nc, locals())


@contextmanager
def semaphores(nc, suffix):
    with ExitStack() as held:
        named = []

        def sem(name):
            named.append(held.enter_context(nc.semaphore(name + suffix)))
            return named[-1]

        yield sem
        with nc.Block() as block:
            @block.sync
            def _(sp):
                for s in named:
                    sp.sem_clear(s)


def prepare(nc, g):
    P_, E, ET, EG, STEPS, SC, SG, NT, F, KC, HMAX, HEADS = (
        P, g["E"], g["ET"], g["EG"], g["STEPS"], g["SC"], g["SG"], g["NT"], g["F"], g["KC"], g["HMAX"], g["HEADS"])
    ps, ident, acc, bias_rows = g["ps"], g["ident"], g["acc"], g["bias_rows"]
    lane, part_iota, w_aug = g["lane"], g["part_iota"], g["w_aug"]
    TABLE = 2 * STEPS // BATCH
    ITERS = g["ITERS"]
    full = ET - (EG - 1) * P - 1
    tail = E - (ET - 1) * P
    pad_node = g["N"]
    assert NT * P > pad_node and full < P
    with ExitStack() as ctx:
        def sb(name, shape, dt=F32):
            return ctx.enter_context(nc.sbuf_tensor(name, shape, dt))

        sem = g["sem"]
        dst_i = sb("dst_i", [P, EG, P], I32)
        src_i = sb("src_i", [P, EG, P], I32)
        dst_f = sb("dst_f", [P, EG, P])
        src_f = sb("src_f", [P, EG, P])
        ends_i = sb("ends_i", [P, 2, EG], I32)
        ends = sb("ends", [P, 2, EG])
        tile_id = sb("tile_id", [P, EG])
        valid = sb("valid", [P, EG])
        count = sb("count", [P, EG])
        totals = sb("totals", [P, EG])
        before = sb("before", [P, EG])
        base = sb("base", [P, EG])
        limit = sb("limit", [P, EG])
        shift = sb("shift", [P, EG])
        shift128 = sb("shift128", [P, EG])
        node_off = sb("node_off", [P, EG])
        ones_g = sb("ones_g", [P, EG])
        below = sb("below", [P, STEPS])
        sel = sb("sel", [P, EG, STEPS])
        tri = sb("tri", [P, P])
        ones = sb("ones", [P, P])
        block_id = sb("block_id", [P, SG])
        places = sb("places", [P, SG, P], BF16)
        n_sum = sb("n_sum", [1, STEPS])
        n_used = sb("n_used", [1, STEPS])
        n_ends = sb("n_ends", [1, STEPS // BATCH, 2])
        n_ring = sb("n_ring", [1, TABLE], I32)
        next_i = sb("next_i", [P, EG, P], I32)
        next_f = sb("next_f", [P, EG, P])
        falls = sb("falls", [P, EG, P])
        faults_p = sb("faults_p", [P, 1])
        faults = sb("faults", [P, 1])
        other = sb("other", [1, STEPS])
        fault = sb("fault", [1, 4])
        marks = sb("marks", [1, ITERS])
        late = sb("late", [1, ITERS])
        n_all = sb("n_all", [1, TABLE], I32)
        step_iota = sb("step_iota", [P, STEPS])
        a_rows = sb("a_rows", [P, 4, F])
        prod = sb("prod", [P, F])

        s_zero, s_edges, s_w, s_a, s_const, s_pool = (
            sem("blank_tiles"), sem("edges_landed"), sem("weights_landed"), sem("attention_rows_landed"),
            sem("constants_ready"), sem("pool_chain"))
        s_falls = sem("falls_found")
        s_v, s_prefix, s_dve_mid, s_pe, s_places, s_bias = (
            sem("dve_chain"), sem("prefix_ready"), sem("dve_tables"), sem("pe_tables"), sem("places_stored"),
            sem("bias_landed"))
        block = ctx.enter_context(nc.Block())

        @block.sync
        def _(sp):
            sp.wait_ge(s_zero, 3)
            for dram, tile in ((g["dst"], dst_i), (g["src"], src_i)):
                whole = (EG - 1) * P * P
                sp.dma_start(tile[:, 0:EG - 1, :],
                             dram[0:whole].rearrange("(g q p) -> q g p", q=P, p=P)).then_inc(s_edges, 16)
                sp.dma_start(tile[0:full, EG - 1, :],
                             dram[whole:whole + full * P].rearrange("(q p) -> q p", p=P)).then_inc(s_edges, 16)
                sp.dma_start(tile[full:full + 1, EG - 1, 0:tail],
                             dram[whole + full * P:E].rearrange("(a p) -> a p", a=1)).then_inc(s_edges, 16)
            whole = (EG - 1) * P * P
            sp.dma_start(next_i[:, 0:EG - 1, :],
                         g["dst"][1:whole + 1].rearrange("(g q p) -> q g p", q=P, p=P)).then_inc(s_edges, 16)
            sp.dma_start(next_i[0:full, EG - 1, :],
                         g["dst"][whole + 1:whole + full * P + 1].rearrange("(q p) -> q p", p=P)).then_inc(s_edges, 16)
            sp.dma_start(next_i[full:full + 1, EG - 1, 0:tail - 1],
                         g["dst"][whole + full * P + 1:E].rearrange("(a p) -> a p", a=1)).then_inc(s_edges, 16)
            for l in (0, 1):
                sp.dma_start(w_aug[:, l, :, 0:F],
                             g["gnn"][l]["W"].rearrange("(k p) n -> p k n", p=P)).then_inc(s_w, 16)
                for n, name in enumerate(("a_src", "a_dst")):
                    sp.dma_start(a_rows[:, 2 * l + n, :],
                                 g["gnn"][l][name].rearrange("h c -> (h c)").partition_broadcast(P)
                                 ).then_inc(s_a, 16)
                sp.dma_start(bias_rows[:, l, :], g["gnn"][l]["b"].partition_broadcast(P)).then_inc(s_bias, 16)
            sp.wait_ge(s_bias, 32)
            sp.wait_ge(s_dve_mid, 4)
            rest = STEPS - (SG - 1) * P
            sp.dma_start(g["place_dram"][0:(SG - 1) * P, :].rearrange("(g q) p -> q g p", q=P),
                         places[:, 0:SG - 1, :]).then_inc(s_places, 16)
            sp.dma_start(g["place_dram"][(SG - 1) * P:STEPS, :], places[0:rest, SG - 1, :]).then_inc(s_places, 16)
            sp.wait_ge(s_places, 32)

        @block.gpsimd
        def _(pool):
            pool.memset(dst_i[:, EG - 1, :], pad_node).then_inc(s_zero, 1)
            pool.memset(src_i[:, EG - 1, :], 0).then_inc(s_zero, 1)
            pool.memset(next_i[:, EG - 1, :], pad_node).then_inc(s_zero, 1)
            pool.memset(ident[:, :], 0.0).then_inc(s_pool, 1)
            pool.memset(ones[:, :], 1.0).then_inc(s_pool, 1)
            pool.wait_ge(s_pool, 2)
            pool.affine_select(out=ident[:, :], in_=ident[:, :], compare_op=ALU.not_equal, fill=1.0, base=0,
                               pattern=[[-1, P]], channel_multiplier=1).then_inc(s_const, 1)
            pool.affine_select(out=tri[:, :], in_=ones[:, :], compare_op=ALU.is_gt, fill=0.0, base=0,
                               pattern=[[1, P]], channel_multiplier=-1).then_inc(s_const, 1)
            pool.iota(step_iota[:, :], [[1, STEPS]], base=0, channel_multiplier=0,
                      allow_small_or_imprecise_dtypes=True).then_inc(s_const, 1)
            pool.iota(part_iota[:, :], [[1, 1]], base=0, channel_multiplier=1,
                      allow_small_or_imprecise_dtypes=True).then_inc(s_const, 1)
            pool.iota(tile_id[:, :], [[P, EG]], base=0, channel_multiplier=1,
                      allow_small_or_imprecise_dtypes=True).then_inc(s_const, 1)
            pool.iota(block_id[:, :], [[P, SG]], base=0, channel_multiplier=1,
                      allow_small_or_imprecise_dtypes=True).then_inc(s_const, 1)
            pool.wait_ge(s_falls, 1)
            nc.gpsimd.partition_all_reduce(faults[:, :], faults_p[:, :], P, bass.bass_isa.ReduceOp.max
                                           ).then_inc(s_falls, 1)

        @block.vector
        def _(dve):
            done = [0]

            def then(ins):
                done[0] += 1
                ins.then_inc(s_v, 1)
                dve.wait_ge(s_v, done[0])

            H0 = HEADS[0]
            then(nc.vector.memset(acc[:, :, 0:F + H0].rearrange("p n (h c) -> p n h c", h=H0)[:, :, :, F // H0:], 1.0))
            then(nc.vector.memset(ones_g[:, :], 1.0))
            dve.wait_ge(s_edges, 144)
            dve.wait_ge(s_const, 6)
            then(nc.vector.tensor_copy(dst_f[:, :, :], dst_i[:, :, :]))
            nc.vector.tensor_copy(src_f[:, :, :], src_i[:, :, :])
            shift_bits = int(np.log2(P))
            nc.vector.tensor_scalar(ends_i[:, 0, :], dst_i[:, :, 0], shift_bits, None, ALU.logical_shift_right)
            then(nc.vector.tensor_scalar(ends_i[:, 1, :], dst_i[:, :, P - 1], shift_bits, None,
                                         ALU.logical_shift_right))
            then(nc.vector.tensor_copy(ends[:, :, :], ends_i[:, :, :]))
            then(nc.vector.tensor_scalar(valid[:, :], tile_id[:, :], float(ET), None, ALU.is_lt))
            then(nc.vector.tensor_tensor(count[:, :], ends[:, 1, :], ends[:, 0, :], ALU.subtract))
            nc.vector.scalar_tensor_tensor(count[:, :], count[:, :], 1.0, valid[:, :], ALU.add, ALU.mult
                                           ).then_inc(s_dve_mid, 1)
            dve.wait_ge(s_dve_mid, 1)
            dve.wait_ge(s_prefix, 1)
            then(nc.vector.tensor_copy(totals[:, :], ps[:, 1, 0:EG]))
            then(nc.vector.tensor_tensor_scan(before[:, :], ones_g[:, :], totals[:, :], 0.0, ALU.mult, ALU.add))
            then(nc.vector.tensor_tensor(before[:, :], before[:, :], totals[:, :], ALU.subtract))
            then(nc.vector.tensor_tensor(base[:, :], ps[:, 0, 0:EG], before[:, :], ALU.add))
            then(nc.vector.tensor_tensor(limit[:, :], base[:, :], count[:, :], ALU.add))
            then(nc.vector.tensor_tensor(shift[:, :], ends[:, 0, :], base[:, :], ALU.subtract))
            then(nc.vector.tensor_scalar(shift128[:, :], shift[:, :], float(P), None, ALU.mult))
            then(nc.vector.tensor_scalar(node_off[:, :], shift[:, :], float(NT - 1), None, ALU.subtract))
            for e in range(EG):
                then(nc.vector.tensor_scalar(dst_f[:, e, :], dst_f[:, e, :], shift128[:, e:e + 1], None,
                                             ALU.subtract))
                then(nc.vector.tensor_scalar(below[:, :], step_iota[:, :], base[:, e:e + 1], None, ALU.is_ge))
                then(nc.vector.scalar_tensor_tensor(sel[:, e, :], step_iota[:, :], limit[:, e:e + 1],
                                                    below[:, :], ALU.is_lt, ALU.mult))
            dve.sem_inc(s_dve_mid, 1)
            then(nc.vector.tensor_copy(next_f[:, :, :], next_i[:, :, :]))
            then(nc.vector.tensor_copy(falls[:, :, :], dst_i[:, :, :]))
            then(nc.vector.tensor_tensor(falls[:, :, :], falls[:, :, :], next_f[:, :, :], ALU.is_gt))
            nc.vector.tensor_reduce(faults_p[:, :], falls[:, :, :].rearrange("p a b -> p (a b)"), AX.X, ALU.max
                                    ).then_inc(s_falls, 1)
            dve.wait_ge(s_w, 32)
            dve.wait_ge(s_a, 64)
            for l, H in enumerate(HEADS):
                for k in range(KC):
                    for n in (0, 1):
                        then(nc.vector.tensor_tensor(prod[:, :], w_aug[:, l, k, 0:F], a_rows[:, 2 * l + n, :],
                                                     ALU.mult))
                        then(nc.vector.tensor_reduce(w_aug[:, l, k, F + n * H:F + (n + 1) * H],
                                                     prod[:, :].rearrange("p (h c) -> p h c", h=H), AX.X, ALU.add))
            dve.wait_ge(s_pe, 1)
            for c in (0, 1):
                cols = slice(c * SC, (c + 1) * SC)
                nc.vector.tensor_copy(g["edge_src"][:, cols], ps[:, c, 0:SC])
                nc.vector.scalar_tensor_tensor(g["edge_place"][:, cols], step_iota[:, cols], -float(P),
                                               ps[:, 2 + c, 0:SC], ALU.mult, ALU.add)
                nc.vector.tensor_copy(n_sum[:, cols], ps[0:1, 4 + c, 0:SC])
                then(nc.vector.tensor_copy(n_used[:, cols], ps[0:1, 6 + c, 0:SC]))
            then(nc.vector.tensor_tensor(n_used[:, :], n_used[:, :], step_iota[0:1, :], ALU.mult))
            then(nc.vector.tensor_tensor(n_sum[:, :], n_sum[:, :], n_used[:, :], ALU.add))
            then(nc.vector.tensor_scalar(n_sum[:, :], n_sum[:, :], float(NT - 1), None, ALU.add))
            by_batch = n_sum[:, :].rearrange("a (b s) -> a b s", s=BATCH)
            nc.vector.tensor_copy(g["step_node"][:, :], n_sum[:, :])
            nc.vector.tensor_copy(lane[:, :], step_iota[:, 0:P])
            nc.vector.tensor_copy(n_ends[:, :, 0:1], by_batch[:, :, 0:1])
            then(nc.vector.tensor_copy(n_ends[:, :, 1:2], by_batch[:, :, BATCH - 1:BATCH]))
            then(nc.vector.tensor_copy(n_all[:, :], n_ends[:, :, :].rearrange("a b e -> a (b e)")))
            then(nc.vector.tensor_scalar(n_ring[:, :], n_all[:, :], SUM_TILES - 1, None, ALU.bitwise_and))
            then(nc.vector.tensor_tensor(n_used[:, :].rearrange("a (b s) -> a b s", s=BATCH), by_batch,
                                         n_ends[:, :, 0:1].to_broadcast([1, STEPS // BATCH, BATCH]), ALU.not_equal))
            nc.vector.tensor_copy(g["batch_nodes"]["all"][:, :], n_all[:, :])
            nc.vector.tensor_copy(g["batch_nodes"]["ring"][:, :], n_ring[:, :])
            then(nc.vector.tensor_copy(g["step_bank"][:, :], n_used[:, :]))
            then(nc.vector.tensor_tensor(other[:, :].rearrange("a (b s) -> a b s", s=BATCH), by_batch,
                                         n_ends[:, :, 1:2].to_broadcast([1, STEPS // BATCH, BATCH]), ALU.not_equal))
            then(nc.vector.tensor_tensor(other[:, :], other[:, :], n_used[:, :], ALU.mult))
            then(nc.vector.tensor_reduce(fault[:, 0:1], other[:, :], AX.X, ALU.max))
            by_iter = n_sum[:, :].rearrange("a (i s) -> a i s", s=BODY)
            then(nc.vector.tensor_scalar(marks[:, :], step_iota[0:1, 0:ITERS], float(GT), None, ALU.mult))
            then(nc.vector.tensor_tensor(late[:, 1:ITERS], by_iter[:, 1:ITERS, 0], marks[:, 1:ITERS], ALU.is_lt))
            then(nc.vector.tensor_reduce(fault[:, 1:2], late[:, 1:ITERS], AX.X, ALU.max))
            then(nc.vector.tensor_scalar(marks[:, :], marks[:, :], float(SUM_TILES - GT), None, ALU.add))
            then(nc.vector.tensor_tensor(late[:, :], by_iter[:, :, BODY - 1], marks[:, :], ALU.is_ge))
            then(nc.vector.tensor_reduce(fault[:, 2:3], late[:, :], AX.X, ALU.max))
            dve.wait_ge(s_falls, 2)
            then(nc.vector.tensor_copy(fault[:, 3:4], faults[0:1, :]))
            then(nc.vector.tensor_reduce(g["disorder"][:, :], fault[:, :], AX.X, ALU.max))
            then(nc.vector.tensor_scalar(block_id[:, :], block_id[:, :], float(P), None, ALU.mult))
            dve.sem_inc(s_dve_mid, 1)
            dve.wait_ge(s_pe, 2)
            for q in range(SG):
                rows = min(P, STEPS - q * P)
                last = nc.vector.tensor_scalar(places[0:rows, q, :], ps[0:rows, q // 4, (q % 4) * P:(q % 4 + 1) * P],
                                               block_id[0:rows, q:q + 1], None, ALU.subtract)
            last.then_inc(s_dve_mid, 1)

        @block.tensor
        def _(pe):
            pe.wait_ge(s_const, 6)
            pe.wait_ge(s_dve_mid, 1)
            nc.tensor.matmul(ps[:, 0, 0:EG], tri[:, :], count[:, :], start=True, stop=True)
            nc.tensor.matmul(ps[:, 1, 0:EG], ones[:, :], count[:, :], start=True, stop=True).then_inc(s_prefix, 1)
            pe.wait_ge(s_dve_mid, 2)
            for c in (0, 1):
                for e in range(EG):
                    first, last = e == 0, e == EG - 1
                    pick = sel[:, e, c * SC:(c + 1) * SC]
                    nc.tensor.matmul(ps[:, c, 0:SC], src_f[:, e, :], pick, start=first, stop=last)
                    nc.tensor.matmul(ps[:, 2 + c, 0:SC], dst_f[:, e, :], pick, start=first, stop=last)
                    nc.tensor.matmul(ps[0:1, 4 + c, 0:SC], node_off[:, e:e + 1], pick, start=first, stop=last)
                    mm = nc.tensor.matmul(ps[0:1, 6 + c, 0:SC], ones_g[:, 0:1], pick, start=first, stop=last)
            mm.then_inc(s_pe, 1)
            pe.wait_ge(s_dve_mid, 3)
            for q in range(SG):
                rows = min(P, STEPS - q * P)
                for e in range(EG):
                    mm = nc.tensor.matmul(ps[0:rows, q // 4, (q % 4) * P:(q % 4 + 1) * P],
                                          sel[:, e, q * P:q * P + rows], dst_f[:, e, :],
                                          start=e == 0, stop=e == EG - 1)
            mm.then_inc(s_pe, 1)


def choose_path(nc, g, layer, sb, sem):
    H, NT, scores, top = g["HEADS"][layer], g["NT"], g["scores"], g["top"]
    top_p = sb("top_p", [P, 2 * H])
    spread = sb("spread", [1, H])
    widest = sb("widest", [1, 1])
    neg_scores = sb("neg_scores", [P, NT, H])
    s_top, s_chain = sem("top"), sem("choice_chain")

    def on_gpsimd(pool):
        pool.wait_ge(s_top, 1)
        nc.gpsimd.partition_all_reduce(top[:, layer, 0:2 * H], top_p[:, :], P, bass.bass_isa.ReduceOp.max
                                       ).then_inc(s_top, 1)

    def on_vector(dve):
        done = [0]

        def then(ins):
            done[0] += 1
            ins.then_inc(s_chain, 1)
            dve.wait_ge(s_chain, done[0])

        then(nc.vector.tensor_scalar(neg_scores[:, :, :], scores[:, :, 0:H], -1.0, None, ALU.mult))
        then(nc.vector.tensor_reduce(top_p[:, 0:H], scores[:, :, 0:H].rearrange("p n h -> p h n"), AX.X, ALU.max))
        nc.vector.tensor_reduce(top_p[:, H:2 * H], neg_scores[:, :, :].rearrange("p n h -> p h n"), AX.X, ALU.max
                                ).then_inc(s_top, 1)
        dve.wait_ge(s_top, 2)
        then(nc.vector.tensor_tensor(spread[:, :], top[0:1, layer, 0:H], top[0:1, layer, H:2 * H], ALU.add))
        then(nc.vector.tensor_scalar(spread[:, :], spread[:, :], MAX_SPREAD, None, ALU.is_gt))
        then(nc.vector.tensor_reduce(widest[:, :], spread[:, :], AX.X, ALU.max))
        then(nc.vector.tensor_tensor(widest[:, :], widest[:, :], g["disorder"][:, :], ALU.max))
        then(nc.vector.tensor_copy(g["by_list"][0:1, layer:layer + 1], widest[:, :]))

    return on_gpsimd, on_vector


def first_rows(nc, g):
    N, F, NT, LAST, KC = (g[k] for k in ("N", "F", "NT", "LAST", "KC"))
    H = g["HEADS"][0]
    C = F // H
    ps, ident, acc, w_aug, scores, x, sem = (g[k] for k in ("ps", "ident", "acc", "w_aug", "scores", "x", "sem"))
    SLOTS = 4
    LAG = {"load": 0, "stats": 2, "norm": 3, "product": 4, "row": 5, "store": 6}
    AHEAD = 2
    ROUNDS = NT // SLOTS
    assert AHEAD * SLOTS >= LAG["store"] and ROUNDS > AHEAD
    with ExitStack() as ctx:
        def sb(name, shape, dt=F32):
            return ctx.enter_context(nc.sbuf_tensor(f"{name}_f", shape, dt))

        inp = sb("inp", [P, SLOTS, F])
        xn = sb("xn", [P, 2, F])
        stats = sb("stats", [P, 2, 6])
        mv = sb("mv", [P, 2, 2])
        rstd = sb("rstd", [P, 2, 1])
        eps = sb("eps", [P, 1])
        xT = sb("xT", [P, 2, KC, P])
        choose_pool, choose_vector = choose_path(nc, g, 0, sb, sem)

        s_in = [sem(f"x_landed{n}_") for n in range(SLOTS)]
        s_eps, s_turn = sem("eps_set"), sem("turn")
        s_st, s_var, s_sq, s_rs = sem("stats_ready"), sem("variance_ready"), sem("deviation_ready"), sem("inverse_ready")
        s_xn, s_tr, s_xT, s_mm, s_row = (
            sem("norm_ready"), sem("transposed"), sem("columns_ready"), sem("product_ready"), sem("row_ready"))
        s_sp_turn, s_stored = sem("store_turn"), sem("row_stored")
        block = ctx.enter_context(nc.Block())

        def turns(eng, stages):
            def round_(i):
                for t in range(SLOTS):
                    for name, f in stages:
                        q = t - LAG[name]
                        if isinstance(i, int) and not 0 <= i * SLOTS + q < NT:
                            continue
                        f(i * SLOTS + q, q % SLOTS, i + q // SLOTS)

            for i in range(AHEAD):
                round_(i)
            with eng.Fori(AHEAD, ROUNDS) as i:
                round_(i)
            for i in range(ROUNDS, ROUNDS + AHEAD + 1):
                round_(i)

        @block.sync
        def _(sp):
            def load(n, slot, r):
                sp.wait_ge(s_xn, n + 1)
                sp.sem_inc(s_sp_turn, 1)
                if isinstance(n, int) and n == NT - 1:
                    sp.dma_start(inp[0:LAST, slot, :], x[(NT - 1) * P:N, :]).then_inc(s_in[slot], 16)
                else:
                    sp.dma_start(inp[:, slot, :], x[bass.ds(n * P, P), :]).then_inc(s_in[slot], 16)

            def store(n, slot, r):
                sp.wait_ge(s_row, n + 1 + 2)
                sp.sem_inc(s_sp_turn, 1)
                sp.dma_start(g["rows_dram"][0][bass.ds(n * P, P), :], acc[:, bass.ds(n, 1), 0:F + 2 * H]
                             .rearrange("p a c -> p (a c)")).then_inc(s_stored, 16)

            turns(sp, (("load", load), ("store", store)))
            sp.wait_ge(s_stored, 16 * NT)

        @block.gpsimd
        def _(pool):
            choose_pool(pool)

        @block.scalar
        def _(act):
            act.wait_ge(s_eps, 1)

            def deviation(n, slot, r):
                act.wait_ge(s_var, n + 1)
                nc.scalar.activation(rstd[:, slot % 2, :], mv[:, slot % 2, 1:2], ACT.Sqrt, bias=eps[:, 0:1]
                                     ).then_inc(s_sq, 1)

            def row(n, slot, r):
                act.wait_ge(s_mm, n + 1 + 2)
                bank = 2 + slot % 2
                heads = acc[:, bass.ds(n, 1), 0:F + H].rearrange("p a (h c) -> p (a h) c", h=H)
                nc.scalar.activation(heads[:, :, 0:C], ps[:, bank, 0:F].rearrange("p (h c) -> p h c", h=H), ACT.Copy)
                nc.scalar.activation(acc[:, bass.ds(n, 1), F + H:F + 2 * H], ps[:, bank, F:F + H].unsqueeze(1),
                                     ACT.Copy)
                nc.scalar.activation(scores[:, bass.ds(n, 1), 0:2 * H], ps[:, bank, F:F + 2 * H].unsqueeze(1),
                                     ACT.Copy).then_inc(s_row, 1)

            turns(act, (("row", row), ("stats", deviation)))

        @block.vector
        def _(dve):
            nc.vector.memset(eps[:, :], LN_EPS).then_inc(s_eps, 1)
            dve.sem_inc(s_xn, SLOTS)
            dve.sem_inc(s_tr, 2)
            dve.sem_inc(s_mm, 2)
            dve.sem_inc(s_row, 2)

            def columns(n, slot, r):
                dve.wait_ge(s_tr, n + 1 + 2)
                dve.wait_ge(s_mm, n + 1)
                nc.vector.tensor_copy(xT[:, slot % 2, :, :],
                                      ps[:, slot % 2, 0:KC * P].rearrange("p (k q) -> p k q", k=KC)).then_inc(s_xT, 1)

            def norm(n, slot, r):
                dve.wait_ge(s_sq, n + 1)
                nc.vector.reciprocal(rstd[:, slot % 2, :], rstd[:, slot % 2, :]).then_inc(s_rs, 1)
                dve.wait_ge(s_rs, n + 1)
                dve.wait_ge(s_tr, n + 1)
                nc.vector.tensor_scalar(xn[:, slot % 2, :], inp[:, slot, :], mv[:, slot % 2, 0:1],
                                        rstd[:, slot % 2, :], ALU.subtract, ALU.mult).then_inc(s_xn, 1)

            def variance(n, slot, r):
                dve.wait_ge(s_in[slot], r * 16 + 16)
                dve.sem_inc(s_turn, 1)
                nc.vector.bn_stats(stats[:, slot % 2, :], inp[:, slot, :]).then_inc(s_st, 1)
                dve.wait_ge(s_st, n + 1)
                dve.sem_inc(s_turn, 1)
                nc.vector.bn_aggr(mv[:, slot % 2, :], stats[:, slot % 2, :]).then_inc(s_var, 1)

            turns(dve, (("product", columns), ("norm", norm), ("stats", variance)))
            dve.wait_ge(s_row, NT + 2)
            choose_vector(dve)

        @block.tensor
        def _(pe):
            def product(n, slot, r):
                pe.wait_ge(s_xT, n + 1)
                pe.wait_ge(s_row, n + 1)
                for k in range(KC):
                    mm = nc.tensor.matmul(ps[:, 2 + slot % 2, 0:F + 2 * H], xT[:, slot % 2, k, :],
                                          w_aug[:, 0, k, 0:F + 2 * H], start=k == 0, stop=k == KC - 1)
                mm.then_inc(s_mm, 1)

            def transposes(n, slot, r):
                pe.wait_ge(s_xn, n + 1 + SLOTS)
                for k in range(KC):
                    mm = nc.tensor.transpose(ps[:, slot % 2, k * P:(k + 1) * P], xn[:, slot % 2, k * P:(k + 1) * P],
                                             ident[:, :])
                mm.then_inc(s_tr, 1)

            turns(pe, (("norm", transposes), ("product", product)))


def transform(nc, g, layer):
    N, F, NT, LAST, KC, ROW, TB, HMAX = (g[k] for k in ("N", "F", "NT", "LAST", "KC", "ROW", "TB", "HMAX"))
    H = g["HEADS"][layer]
    C = F // H
    ps, ident, acc, bias_rows, w_aug, scores = (g[k] for k in ("ps", "ident", "acc", "bias_rows", "w_aug", "scores"))
    x, rows_dram, top = g["x"], g["rows_dram"][layer], g["top"]
    with ExitStack() as ctx:
        def sb(name, shape, dt=F32):
            return ctx.enter_context(nc.sbuf_tensor(f"{name}{layer}", shape, dt))

        sem = g["sem"]
        inp = sb("t_in", [P, TB, F])
        xn = sb("t_norm", [P, TB, F])
        neg = sb("t_neg", [P, TB, F])
        pos = sb("t_pos", [P, TB, F])
        stats = sb("t_stats", [P, TB, 6])
        mv = sb("t_mv", [P, TB, 2])
        rstd = sb("t_rstd", [P, TB, 1])
        eps = sb("t_eps", [P, 1])
        ones_col = sb("t_ones", [P, 1])
        xT = sb("t_xT", [P, 2, KC, P])
        zinv = sb("t_zinv", [P, TB, HMAX])

        s_in = [sem(f"t_landed{j}_") for j in range(TB)]
        s_eps = sem("t_eps_set")
        s_turn = sem("t_turn")
        s_var = sem("t_var_ready")
        s_std = sem("t_std_ready")
        s_c = sem("t_dve_chain")
        s_act = sem("t_act_done")
        s_pool = sem("t_pool_done")
        s_xn = sem("t_norm_ready")
        s_tr = sem("t_transposed")
        s_xT = sem("t_xT_ready")
        s_mm = sem("t_product_ready")
        s_row = sem("t_row_copied")
        s_sco = sem("t_scores_copied")
        s_asco = sem("t_row_scores")
        s_store = g["stored"][layer]
        choose_pool, choose_vector = choose_path(nc, g, layer, sb, sem)
        block = ctx.enter_context(nc.Block())
        R = NT // TB
        tail_rows = LAST

        @block.sync
        def _(sp):
            def program():
                if layer == 0:
                    def load(i, last=False):
                        for j in range(TB):
                            sp.wait_ge(s_xn, i * TB + j + 1)
                            if last and j == TB - 1:
                                sp.dma_start(inp[0:tail_rows, j, :], x[(NT - 1) * P:N, :]).then_inc(s_in[j], 16)
                            else:
                                sp.dma_start(inp[:, j, :], x[bass.ds((i * TB + j) * P, P), :]).then_inc(s_in[j], 16)

                    with sp.Fori(0, R - 1) as i:
                        load(i)
                    load(R - 1, last=True)

            if layer == 0:
                program()
            else:
                with sp.If(listed(nc, sp, g, 0) == 1):
                    program()

        @block.gpsimd
        def _(pool):
            def program():
                def store(i):
                    pool.wait_ge(s_row, (i + 1) * TB)
                    pool.wait_ge(s_sco, (i + 1) * TB)
                    nc.gpsimd.tensor_copy(acc[:, bass.ds(i * TB, TB), F + H:F + 2 * H],
                                          scores[:, bass.ds(i * TB, TB), 0:H]).then_inc(s_asco, 1)
                    pool.wait_ge(s_asco, i + 1)
                    pool.dma_start(rows_dram.rearrange("(n p) c -> p n c", p=P)[:, bass.ds(i * TB, TB), :],
                                   acc[:, bass.ds(i * TB, TB), 0:F + 2 * H]).then_inc(s_store, 16)

                with pool.Fori(0, R) as i:
                    if layer == 1:
                        pool.wait_ge(s_c, i * 3 + 2)
                        nc.gpsimd.tensor_tensor(pos[:, :, :], inp[:, :, :],
                                                bias_rows[:, 0, :].unsqueeze(1).to_broadcast([P, TB, F]),
                                                ALU.add).then_inc(s_pool, 1)
                    store(i)
                choose_pool(pool)
                pool.wait_ge(s_store, 16 * R)

            if layer == 0:
                program()
            else:
                with pool.If(listed(nc, pool, g, 0) == 1):
                    program()

        @block.scalar
        def _(act):
            def program():
                with act.Fori(0, R) as i:
                    if layer == 0:
                        act.wait_ge(s_eps, 1)
                        act.wait_ge(s_var, i + 1)
                        nc.scalar.activation(rstd[:, :, :], mv[:, :, 1:2], ACT.Sqrt, bias=eps[:, 0:1]).then_inc(s_std, 1)
                    else:
                        act.wait_ge(s_c, i * 3 + 3)
                        nc.scalar.activation(neg[:, :, :], neg[:, :, :], ACT.Exp).then_inc(s_act, 1)
                    for j in range(TB):
                        act.wait_ge(s_mm, i * TB + j + 1)
                        nc.scalar.activation(
                            acc[:, bass.ds(i * TB + j, 1), 0:F + H].rearrange("p a (h c) -> p (a h) c", h=H)[:, :, 0:C],
                            ps[:, 2 + j % 2, 0:F].rearrange("p (h c) -> p h c", h=H), ACT.Copy).then_inc(s_row, 1)

            if layer == 0:
                program()
            else:
                with act.If(listed(nc, act, g, 0) == 1):
                    program()

        @block.vector
        def _(dve):
            def program():
                if layer == 0:
                    nc.vector.memset(eps[:, :], LN_EPS).then_inc(s_eps, 1)
                else:
                    nc.vector.memset(ones_col[:, :], 1.0).then_inc(s_eps, 1)
                    dve.wait_ge(s_eps, 1)

                dve.sem_inc(s_xn, TB)

                def tile_products(i, j):
                    n = i * TB + j
                    dve.wait_ge(s_tr, n + 1)
                    nc.vector.tensor_copy(xT[:, j % 2, :, :],
                                          ps[:, j % 2, 0:KC * P].rearrange("p (k q) -> p k q", k=KC)).then_inc(s_xT, 1)
                    dve.wait_ge(s_mm, n + 1)
                    nc.vector.tensor_copy(scores[:, bass.ds(n, 1), 0:2 * H],
                                          ps[:, 4 + j % 2, 0:2 * H].unsqueeze(1)).then_inc(s_sco, 1)

                def body(i, last=False):
                    if layer == 0:
                        for j in range(TB):
                            dve.wait_ge(s_in[j], i * 16 + 16)
                            dve.sem_inc(s_turn, 1)
                            nc.vector.bn_stats(stats[:, j, :], inp[:, j, :]).then_inc(s_c, 1)
                        for j in range(TB):
                            dve.wait_ge(s_c, i * (TB + 1) + j + 1)
                            dve.sem_inc(s_turn, 1)
                            ins = nc.vector.bn_aggr(mv[:, j, :], stats[:, j, :])
                        ins.then_inc(s_var, 1)
                        dve.wait_ge(s_std, i + 1)
                        nc.vector.reciprocal(rstd[:, :, :], rstd[:, :, :]).then_inc(s_c, 1)
                        dve.wait_ge(s_c, (i + 1) * (TB + 1))
                        for j in range(TB):
                            nc.vector.tensor_scalar(xn[:, j, :], inp[:, j, :], mv[:, j, 0:1], rstd[:, j, :],
                                                    ALU.subtract, ALU.mult).then_inc(s_xn, 1)
                    else:
                        H0 = g["HEADS"][0]
                        C0 = F // H0
                        sums = acc[:, bass.ds(i * TB, TB), 0:F + H0].rearrange("p n (h c) -> p n h c", h=H0)
                        nc.vector.reciprocal(zinv[:, :, 0:H0], sums[:, :, :, C0]).then_inc(s_c, 1)
                        dve.wait_ge(s_c, i * 3 + 1)
                        for j in range(TB):
                            one = acc[:, bass.ds(i * TB + j, 1), 0:F + H0].rearrange("p a (h c) -> p (a h) c", h=H0)
                            ins = nc.vector.tensor_tensor(
                                inp[:, j, :].rearrange("p (h c) -> p h c", h=H0), one[:, :, 0:C0],
                                zinv[:, j, 0:H0].unsqueeze(2).to_broadcast([P, H0, C0]), ALU.mult)
                        ins.then_inc(s_c, 1)
                        dve.wait_ge(s_pool, i + 1)
                        nc.vector.tensor_scalar(neg[:, :, :], pos[:, :, :], 0.0, None, ALU.min).then_inc(s_c, 1)
                        dve.wait_ge(s_act, i + 1)
                        nc.vector.tensor_scalar(pos[:, :, :], pos[:, :, :], 0.0, -1.0, ALU.max, ALU.add
                                                ).then_inc(s_std, 1)
                        dve.wait_ge(s_std, i + 1)
                        nc.vector.tensor_copy(acc[:, bass.ds(i * TB, TB), F:F + 1],
                                              ones_col[:, :].unsqueeze(1).to_broadcast([P, TB, 1]))
                        for j in range(TB):
                            nc.vector.tensor_tensor(xn[:, j, :], neg[:, j, :], pos[:, j, :], ALU.add).then_inc(s_xn, 1)
                    for j in range(TB):
                        tile_products(i, j)

                if layer == 0:
                    with dve.Fori(0, R - 1) as i:
                        body(i)
                    body(R - 1, last=True)
                else:
                    with dve.Fori(0, R) as i:
                        body(i)
                dve.wait_ge(s_sco, NT)
                choose_vector(dve)

            if layer == 0:
                program()
            else:
                with dve.If(listed(nc, dve, g, 0) == 1):
                    program()

        @block.tensor
        def _(pe):
            def program():
                def transposes(i, j):
                    pe.wait_ge(s_xn, TB + i * TB + j + 1)
                    for k in range(KC):
                        mm = nc.tensor.transpose(ps[:, j % 2, k * P:(k + 1) * P], xn[:, j, k * P:(k + 1) * P], ident[:, :])
                    mm.then_inc(s_tr, 1)

                def product(i, j):
                    pe.wait_ge(s_xT, i * TB + j + 1)
                    for k in range(KC):
                        nc.tensor.matmul(ps[:, 2 + j % 2, 0:F], xT[:, j % 2, k, :],
                                         w_aug[:, layer, k, 0:F], start=k == 0, stop=k == KC - 1)
                    for k in range(KC):
                        mm = nc.tensor.matmul(ps[:, 4 + j % 2, 0:2 * H], xT[:, j % 2, k, :],
                                              w_aug[:, layer, k, F:F + 2 * H], start=k == 0, stop=k == KC - 1)
                    mm.then_inc(s_mm, 1)

                with pe.Fori(0, R) as i:
                    for j in range(TB):
                        if j >= 2:
                            pe.wait_ge(s_row, i * TB + j - 1)
                        transposes(i, j)
                        product(i, j)

            if layer == 0:
                program()
            else:
                with pe.If(listed(nc, pe, g, 0) == 1):
                    program()


def guards(nc, g, layer, sb, sem):
    NT, HMAX = g["NT"], g["HMAX"]
    H = g["HEADS"][layer]
    M = 2 * H
    scores = g["scores"]
    table = sb("node_table", [P, NT, M * PARTS], BF16)
    node_dm = sb("node_dm", [P, NT, M])
    rest1 = sb("rest1", [P, NT, M])
    rest2 = node_dm
    self_w = sb("self_w", [P, NT, H])
    self_e = sb("self_e", [P, NT, H])
    top = g["top"]
    s_c, s_self, s_selfw, s_table = (
        sem("scalar_chain"), sem("self_scores"), sem("self_weights"),
        sem("table_ready"))

    def on_scalar(act):
        act.wait_ge(s_self, 1)
        nc.scalar.activation(self_w[:, :, :], self_e[:, :, :], ACT.Exp).then_inc(s_selfw, 1)

    def on_vector(dve):
        done = [0]

        def then(ins):
            done[0] += 1
            ins.then_inc(s_c, 1)
            dve.wait_ge(s_c, done[0])

        then(nc.vector.tensor_tensor(rest1[:, :, 0:H], scores[:, :, H:M],
                                     top[:, layer, 0:H].unsqueeze(1).to_broadcast([P, NT, H]), ALU.add))
        nc.vector.tensor_copy(node_dm[:, :, 0:H], scores[:, :, H:M])
        then(nc.vector.scalar_tensor_tensor(node_dm[:, :, H:M], rest1[:, :, 0:H], SLOPE, rest1[:, :, 0:H],
                                            ALU.mult, ALU.max))
        then(nc.vector.tensor_tensor(self_e[:, :, :], scores[:, :, 0:H], scores[:, :, H:M], ALU.add))
        then(nc.vector.scalar_tensor_tensor(self_e[:, :, :], self_e[:, :, :], SLOPE, self_e[:, :, :],
                                            ALU.mult, ALU.max))
        nc.vector.tensor_tensor(self_e[:, :, :], self_e[:, :, :], node_dm[:, :, H:M], ALU.subtract
                                ).then_inc(s_self, 1)
        parts = table[:, :, :].rearrange("p n (m q) -> p n m q", q=PARTS)
        then(nc.vector.tensor_copy(parts[:, :, :, 0], node_dm[:, :, :]))
        then(nc.vector.tensor_tensor(rest1[:, :, :], node_dm[:, :, :], parts[:, :, :, 0], ALU.subtract))
        then(nc.vector.tensor_copy(parts[:, :, :, 1], rest1[:, :, :]))
        then(nc.vector.tensor_tensor(rest2[:, :, :], rest1[:, :, :], parts[:, :, :, 1], ALU.subtract))
        nc.vector.tensor_copy(parts[:, :, :, 2], rest2[:, :, :]).then_inc(s_table, 1)
        dve.wait_ge(s_selfw, 1)

    return table, self_w, s_table, on_scalar, on_vector


def edge_parts(nc, g, layer, sb, sem, table, s_table, sums, ring_slots, node_of):
    F, NT, ITERS = g["F"], g["NT"], g["ITERS"]
    H = g["HEADS"][layer]
    W = F + H
    ROW = F + 2 * H
    M = 2 * H
    NB = BODY // BATCH
    RU = ring_slots // UNIT
    NU = BODY // UNIT
    BU = BATCH // UNIT
    GROUP = BODY // 2
    GB = GROUP // BATCH
    assert NU % RU == 0
    ps = g["ps"]
    edge_src, edge_place, step_node, step_bank = g["edge_src"], g["edge_place"], g["step_node"], g["step_bank"]
    batch_nodes = g["batch_nodes"][node_of]
    rows_dram = g["rows_dram"][layer]
    LASTB = ITERS * NB - 1

    ring = sb("gathered_rows", [P, ring_slots, ROW])
    idx = sb("gather_index", [P, 2, GROUP], I32)
    onehot_t = sb("onehot_t", [P, 2, BATCH * P], BF16)
    onehot = sb("onehot", [P, 2, BATCH, P])
    place_now = sb("place_now", [P, 2, BATCH])
    adm = sb("adm", [P, 2, BATCH, M])
    e_sum = sb("e_sum", [P, 2, BATCH, H])
    e_leaky = sb("e_leaky", [P, 2, BATCH, H])
    e_less = sb("e_less", [P, 2, BATCH, H])
    weight = sb("weight", [P, 2, BATCH, H])
    zero_w = sb("zero_w", [P, P], BF16)
    zero_r = sb("zero_r", [P, W + W % 2], BF16)

    s_prow = [sem(f"place_rows_landed{n}_") for n in (0, 1)]
    s_idx = sem("index_ready")
    s_turn = sem("gather_turn")
    s_sp_turn = sem("load_turn")
    s_gath = g["gathered"][layer]
    s_oht = sem("onehot_t_ready")
    s_admp = sem("adm_product_ready")
    s_adm = sem("adm_summed")
    s_e = sem("score_chain")
    s_scores = sem("scores_ready")
    s_w = sem("weights_ready")
    s_oh = sem("onehot_ready")
    s_wt = sem("weighted")
    s_prod = sem("products_ready")
    s_add = sem("sums_added")
    s_rows_free = sem("place_rows_free")
    s_zero = sem("zeros_set")

    def slots_of(unit):
        return ring[:, unit % RU * UNIT:(unit % RU + 1) * UNIT, :]

    class Parts:
        sums_added = s_add


        @staticmethod
        def sync_batch(sp, i, jb):
            b = i * NB + jb
            sp.wait_ge(s_rows_free, b + 1)
            sp.sem_inc(s_sp_turn, 1)
            rows = g["place_dram"][bass.ds(b * BATCH, BATCH), :].rearrange("s p -> (s p)")
            sp.dma_start(onehot_t[:, jb % 2, :], rows.partition_broadcast(P)).then_inc(s_prow[jb % 2], 16)

        @staticmethod
        def gpsimd_batch(pool, i, jb):
            b = i * NB + jb
            if jb % GB == 0:
                pool.wait_ge(s_idx, i * (NB // GB) + jb // GB + 1)
            for j in range(BATCH):
                step = jb * BATCH + j
                if j % UNIT == 0:
                    pool.wait_ge(s_prod, i * NU + step // UNIT + 1)
                    pool.sem_inc(s_turn, 1)
                nc.gpsimd.indirect_dma_start(
                    ring[:, step % ring_slots, :], None, rows_dram,
                    bass.IndirectOffsetOnAxis(idx[:, step // GROUP % 2, step % GROUP:step % GROUP + 1], 0)
                ).then_inc(s_gath[step // UNIT % RU], 16)

        @staticmethod
        def scalar_start(act):
            nc.scalar.activation(idx[:, 0, :], edge_src[:, 0:GROUP], ACT.Copy).then_inc(s_idx, 1)

        @staticmethod
        def scalar_batch(act, i, jb):
            nj = (jb + 1) % NB
            b1 = i * NB + jb + 1
            if H == 1:
                nc.scalar.activation(place_now[:, nj % 2, :], edge_place[:, bass.ds(b1 * BATCH, BATCH)], ACT.Copy)
            act.wait_ge(s_scores, b1 + 1)
            nc.scalar.activation(weight[:, nj % 2, :, :], e_less[:, nj % 2, :, :], ACT.Exp).then_inc(s_w, 1)

        @staticmethod
        def scalar_index(act, i, jb, last):
            if jb % GB == 0 and not (last and jb + GB == NB):
                half = jb // GB + 1
                group = i * (NB // GB) + half
                act.wait_ge(s_prod, (group - 1) * (GROUP // UNIT) + RU)
                nc.scalar.activation(idx[:, half % 2, :], edge_src[:, bass.ds(group * GROUP, GROUP)],
                                     ACT.Copy).then_inc(s_idx, 1)

        @staticmethod
        def scalar_first(act):
            if H == 1:
                nc.scalar.activation(place_now[:, 0, :], edge_place[:, 0:BATCH], ACT.Copy)
            act.wait_ge(s_scores, 1)
            nc.scalar.activation(weight[:, 0, :, :], e_less[:, 0, :, :], ACT.Exp).then_inc(s_w, 1)

        @staticmethod
        def vector_start(dve):
            nc.vector.memset(zero_w[:, :], 0.0).then_inc(s_zero, 1)
            nc.vector.memset(zero_r[:, :], 0.0).then_inc(s_zero, 1)
            dve.sem_inc(s_rows_free, 2)

        @staticmethod
        def scores_of(dve, i, jb, stage):
            b = i * NB + jb
            h = jb % 2
            if stage == "node one-hot":
                dve.wait_ge(s_prow[h], (i * (NB // 2) + jb // 2 + 1) * 16)
                nc.vector.tensor_scalar(onehot_t[:, h, :], onehot_t[:, h, :], g["part_iota"][:, 0:1], None,
                                        ALU.is_equal).then_inc(s_oht, 1)
            if stage == "sum":
                dve.wait_ge(s_admp, b + 1)
                dve.sem_inc(s_rows_free, 1)
                nc.vector.tensor_reduce(
                    adm[:, h, :, :],
                    ps[:, 4, 0:BATCH * M * PARTS].rearrange("p (s m q) -> p s m q", s=BATCH, q=PARTS),
                    AX.X, ALU.add).then_inc(s_adm, 1)
                dve.wait_ge(s_adm, b + 1)
                for u in range(BU):
                    unit = jb * BU + u
                    dve.wait_ge(s_gath[unit % RU], (i * (NU // RU) + unit // RU + 1) * 16 * UNIT)
                    ins = nc.vector.tensor_tensor(
                        e_sum[:, h, u * UNIT:(u + 1) * UNIT, :], slots_of(unit)[:, :, F + H:F + 2 * H],
                        adm[:, h, u * UNIT:(u + 1) * UNIT, 0:H], ALU.add)
                ins.then_inc(s_e, 1)
            if stage == "leaky":
                dve.wait_ge(s_e, 2 * b + 1)
                nc.vector.scalar_tensor_tensor(e_leaky[:, h, :, :], e_sum[:, h, :, :], SLOPE, e_sum[:, h, :, :],
                                               ALU.mult, ALU.max).then_inc(s_e, 1)
            if stage == "less guard":
                dve.wait_ge(s_e, 2 * b + 2)
                nc.vector.tensor_tensor(e_less[:, h, :, :], e_leaky[:, h, :, :], adm[:, h, :, H:M], ALU.subtract
                                        ).then_inc(s_scores, 1)

        @staticmethod
        def weigh(dve, i, jb, u):
            b = i * NB + jb
            h = jb % 2
            if u == 0:
                if H > 1:
                    places = edge_place[:, bass.ds(b * BATCH, BATCH)]
                    nc.vector.tensor_tensor(onehot[:, h, :, :],
                                            g["lane"][:, :].unsqueeze(1).to_broadcast([P, BATCH, P]),
                                            places.unsqueeze(2).to_broadcast([P, BATCH, P]), ALU.is_equal
                                            ).then_inc(s_oh, 1)
                dve.wait_ge(s_w, b + 1)
            if H == 1:
                for j in range(u * UNIT, (u + 1) * UNIT):
                    ins = nc.vector.tensor_scalar(onehot[:, h, j, :], g["lane"][:, :],
                                                  place_now[:, h, j:j + 1], weight[:, h, j, :],
                                                  ALU.is_equal, ALU.mult)
            else:
                w_rows = slots_of(jb * BU + u)[:, :, 0:W].rearrange("p s (h c) -> p s h c", h=H)
                ins = nc.vector.tensor_tensor(
                    w_rows, w_rows, weight[:, h, u * UNIT:(u + 1) * UNIT, :].unsqueeze(3).to_broadcast(
                        [P, UNIT, H, W // H]), ALU.mult)
            ins.then_inc(s_wt, 1)

        @staticmethod
        def add_batch(dve, i, jb, which, state):
            b = i * NB + jb
            if which == 0:
                _, state["nodes"] = nc.values_load_multi_w_load_instructions(
                    batch_nodes[:, bass.ds(b * 2, 2)], engines=[dve.engine], min_val=0,
                    max_val=sums.shape[1] - 1,
                    skip_runtime_bounds_check_because="prepare() keeps it to the node tiles")
                dve.wait_ge(s_prod, (b + 1) * BU + RU)
            if not (isinstance(i, int) and b == 0 and which == 0):
                dve.wait_ge(s_add, 2 * b + which)
            tile = sums[:, bass.ds(state["nodes"][which], 1), 0:W].rearrange("p a c -> p (a c)")
            nc.vector.tensor_tensor(tile, ps[:, 2 * (jb % 2) + which, 0:W], tile, ALU.add).then_inc(s_add, 1)

        @staticmethod
        def vector_first(dve):
            for stage in ("node one-hot", "sum", "leaky", "less guard"):
                Parts.scores_of(dve, 0, 0, stage)
            for u in range(BU):
                Parts.weigh(dve, 0, 0, u)
            Parts.scores_of(dve, 0, 1, "node one-hot")

        @staticmethod
        def vector_piece(dve, i, j, last, state):
            jb, piece = j // BATCH, j % BATCH
            if piece in (2, 3) and not (isinstance(i, int) and i == 0 and jb == 0):
                Parts.add_batch(dve, i if jb else i - 1, (jb - 1) % NB, piece - 2, state)
            i1, jb1 = i + (jb + 1) // NB, (jb + 1) % NB
            if not (last and jb == NB - 1):
                if piece == 0:
                    Parts.scores_of(dve, i1, jb1, "sum")
                if piece == 1:
                    Parts.scores_of(dve, i1, jb1, "leaky")
                    Parts.scores_of(dve, i1, jb1, "less guard")
                if piece in (3, 5):
                    Parts.weigh(dve, i1, jb1, piece // 4)
            if piece == 4 and not (last and jb >= NB - 2):
                Parts.scores_of(dve, i + (jb + 2) // NB, (jb + 2) % NB, "node one-hot")

        @staticmethod
        def vector_last(dve, state):
            for which in (0, 1):
                Parts.add_batch(dve, ITERS - 1, NB - 1, which, state)

        @staticmethod
        def tensor_start(pe):
            pe.sem_inc(s_prod, RU)
            pe.wait_ge(s_table, 1)
            pe.wait_ge(s_zero, 2)

        @staticmethod
        def node_products(pe, i, jb):
            b = i * NB + jb
            _, nodes = nc.values_load_multi_w_load_instructions(
                step_node[0:1, bass.ds(b * BATCH, BATCH)], engines=[pe.engine], min_val=0, max_val=NT - 1,
                skip_runtime_bounds_check_because="prepare() keeps it to the node tiles")
            pe.wait_ge(s_oht, b + 1)
            if not isinstance(i, int) or b >= 1:
                pe.wait_ge(s_adm, b)
            for j in range(BATCH):
                mm = nc.tensor.matmul(ps[:, 4, j * M * PARTS:(j + 1) * M * PARTS],
                                      onehot_t[:, jb % 2, j * P:(j + 1) * P],
                                      table[:, bass.ds(nodes[j], 1), 0:M * PARTS].rearrange("p a c -> p (a c)"),
                                      start=True, stop=True)
            mm.then_inc(s_admp, 1)

        @staticmethod
        def tensor_step(pe, i, j, last, state):
            jb, q = j // BATCH, j % BATCH
            b = i * NB + jb
            first_bank = 2 * (jb % 2)
            if q == 0:
                _, state["banks"] = nc.values_load_multi_w_load_instructions(
                    step_bank[0:1, bass.ds(b * BATCH, BATCH)], engines=[pe.engine], min_val=0, max_val=1,
                    skip_runtime_bounds_check_because="a comparison's outcome")
                if not isinstance(i, int) or b >= 2:
                    pe.wait_ge(s_add, 2 * b - 2)
                nc.tensor.matmul(ps[:, first_bank + 1, 0:W], zero_w[:, :], zero_r[:, 0:W], start=True, stop=False,
                                 skip_group_check=True)
                if H > 1:
                    pe.wait_ge(s_oh, b + 1)
                pe.wait_ge(s_wt, (b + 1) * BU)
            bank = ps[:, first_bank, 0:W] if q == 0 else \
                ps[:, bass.ds(state["banks"][q] + first_bank, 1), 0:W].rearrange("p a c -> p (a c)")
            mm = nc.tensor.matmul(bank, onehot[:, jb % 2, q, :], ring[:, (jb * BATCH + q) % ring_slots, 0:W],
                                  start=q == 0, stop=q == BATCH - 1, skip_group_check=True)
            if q % UNIT == UNIT - 1:
                mm.then_inc(s_prod, 1)
            if q == BATCH - 1 and not (last and jb >= NB - 2):
                Parts.node_products(pe, i + (jb + 2) // NB, (jb + 2) % NB)

    Parts.onehot = onehot
    return Parts


def second_rows(nc, g, sb, sem):
    F, KC, ps, ident, acc, scores, w_aug = (g[k] for k in ("F", "KC", "ps", "ident", "acc", "scores", "w_aug"))
    H0 = g["HEADS"][0]
    W0 = F + H0
    C0 = F // H0
    zinv = sb("zinv", [P, 2, H0])
    hid = sb("hid", [P, 2, F])
    minus = sb("minus", [P, 2, F])
    plus = sb("plus", [P, 2, F])
    xT = sb("xT", [P, 2, KC, P])
    ones_col = sb("ones_col", [P, 1])
    s_z = sem("sum_inverted")
    s_hid, s_elu, s_h, s_tr, s_xT, s_mm, s_row, s_ones = (
        sem("hidden_ready"), sem("elu_parts_ready"), sem("elu_ready"), sem("hidden_transposed"), sem("hidden_T_ready"),
        sem("row_product"), sem("row_ready"), sem("ones_set"))

    class Stages:
        row_ready = s_row

        @staticmethod
        def start(dve):
            nc.vector.memset(ones_col[:, :], 1.0).then_inc(s_ones, 1)
            dve.sem_inc(s_elu, 2)
            dve.sem_inc(s_tr, 2)
            dve.sem_inc(s_mm, 2)
            dve.sem_inc(s_row, 2)

        @staticmethod
        def attention(dve, n, slot):
            tile = acc[:, bass.ds(n, 1), 0:W0].rearrange("p a (h c) -> p (a h) c", h=H0)
            nc.vector.reciprocal(zinv[:, slot, :], tile[:, :, C0]).then_inc(s_z, 1)
            dve.wait_ge(s_z, n + 1)
            dve.wait_ge(s_tr, n + 1)
            for h in range(H0):
                cols = slice(h * C0, (h + 1) * C0)
                ins = nc.vector.scalar_tensor_tensor(hid[:, slot, cols], tile[:, h, 0:C0], zinv[:, slot, h:h + 1],
                                                     g["bias_rows"][:, 0, cols], ALU.mult, ALU.add)
            ins.then_inc(s_hid, 1)

        @staticmethod
        def elu_parts(act, n, slot):
            act.wait_ge(s_hid, n + 1)
            nc.scalar.activation(plus[:, slot, :], hid[:, slot, :], ACT.Relu).then_inc(s_elu, 0 + 1)
            nc.scalar.activation(minus[:, slot, :], hid[:, slot, :], ACT.Relu, scale=-1.0).then_inc(s_elu, 1)
            act.wait_ge(s_elu, 3 * n + 2 + 2)
            nc.scalar.activation(minus[:, slot, :], minus[:, slot, :], ACT.Exp, scale=-1.0).then_inc(s_elu, 1)

        @staticmethod
        def elu(dve, n, slot):
            dve.wait_ge(s_elu, 3 * n + 3 + 2)
            nc.vector.scalar_tensor_tensor(hid[:, slot, :], minus[:, slot, :], -1.0, plus[:, slot, :],
                                           ALU.add, ALU.add).then_inc(s_h, 1)

        @staticmethod
        def transposes(pe, n, slot, bank):
            pe.wait_ge(s_h, n + 1)
            for k in range(KC):
                mm = nc.tensor.transpose(ps[:, bank, k * P:(k + 1) * P], hid[:, slot, k * P:(k + 1) * P], ident[:, :])
            mm.then_inc(s_tr, 1)

        @staticmethod
        def transposed(act, n, slot, bank):
            act.wait_ge(s_tr, n + 1 + 2)
            act.wait_ge(s_mm, n + 1)
            nc.scalar.activation(xT[:, slot, :, :], ps[:, bank, 0:KC * P].rearrange("p (k q) -> p k q", k=KC),
                                 ACT.Copy).then_inc(s_xT, 1)

        @staticmethod
        def product(pe, n, slot, bank):
            pe.wait_ge(s_xT, n + 1)
            pe.wait_ge(s_row, n + 1)
            for k in range(KC):
                mm = nc.tensor.matmul(ps[:, bank, 0:F + 2], xT[:, slot, k, :], w_aug[:, 1, k, 0:F + 2],
                                      start=k == 0, stop=k == KC - 1)
            mm.then_inc(s_mm, 1)

        @staticmethod
        def row(act, n, bank):
            act.wait_ge(s_mm, n + 1 + 2)
            nc.scalar.activation(acc[:, bass.ds(n, 1), 0:F], ps[:, bank, 0:F].unsqueeze(1), ACT.Copy)
            nc.scalar.activation(acc[:, bass.ds(n, 1), F:F + 1], ones_col[:, :].unsqueeze(1), ACT.Copy)
            nc.scalar.activation(acc[:, bass.ds(n, 1), F + 1:F + 2], ps[:, bank, F:F + 1].unsqueeze(1), ACT.Copy)
            nc.scalar.activation(scores[:, bass.ds(n, 1), 0:2], ps[:, bank, F:F + 2].unsqueeze(1), ACT.Copy
                                 ).then_inc(s_row, 1)

        @staticmethod
        def store(sp, n):
            sp.wait_ge(s_row, n + 1 + 2)
            sp.sem_inc(s_stored_turn, 1)
            sp.dma_start(g["rows_dram"][1][bass.ds(n * P, P), :], acc[:, bass.ds(n, 1), 0:F + 2]
                         .rearrange("p a c -> p (a c)")).then_inc(s_stored, 16)

    s_stored, s_stored_turn = sem("row_stored"), sem("store_turn")
    Stages.stored = s_stored
    return Stages


def first_edges(nc, g):
    F, NT, ITERS, HEADS = g["F"], g["NT"], g["ITERS"], g["HEADS"]
    H = HEADS[0]
    W = F + H
    acc = g["acc"]
    NB = BODY // BATCH
    PER = BODY // GT
    BEHIND = (ITERS - 1) * GT
    with ExitStack() as ctx:
        def sb(name, shape, dt=F32):
            return ctx.enter_context(nc.sbuf_tensor(f"{name}_e0", shape, dt))

        sem = g["sem"]
        table, self_w, s_table, guard_act, guard_dve = guards(nc, g, 0, sb, sem)
        parts = edge_parts(nc, g, 0, sb, sem, table, s_table, acc, RING, "all")
        rows = second_rows(nc, g, sb, sem)
        choose_pool, choose_vector = choose_path(nc, g, 1, sb, sem)
        s_loops = sem("loops_weighted")
        block = ctx.enter_context(nc.Block())

        def loop(eng, edge, stages):
            def body(i, last):
                for j in range(BODY):
                    edge(i, j, last)
                    if j % PER in stages and not (isinstance(i, int) and i == 0):
                        stages[j % PER]((i - 1) * GT + j // PER, j // PER % 2, (5, 6))

            body(0, False)
            with eng.Fori(1, ITERS - 1) as i:
                body(i, False)
            body(ITERS - 1, True)

        def rest(stages):
            order = sorted(stages)
            for turn in range(NT - BEHIND + LAG[-1]):
                for q in reversed(order):
                    n = BEHIND + turn - LAG[ORDER.index(q)]
                    if BEHIND <= n < NT:
                        stages[q](n, n % 2, ((5, 6), (0, 1))[n % 2])

        ORDER = (4, 7, 9, 10, 12, 14, 16, 17)
        LAG = (0, 0, 1, 1, 1, 2, 2, 2)

        @block.sync
        def _(sp):
            with sp.If(listed(nc, sp, g, 0) == 0):
                for jb in range(2):
                    parts.sync_batch(sp, 0, jb)

                def edge(i, j, last):
                    jb = j // BATCH + 2
                    if j % BATCH == 0 and not (last and jb >= NB):
                        parts.sync_batch(sp, i + jb // NB, jb % NB)

                stages = {17: lambda n, slot, banks: rows.store(sp, n)}
                loop(sp, edge, stages)
                rest(stages)
                sp.wait_ge(rows.stored, 16 * NT)

        @block.gpsimd
        def _(pool):
            with pool.If(listed(nc, pool, g, 0) == 0):
                with pool.Fori(0, ITERS) as i:
                    for jb in range(NB):
                        parts.gpsimd_batch(pool, i, jb)
                choose_pool(pool)

        @block.scalar
        def _(act):
            with act.If(listed(nc, act, g, 0) == 0):
                parts.scalar_start(act)
                guard_act(act)
                parts.scalar_first(act)

                def edge(i, j, last):
                    jb, q = j // BATCH, j % BATCH
                    if q == 1 and not (last and jb == NB - 1):
                        parts.scalar_batch(act, i, jb)
                    if q == 7:
                        parts.scalar_index(act, i, jb, last)

                stages = {7: lambda n, slot, banks: rows.elu_parts(act, n, slot),
                          12: lambda n, slot, banks: rows.transposed(act, n, slot, banks[0]),
                          16: lambda n, slot, banks: rows.row(act, n, banks[1])}
                loop(act, edge, stages)
                rest(stages)

        @block.vector
        def _(dve):
            with dve.If(listed(nc, dve, g, 0) == 0):
                state = {}
                guard_dve(dve)
                parts.vector_start(dve)
                rows.start(dve)
                loops = acc[:, :, 0:W].rearrange("p n (h c) -> p n h c", h=H)
                nc.vector.tensor_tensor(loops, loops, self_w[:, :, :].unsqueeze(3).to_broadcast(
                    [P, NT, H, W // H]), ALU.mult).then_inc(s_loops, 1)
                parts.vector_first(dve)
                dve.wait_ge(s_loops, 1)

                def edge(i, j, last):
                    parts.vector_piece(dve, i, j, last, state)

                stages = {4: lambda n, slot, banks: rows.attention(dve, n, slot),
                          9: lambda n, slot, banks: rows.elu(dve, n, slot)}
                loop(dve, edge, stages)
                parts.vector_last(dve, state)
                dve.wait_ge(parts.sums_added, 2 * NB * ITERS)
                rest(stages)
                dve.wait_ge(rows.row_ready, NT + 2)
                choose_vector(dve)

        @block.tensor
        def _(pe):
            with pe.If(listed(nc, pe, g, 0) == 0):
                state = {}
                parts.tensor_start(pe)
                parts.node_products(pe, 0, 0)
                parts.node_products(pe, 0, 1)

                def edge(i, j, last):
                    parts.tensor_step(pe, i, j, last, state)

                stages = {10: lambda n, slot, banks: rows.transposes(pe, n, slot, banks[0]),
                          14: lambda n, slot, banks: rows.product(pe, n, slot, banks[1])}
                loop(pe, edge, stages)
                pe.wait_ge(parts.sums_added, 2 * NB * ITERS)
                rest(stages)


def listed(nc, eng, g, layer):
    _, values = nc.values_load_multi_w_load_instructions(
        g["by_list"][0:1, layer:layer + 1], engines=[eng.engine], min_val=0, max_val=1,
        skip_runtime_bounds_check_because="a comparison's outcome")
    return values[0]


def general_edges(nc, g, layer):
    E, ET, F, NT, N = g["E"], g["ET"], g["F"], g["NT"], g["N"]
    H = g["HEADS"][layer]
    W = F + H
    ps, ident, acc, scores = g["ps"], g["ident"], g["acc"], g["scores"]
    rows_dram, scores_dram, totals_dram = g["rows_dram"][layer], g["scores_dram"][layer], g["totals_dram"][layer]
    tail = E - (ET - 1) * P
    with ExitStack() as ctx:
        def sb(name, shape, dt=F32):
            return ctx.enter_context(nc.sbuf_tensor(f"g_{name}{layer}", shape, dt))

        sem = g["sem"]
        state = sb("state", [P, NT, 2 * H])
        src_of = {False: sb("src_of", [P, 1], I32), True: sb("src_of_last", [P, 1], I32)}
        dst_of = {False: sb("dst_of", [P, 1], I32), True: sb("dst_of_last", [P, 1], I32)}
        dst_f = sb("dst_f", [P, 1])
        rows = sb("rows", [P, F + 2 * H])
        node = sb("node", [P, 2 * H])
        total = sb("total", [P, W])
        diag = sb("diag", [P, 1 + H, P])
        ones = sb("ones", [P, P])
        same = sb("same", [P, P])
        out_of = sb("out_of", [P, P])
        held = sb("held", [P, H, P])
        best = sb("best", [P, H])
        e_sum = sb("e_sum", [P, H])
        guard = sb("guard", [P, H])
        weight = sb("weight", [P, H])
        node_sum = sb("node_sum", [P, NT, H])
        node_guard = sb("node_guard", [P, NT, H])
        node_w = sb("node_w", [P, NT, H])
        sums = sb("sums", [P, 7, W])

        s_set, s_init, s_turn = sem("state_set"), sem("state_stored"), sem("turn")
        s_list, s_free = sem("list_landed"), sem("list_used")
        s_got, s_node, s_put = g["listed_rows"][layer]
        s_diag, s_bc = sem("diagonals_ready"), sem("rows_broadcast")
        s_new = sem("new_state_ready")
        s_score, s_exp, s_prod = sem("scores_ready"), sem("weights_ready"), sem("sums_ready")
        s_c, s_back, s_taken, s_final = sem("dve_chain"), sem("totals_back"), sem("totals_used"), sem("rows_stored")
        block = ctx.enter_context(nc.Block())
        R = NT // 7

        def tiles(eng, step, passes=(0, ET)):
            for base in passes:
                with eng.Fori(0, ET - 1) as e:
                    step(e, e + base, base > 0, False)
                step(ET - 1, base + ET - 1, base > 0, True)

        def by_tile(dram, first, tiles_):
            return dram.rearrange("(n p) c -> p n c", p=P)[:, bass.ds(first, tiles_), :]

        @block.sync
        def _(sp):
            with sp.If(listed(nc, sp, g, layer) == 1):
                sp.wait_ge(s_set, 1)
                sp.dma_start(by_tile(scores_dram, 0, NT), state[:, :, :]).then_inc(s_init, 16)
                for r in range(R):
                    sp.dma_start(by_tile(totals_dram, r * 7, 7), sums[:, :, :]).then_inc(s_init, 16)

                def step(e, n, second, last):
                    sp.wait_ge(s_free, n + 1)
                    sp.sem_inc(s_turn, 1)
                    if last:
                        sp.dma_start(src_of[True][0:tail, :], g["src"][(ET - 1) * P:E].rearrange("(p a) -> p a", a=1)
                                     ).then_inc(s_list, 16)
                        sp.dma_start(dst_of[True][0:tail, :], g["dst"][(ET - 1) * P:E].rearrange("(p a) -> p a", a=1)
                                     ).then_inc(s_list, 16)
                    else:
                        sp.dma_start(src_of[False][:, :], g["src"][bass.ds(e * P, P)].rearrange("(p a) -> p a", a=1)
                                     ).then_inc(s_list, 16)
                        sp.dma_start(dst_of[False][:, :], g["dst"][bass.ds(e * P, P)].rearrange("(p a) -> p a", a=1)
                                     ).then_inc(s_list, 16)

                tiles(sp, step)
                sp.wait_ge(s_put, 16 * 2 * ET)
                sp.dma_start(state[:, :, :], by_tile(scores_dram, 0, NT)).then_inc(s_back, 16)
                for r in range(R):
                    if r:
                        sp.wait_ge(s_taken, r)
                    sp.dma_start(sums[:, :, :], by_tile(totals_dram, r * 7, 7)).then_inc(s_back, 16)
                sp.wait_ge(s_taken, R)
                if layer == 1:
                    sp.dma_start(by_tile(rows_dram, 0, NT), acc[:, :, 0:F + 2 * H]).then_inc(s_final, 16)
                    sp.wait_ge(s_final, 16)

        @block.gpsimd
        def _(pool):
            with pool.If(listed(nc, pool, g, layer) == 1):
                pool.wait_ge(s_init, 16 * (R + 1))

                def step(e, n, second, last):
                    pool.wait_ge(s_list, n * 32 + 32)
                    pool.sem_inc(s_turn, 1)
                    nc.gpsimd.indirect_dma_start(rows[:, :], None, rows_dram,
                                                 bass.IndirectOffsetOnAxis(src_of[last][:, 0:1], 0)).then_inc(s_got, 16)
                    nc.gpsimd.indirect_dma_start(node[:, :], None, scores_dram,
                                                 bass.IndirectOffsetOnAxis(dst_of[last][:, 0:1], 0)).then_inc(s_node, 16)
                    if second:
                        nc.gpsimd.indirect_dma_start(total[:, :], None, totals_dram,
                                                     bass.IndirectOffsetOnAxis(dst_of[last][:, 0:1], 0)).then_inc(s_node, 16)
                    pool.wait_ge(s_new, n + 1)
                    pool.sem_inc(s_turn, 1)
                    if second:
                        nc.gpsimd.indirect_dma_start(totals_dram, bass.IndirectOffsetOnAxis(dst_of[last][:, 0:1], 0),
                                                     total[:, :], None).then_inc(s_put, 16)
                    else:
                        nc.gpsimd.indirect_dma_start(scores_dram, bass.IndirectOffsetOnAxis(dst_of[last][:, 0:1], 0),
                                                     node[:, :], None).then_inc(s_put, 16)
                    pool.wait_ge(s_put, n * 16 + 16)
                    pool.sem_inc(s_free, 1)

                tiles(pool, step)

        @block.scalar
        def _(act):
            with act.If(listed(nc, act, g, layer) == 1):
                def step(e, n, second, last):
                    act.wait_ge(s_score, n - (ET - 1))
                    nc.scalar.activation(weight[:, :], e_sum[:, :], ACT.Exp).then_inc(s_exp, 1)

                tiles(act, step, passes=(ET,))
                act.wait_ge(s_score, ET + 1)
                nc.scalar.activation(node_w[:, :, :], node_sum[:, :, :], ACT.Exp).then_inc(s_exp, 1)

        @block.tensor
        def _(pe):
            with pe.If(listed(nc, pe, g, layer) == 1):
                def step(e, n, second, last):
                    pe.wait_ge(s_diag, n + 1)
                    for m in range(1 if second else 1 + H):
                        mm = nc.tensor.matmul(ps[:, m, 0:P], ones[:, :], diag[:, m, :], start=True, stop=True)
                    mm.then_inc(s_bc, 1)
                    if second:
                        pe.wait_ge(s_prod, n - (ET - 1))
                        nc.tensor.matmul(ps[:, 6, 0:W], same[:, :], rows[:, 0:W], start=True, stop=True
                                         ).then_inc(s_bc, 1)

                tiles(pe, step)

        @block.vector
        def _(dve):
            with dve.If(listed(nc, dve, g, layer) == 1):
                CHAIN = {False: 3 + 2 * H, True: 7}

                nc.vector.memset(src_of[True][:, :], 0).then_inc(s_c, 1)
                nc.vector.memset(dst_of[True][:, :], N).then_inc(s_c, 1)
                nc.vector.memset(ones[:, :], 1.0).then_inc(s_c, 1)
                nc.vector.tensor_copy(state[:, :, 0:H], scores[:, :, H:2 * H]).then_inc(s_c, 1)
                nc.vector.tensor_copy(state[:, :, H:2 * H], scores[:, :, 0:H]).then_inc(s_c, 1)
                nc.vector.memset(sums[:, :, :], 0.0).then_inc(s_c, 1)
                dve.wait_ge(s_c, 6)
                dve.sem_inc(s_set, 1)
                dve.sem_inc(s_free, 1)

                def step(e, n, second, last):
                    if not second:
                        links = 6 + n * CHAIN[False]
                    else:
                        links = 6 + ET * CHAIN[False] + (n - ET) * CHAIN[True]
                    done = [0]

                    def then(ins):
                        done[0] += 1
                        ins.then_inc(s_c, 1)
                        dve.wait_ge(s_c, links + done[0])

                    dve.wait_ge(s_list, n * 32 + 32)
                    then(nc.vector.tensor_copy(dst_f[:, :], dst_of[last][:, :]))
                    if second:
                        dve.wait_ge(s_got, n * 16 + 16)
                        nc.vector.tensor_scalar(diag[:, 0, :], ident[:, :], dst_f[:, 0:1], None, ALU.mult
                                                ).then_inc(s_diag, 1)
                    else:
                        nc.vector.tensor_scalar(diag[:, 0, :], ident[:, :], dst_f[:, 0:1], None, ALU.mult)
                        dve.wait_ge(s_got, n * 16 + 16)
                        for h in range(H):
                            ins = nc.vector.tensor_scalar(diag[:, 1 + h, :], ident[:, :],
                                                          rows[:, F + H + h:F + H + h + 1], None, ALU.mult)
                        ins.then_inc(s_diag, 1)
                    if second:
                        dve.wait_ge(s_bc, ET + (n - ET) * 2 + 1)
                        then(nc.vector.tensor_scalar(same[:, :], ps[:, 0, 0:P], dst_f[:, 0:1], None, ALU.is_equal))
                        dve.wait_ge(s_node, ET * 16 + (n - ET) * 32 + 32)
                        then(nc.vector.tensor_tensor(guard[:, :], node[:, 0:H], node[:, H:2 * H], ALU.add))
                        then(nc.vector.scalar_tensor_tensor(guard[:, :], guard[:, :], SLOPE, guard[:, :],
                                                            ALU.mult, ALU.max))
                        then(nc.vector.tensor_tensor(e_sum[:, :], node[:, 0:H], rows[:, F + H:F + 2 * H], ALU.add))
                        then(nc.vector.scalar_tensor_tensor(e_sum[:, :], e_sum[:, :], SLOPE, e_sum[:, :],
                                                            ALU.mult, ALU.max))
                        nc.vector.tensor_tensor(e_sum[:, :], e_sum[:, :], guard[:, :], ALU.subtract
                                                ).then_inc(s_score, 1)
                        dve.wait_ge(s_exp, n - (ET - 1))
                        w_rows = rows[:, 0:W].rearrange("p (h c) -> p h c", h=H)
                        nc.vector.tensor_tensor(w_rows, w_rows, weight[:, :].unsqueeze(2).to_broadcast(
                            [P, H, W // H]), ALU.mult).then_inc(s_prod, 1)
                        dve.wait_ge(s_bc, ET + (n - ET) * 2 + 2)
                        then(nc.vector.tensor_tensor(total[:, :], ps[:, 6, 0:W], total[:, :], ALU.add))
                        assert done[0] == CHAIN[True]
                        dve.sem_inc(s_new, 1)
                    else:
                        dve.wait_ge(s_bc, n + 1)
                        then(nc.vector.tensor_scalar(same[:, :], ps[:, 0, 0:P], dst_f[:, 0:1], None, ALU.is_equal))
                        then(nc.vector.tensor_scalar(out_of[:, :], same[:, :], -1.0, FAR, ALU.add, ALU.mult))
                        for h in range(H):
                            then(nc.vector.tensor_tensor(held[:, h, :], ps[:, 1 + h, 0:P], out_of[:, :], ALU.add))
                            then(nc.vector.tensor_reduce(best[:, h:h + 1], held[:, h, :], AX.X, ALU.max))
                        assert done[0] == CHAIN[False]
                        dve.wait_ge(s_node, n * 16 + 16)
                        nc.vector.tensor_tensor(node[:, H:2 * H], node[:, H:2 * H], best[:, :], ALU.max
                                                ).then_inc(s_new, 1)

                tiles(dve, step)
                done = [6 + ET * (CHAIN[False] + CHAIN[True])]

                def then(ins):
                    done[0] += 1
                    ins.then_inc(s_c, 1)
                    dve.wait_ge(s_c, done[0])

                dve.wait_ge(s_back, 32)
                then(nc.vector.tensor_tensor(node_guard[:, :, :], state[:, :, 0:H], state[:, :, H:2 * H], ALU.add))
                then(nc.vector.scalar_tensor_tensor(node_guard[:, :, :], node_guard[:, :, :], SLOPE,
                                                    node_guard[:, :, :], ALU.mult, ALU.max))
                then(nc.vector.tensor_tensor(node_sum[:, :, :], scores[:, :, 0:H], scores[:, :, H:2 * H], ALU.add))
                then(nc.vector.scalar_tensor_tensor(node_sum[:, :, :], node_sum[:, :, :], SLOPE,
                                                    node_sum[:, :, :], ALU.mult, ALU.max))
                nc.vector.tensor_tensor(node_sum[:, :, :], node_sum[:, :, :], node_guard[:, :, :], ALU.subtract
                                        ).then_inc(s_score, 1)
                dve.wait_ge(s_exp, ET + 1)
                own = acc[:, :, 0:W].rearrange("p n (h c) -> p n h c", h=H)
                then(nc.vector.tensor_tensor(own, own, node_w[:, :, :].unsqueeze(3).to_broadcast(
                    [P, NT, H, W // H]), ALU.mult))
                for r in range(R):
                    dve.wait_ge(s_back, (r + 2) * 16)
                    nc.vector.tensor_tensor(acc[:, r * 7:(r + 1) * 7, 0:W], acc[:, r * 7:(r + 1) * 7, 0:W],
                                            sums[:, :, :], ALU.add).then_inc(s_taken, 1)


def edges_and_mixture(nc, g):
    N, F, NT, LAST, KC, X, ITERS = (g[k] for k in ("N", "F", "NT", "LAST", "KC", "X", "ITERS"))
    ps, ident, bias_rows = g["ps"], g["ident"], g["bias_rows"]
    ffn, x, out = g["ffn"], g["x"], g["out"]
    rows_dram = g["rows_dram"][1]
    W = F + 1
    NB = BODY // BATCH
    TOK = GT * P
    GROUPS = (NT - 1) // GT
    assert NT - 1 == GROUPS * GT and GROUPS + 1 >= ITERS
    STEPS_BEFORE = {"bias": 0, "sums": 4, "attention": 6, "stats": 8, "deviation": 10, "norm": 12, "transpose": 14,
                    "split": 16, "logits": 16, "softmax": 18, "shares": 20, "share_T": 22, "biased": 24}
    FIRST_SLOT_STEP = 26
    PIECES = list(STEPS_BEFORE)
    with ExitStack() as ctx:
        def sb(name, shape, dt=F32):
            return ctx.enter_context(nc.sbuf_tensor(f"m_{name}", shape, dt))

        sem = g["sem"]
        w_hi = sb("w_hi", [P, 3, X, KC, F], F32R)
        w_lo = sb("w_lo", [P, 3, X, KC, F], F32R)
        h_hi = sb("h_hi", [P, 2, KC, TOK], F32R)
        h_lo = sb("h_lo", [P, 2, KC, TOK], F32R)
        h_f = sb("h_f", [P, 2, TOK])
        x_hi = sb("x_hi", [P, KC, TOK], F32R)
        x_lo = sb("x_lo", [P, KC, TOK], F32R)
        xr = sb("xr", [P, 2, GT, F])
        own = sb("own", [P, GT, F + 2])
        xn = own
        bn_rows = xr[0:2 * 5 * X, 1, 0, :]
        bn = sb("bn", [P, KC, 2, 5, X])
        bn_s = sb("bn_s", [P, KC, 2, X])
        bn_t = sb("bn_t", [P, KC, 2, X])
        wr = sb("wr", [P, KC, X])
        br = sb("br", [P, X])
        bo = sb("bo", [X, F])
        stats = sb("stats", [P, GT, 6])
        mv = sb("mv", [P, GT, 2])
        rstd = sb("rstd", [P, GT, 1])
        eps = sb("eps", [P, 3])
        zinv = sb("zinv", [P, GT, 1])
        logit = sb("logit", [P, GT, X])
        lmax = sb("lmax", [P, GT, 1])
        lsum = sb("lsum", [P, GT, 1])
        probs = [sb(f"prob{n}_", [P, GT, X]) for n in (0, 1)]
        loop_w = sb("loop_w", [P, GT, 1])
        probT = sb("probT", [X, GT, P])
        sums = sb("sums", [P, SUM_TILES, W])
        w_raw = h_f

        def xr_half(half, tiles):
            return xr[:, bass.ds(half, 1), 0:tiles, :].rearrange("p a n f -> p (a n) f")

        assert TOK == KC * F

        def columns_of(ahead):
            if ahead:
                return lambda c: parts.onehot[:, c, 0:GT, :].rearrange("p s q -> p (s q)")
            return lambda c: h_f[:, c, :]

        def prob_of(grp):
            return probs[grp % 2] if isinstance(grp, int) and grp >= ITERS - 1 else probs[(ITERS - 1) % 2]

        def banks_of(ahead):
            return (0, 1, 2, 3, 0, 1) if ahead else (5, 6, 7, 5, 7, 6)


        table, self_w, s_table, guard_act, guard_dve = guards(nc, g, 1, sb, sem)
        parts = edge_parts(nc, g, 1, sb, sem, table, s_table, sums, RING2, "ring")

        s_small, s_eps, s_bnc, s_bnq, s_turn = (
            sem("small_landed"), sem("eps_set"), sem("bn_chain"), sem("bn_sqrt"), sem("turn"))
        s_sp_turn, s_bnT = sem("group_turn"), sem("bn_transposed")
        s_raw = [sem("raw_landed0"), sem("raw_landed1")]
        s_whi, s_wlo = sem("w_hi_ready"), sem("w_lo_ready")
        s_x, s_own, s_own_free = sem("x_landed"), sem("own_rows_landed"), sem("own_rows_used")
        s_zer = sem("sums_zeroed")
        s_loop = sem("loop_weights")
        s_c, s_sq, s_xn, s_tr = sem("norm_chain"), sem("std_ready"), sem("norm_ready"), sem("transposed")
        s_st = sem("stats_ready")
        s_r = sem("router_chain")
        s_xhi, s_xlo, s_xf = sem("x_hi_ready"), sem("x_lo_ready"), sem("xT_ready")
        s_log, s_lm, s_ex, s_pr, s_pt, s_ptc, s_bop, s_yin = (
            sem("logits_ready"), sem("logits_less_max"), sem("router_exp"), sem("prob_ready"), sem("prob_transposed"),
            sem("probT_ready"), sem("bias_product"), sem("bias_added"))
        s_h, s_hf, s_hhi, s_hlo = sem("hidden_product"), sem("hidden_ready"), sem("hidden_hi"), sem("hidden_lo")
        s_y, s_ya, s_out = sem("y_product"), sem("y_added"), sem("stored")
        block = ctx.enter_context(nc.Block())
        names = (("b1", "g1", "be1", "m1", "v1"), ("b2", "g2", "be2", "m2", "v2"))
        CH = 2 * KC * X
        NSM = 2 * 5 + 2 + KC
        NW = 3 * X

        def products_of(tiles):
            yield "hidden", 0, 0, 0, 7
            yield "hidden", 0, 0, 1, 5
            for e in range(X):
                yield "hidden", 1, e, 0, 5
                yield "hidden", 1, e, 1, 6
                if e + 1 < X:
                    yield "hidden", 0, e + 1, 0, 7
                    yield "hidden", 0, e + 1, 1, 5
                yield "output", 2, e, 0, 6
                if tiles > 2:
                    yield "output", 2, e, 1, 7

        slots = list(products_of(GT))
        SLOTS = len(slots)
        hidden = [(m, e, c) for kind, m, e, c, _ in slots if kind == "hidden"]
        rank = {k: n for n, k in enumerate(hidden)}

        AHEAD = dict(zip([p for p in PIECES if p != "split"], (8, 10, 12, 14, 16, 18, 20, 23, 26, 29, 32, 35)))
        AHEAD["split"] = slots.index(("hidden", 0, X - 1, KC - 1, 5)) + 1

        def step_of(k):
            return FIRST_SLOT_STEP + (BODY - FIRST_SLOT_STEP) * k // SLOTS

        def outputs_before(grp, tiles, e, c):
            return grp * 2 * X + e * (2 if tiles > 2 else 1) + c

        def slots_of_group(tiles):
            return len(list(products_of(tiles)))

        def schedule(eng, ordered, edge, part):
            def iteration(i, group, last=False):
                starts = [STEPS_BEFORE[p] for p in PIECES] + [step_of(k) for k in range(SLOTS)] + [BODY]
                for n, k in enumerate(PIECES + list(range(SLOTS))):
                    part(group, GT, k)
                    if ordered:
                        for j in range(starts[n], starts[n + 1]):
                            edge(i, j, last)

            iteration(0, None)
            with eng.Fori(1, ITERS - 1) as i:
                iteration(i, i - 1)
            iteration(ITERS - 1, ITERS - 2, last=True)
            for p in PIECES:
                part(ITERS - 1, GT, p)
            for group in range(ITERS - 1, GROUPS + 1):
                tiles = GT if group < GROUPS else 1
                for k in range(slots_of_group(tiles)):
                    part(group, tiles, k)
                    for p in PIECES:
                        if group < GROUPS and AHEAD[p] == k:
                            part(group + 1, GT if group + 1 < GROUPS else 1, p, ahead=True)

        @block.sync
        def _(sp):
            def program(ordered):
                for l in (0, 1):
                    for n, name in enumerate(names[l]):
                        first = (l * 5 + n) * X
                        sp.dma_start(bn_rows[first:first + X, :], ffn[name]).then_inc(s_small, 16)
                for k in range(KC):
                    sp.dma_start(wr[:, k, :], ffn["Wr"][k * P:(k + 1) * P, :]).then_inc(s_small, 16)
                sp.dma_start(br[:, :], ffn["br"].partition_broadcast(P)).then_inc(s_small, 16)
                sp.dma_start(bo[:, :], ffn["bo"]).then_inc(s_small, 16)

                if ordered:
                    for jb in range(2):
                        parts.sync_batch(sp, 0, jb)

                def edge(i, j, last):
                    jb = j // BATCH + 2
                    if j % BATCH == 0 and not (last and jb >= NB):
                        parts.sync_batch(sp, i + jb // NB, jb % NB)

                def load_group(grp, tiles):
                    if tiles == 1:
                        sp.dma_start(xr[0:LAST, GROUPS % 2, 0, :], x[(NT - 1) * P:N, :]).then_inc(s_x, 16)
                        sp.dma_start(own[:, 0:1, :], rows_dram[(NT - 1) * P:NT * P, :].rearrange(
                            "(n p) c -> p n c", p=P)).then_inc(s_own, 16)
                    else:
                        sp.dma_start(xr_half(grp % 2, GT), x[bass.ds(grp * TOK, TOK), :].rearrange(
                            "(n p) f -> p n f", p=P)).then_inc(s_x, 16)
                        sp.dma_start(own[:, :, :], rows_dram[bass.ds(grp * TOK, TOK), :].rearrange(
                            "(n p) c -> p n c", p=P)).then_inc(s_own, 16)

                sp.wait_ge(s_eps, 4)
                load_group(0, GT)
                sp.sem_inc(s_out, 16)

                def part(grp, tiles, k, ahead=False):
                    if grp is None:
                        if isinstance(k, int):
                            n = k // 2
                            if k % 2 or n >= NW:
                                return
                            if n >= 2:
                                sp.wait_ge(s_wlo, n - 1)
                            sp.dma_start(w_raw[:, n % 2, :].rearrange("p (k n) -> p k n", n=F),
                                         ffn[("W1", "W2", "Wo")[n // X]][n % X].rearrange("(k p) n -> p k n", p=P)
                                         ).then_inc(s_raw[n % 2], 16)
                        return
                    half = grp % 2
                    if k == 4:
                        nxt = grp + 1
                        if tiles == GT:
                            sp.wait_ge(s_tr, KC * nxt)
                            sp.sem_inc(s_sp_turn, 1)
                            sp.wait_ge(s_out, 16 * nxt)
                            sp.sem_inc(s_sp_turn, 1)
                            load_group(nxt, GT if not isinstance(nxt, int) or nxt < GROUPS else 1)
                    if k == slots_of_group(tiles) - 1:
                        sp.wait_ge(s_ya, 1 + grp * GT * X + tiles * X)
                        sp.sem_inc(s_sp_turn, 1)
                        if tiles == 1:
                            sp.dma_start(out[(NT - 1) * P:N, :], xr[0:LAST, GROUPS % 2, 0, :]).then_inc(s_out, 16)
                        else:
                            sp.dma_start(out[bass.ds(grp * TOK, TOK), :].rearrange("(n p) f -> p n f", p=P),
                                         xr_half(half, GT)).then_inc(s_out, 16)

                schedule(sp, ordered, edge, part)
                sp.wait_ge(s_out, 16 * (GROUPS + 2))

            with sp.If(listed(nc, sp, g, 1) == 0):
                program(True)
            with sp.If(listed(nc, sp, g, 1) == 1):
                program(False)

        @block.gpsimd
        def _(pool):
            def program(ordered):

                if ordered:
                    with pool.Fori(0, ITERS) as i:
                        for jb in range(NB):
                            parts.gpsimd_batch(pool, i, jb)

            with pool.If(listed(nc, pool, g, 1) == 0):
                program(True)

        @block.scalar
        def _(act):
            def program(ordered):
                if ordered:
                    parts.scalar_start(act)
                    guard_act(act)
                act.wait_ge(s_eps, 3)
                if ordered:
                    parts.scalar_first(act)

                def edge(i, j, last):
                    jb, q = j // BATCH, j % BATCH
                    if q == 1 and not (last and jb == NB - 1):
                        parts.scalar_batch(act, i, jb)
                    if q == 7:
                        parts.scalar_index(act, i, jb, last)

                def part(grp, tiles, k, ahead=False):
                    if grp is None:
                        if k == "deviation":
                            act.wait_ge(s_bnq, 1)
                            nc.scalar.activation(bn[:, :, :, 4, :], bn[:, :, :, 4, :], ACT.Sqrt, bias=eps[:, 1:2]
                                                 ).then_inc(s_bnq, 1)
                        if isinstance(k, int):
                            n = k // 2
                            if k % 2 or n >= NW:
                                return
                            act.wait_ge(s_raw[n % 2], 16 * (n // 2 + 1))
                            nc.scalar.activation(w_hi[:, n // X, n % X, :, :].rearrange("p k n -> p (k n)"),
                                                 w_raw[:, n % 2, :], ACT.Copy).then_inc(s_whi, 1)
                        return
                    T = tiles * P
                    if k == "deviation":
                        act.wait_ge(s_st, grp + 1)
                        nc.scalar.activation(rstd[:, 0:tiles, :], mv[:, 0:tiles, 1:2], ACT.Sqrt, bias=eps[:, 0:1]
                                             ).then_inc(s_sq, 1)
                    if k == "bias":
                        act.wait_ge(s_own_free, grp + 1)
                        nc.scalar.activation(loop_w[:, 0:tiles, :], self_w[:, bass.ds(grp * GT, tiles), :], ACT.Copy
                                             ).then_inc(s_loop, 1)
                    if k == "attention":
                        act.wait_ge(s_own_free, grp + 2)
                        if tiles == GT:
                            nc.scalar.activation(sums[:, bass.ds((grp % (SUM_TILES // GT)) * GT, GT), :],
                                                 eps[:, 2:3].unsqueeze(1).to_broadcast([P, GT, W]), ACT.Copy
                                                 ).then_inc(s_zer, 1)
                    columns = columns_of(ahead)
                    if k == "transpose":
                        for c in range(KC):
                            act.wait_ge(s_tr, grp * KC + c + 1)
                            nc.scalar.activation(columns(c)[:, 0:T], ps[:, banks_of(ahead)[c], 0:T], ACT.Copy
                                                 ).then_inc(s_xf, 1)
                    if k == "split":
                        if ahead:
                            act.wait_ge(s_h, (grp - 1) * CH + rank[(0, X - 1, KC - 1)] + 1)
                        act.wait_ge(s_xf, grp * KC + KC)
                        for c in range(KC):
                            nc.scalar.activation(x_hi[:, c, 0:T], columns(c)[:, 0:T], ACT.Copy).then_inc(s_xhi, 1)
                    if k == "softmax":
                        act.wait_ge(s_lm, grp + 1)
                        nc.scalar.activation(prob_of(grp)[:, 0:tiles, :], logit[:, 0:tiles, :], ACT.Exp).then_inc(s_ex, 1)
                    if isinstance(k, int):
                        kind, m, e, c, bank = list(products_of(tiles))[k]
                        if kind == "output":
                            return
                        r = rank[(m, e, c)]
                        if r < 2:
                            act.wait_ge(s_log, grp + 1)
                            act.wait_ge(s_xlo, grp * KC + KC)
                            if isinstance(grp, int) and grp > ITERS - 1:
                                act.wait_ge(s_hlo, grp * CH + r - 1)
                        else:
                            act.wait_ge(s_hlo, grp * CH + r - 1)
                        act.wait_ge(s_h, grp * CH + r + 1)
                        product = ps[:, bank, 0:T]
                        scale, shift = bn_s[:, c, m, e:e + 1], bn_t[:, c, m, e:e + 1]
                        nc.scalar.activation(h_f[:, r % 2, 0:T], product, ACT.Relu, bias=shift, scale=scale
                                             ).then_inc(s_hf, 1)
                        nc.scalar.activation(h_hi[:, m, c, 0:T], product, ACT.Relu, bias=shift, scale=scale
                                             ).then_inc(s_hhi, 1)

                schedule(act, ordered, edge, part)

            with act.If(listed(nc, act, g, 1) == 0):
                program(True)
            with act.If(listed(nc, act, g, 1) == 1):
                program(False)

        @block.vector
        def _(dve):
            def program(ordered):
                done = [0]
                state = {}

                def then(ins):
                    done[0] += 1
                    ins.then_inc(s_bnc, 1)
                    dve.wait_ge(s_bnc, done[0])

                nc.vector.memset(eps[:, 0:1], LN_EPS).then_inc(s_eps, 1)
                nc.vector.memset(eps[:, 1:2], BN_EPS).then_inc(s_eps, 1)
                nc.vector.memset(eps[:, 2:3], 0.0).then_inc(s_eps, 1)
                nc.vector.memset(sums[:, :, :], 0.0).then_inc(s_eps, 1)
                dve.wait_ge(s_eps, 4)
                if ordered:
                    guard_dve(dve)
                    parts.vector_start(dve)
                else:
                    nc.vector.memset(self_w[:, :, :], 1.0).then_inc(s_eps, 1)
                    dve.wait_ge(s_eps, 5)
                dve.sem_inc(s_ya, 1)
                dve.sem_inc(s_own_free, 1)
                if ordered:
                    parts.vector_first(dve)

                def edge(i, j, last):
                    parts.vector_piece(dve, i, j, last, state)
                    if last and j == BODY - 1:
                        parts.vector_last(dve, state)

                def part(grp, tiles, k, ahead=False):
                    if grp is None:
                        if k == "bias":
                            dve.wait_ge(s_small, 16 * NSM)
                            dve.wait_ge(s_bnT, 1)
                            nc.vector.tensor_copy(bn[:, :, :, :, :], ps[:, 5, 0:KC * 10 * X].rearrange(
                                "p (k l n e) -> p k l n e", k=KC, l=2, n=5)).then_inc(s_bnq, 1)
                        if k == "softmax":
                            dve.wait_ge(s_bnq, 2)
                            b_, g_, be_, m_, v_ = (bn[:, :, :, n, :] for n in range(5))
                            then(nc.vector.reciprocal(v_, v_))
                            then(nc.vector.tensor_tensor(bn_s[:, :, :, :], v_, g_, ALU.mult))
                            then(nc.vector.tensor_tensor(bn_t[:, :, :, :], b_, m_, ALU.subtract))
                            then(nc.vector.tensor_tensor(bn_t[:, :, :, :], bn_t[:, :, :, :], bn_s[:, :, :, :], ALU.mult))
                            then(nc.vector.tensor_tensor(bn_t[:, :, :, :], bn_t[:, :, :, :], be_, ALU.add))
                        if isinstance(k, int):
                            n = k // 2
                            if k % 2 or n >= NW:
                                return
                            dve.wait_ge(s_whi, n + 1)
                            nc.vector.tensor_tensor(w_lo[:, n // X, n % X, :, :].rearrange("p k n -> p (k n)"),
                                                    w_raw[:, n % 2, :],
                                                    w_hi[:, n // X, n % X, :, :].rearrange("p k n -> p (k n)").bitcast(F32),
                                                    ALU.subtract).then_inc(s_wlo, 1)
                        return
                    T = tiles * P
                    half = grp % 2
                    mine = xr_half(half, tiles)

                    def my_tile(q):
                        return xr[:, bass.ds(half, 1), q, :].rearrange("p a f -> p (a f)")

                    if k == "bias":
                        dve.wait_ge(s_x, 16 * grp + 16)
                        nc.vector.tensor_tensor(mine, mine, bias_rows[:, 1, :].unsqueeze(1).to_broadcast([P, tiles, F]),
                                                ALU.add).then_inc(s_c, 1)
                    if k == "sums":
                        dve.wait_ge(s_own, 16 * grp + 16)
                        dve.wait_ge(s_loop, grp + 1)
                        if not ordered:
                            pass
                        elif isinstance(grp, int) and grp >= ITERS - 1:
                            dve.wait_ge(parts.sums_added, 2 * NB * ITERS)
                        else:
                            dve.wait_ge(parts.sums_added, 2 * NB * (grp + 1))
                        for q in range(tiles):
                            tile_sums = sums[:, bass.ds((grp % (SUM_TILES // GT)) * GT + q, 1), 0:W]
                            ins = nc.vector.scalar_tensor_tensor(
                                own[:, q, 0:W], own[:, q, 0:W], loop_w[:, q, :],
                                tile_sums.rearrange("p a c -> p (a c)"), ALU.mult, ALU.add)
                        ins.then_inc(s_own_free, 1)
                    if k == "attention":
                        dve.wait_ge(s_own_free, grp + 2)
                        nc.vector.reciprocal(zinv[:, 0:tiles, :], own[:, 0:tiles, F:F + 1]).then_inc(s_c, 1)
                        dve.wait_ge(s_c, grp * 5 + 2)
                        for q in range(tiles):
                            ins = nc.vector.scalar_tensor_tensor(my_tile(q), own[:, q, 0:F], zinv[:, q, :], my_tile(q),
                                                                 ALU.mult, ALU.add)
                        ins.then_inc(s_c, 1)
                    if k == "stats":
                        dve.wait_ge(s_c, grp * 5 + 3)
                        dve.sem_inc(s_turn, 1)
                        for q in range(tiles):
                            ins = nc.vector.bn_stats(stats[:, q, :], my_tile(q))
                        ins.then_inc(s_c, 1)
                        dve.wait_ge(s_c, grp * 5 + 4)
                        dve.sem_inc(s_turn, 1)
                        for q in range(tiles):
                            ins = nc.vector.bn_aggr(mv[:, q, :], stats[:, q, :])
                        ins.then_inc(s_st, 1)
                    if k == "norm":
                        if tiles == GT:
                            dve.wait_ge(s_zer, grp + 1)
                        dve.wait_ge(s_sq, grp + 1)
                        nc.vector.reciprocal(rstd[:, 0:tiles, :], rstd[:, 0:tiles, :]).then_inc(s_c, 1)
                        dve.wait_ge(s_c, grp * 5 + 5)
                        for q in range(tiles):
                            nc.vector.tensor_scalar(xn[:, q, 0:F], my_tile(q), mv[:, q, 0:1], rstd[:, q, :],
                                                    ALU.subtract, ALU.mult).then_inc(s_xn, 1)
                    if k == "split":
                        for c in range(KC):
                            dve.wait_ge(s_xhi, grp * KC + c + 1)
                            nc.vector.tensor_tensor(x_lo[:, c, 0:T], columns_of(ahead)(c)[:, 0:T], x_hi[:, c, 0:T].bitcast(F32),
                                                    ALU.subtract).then_inc(s_xlo, 1)
                    if k == "softmax":
                        dve.wait_ge(s_log, grp + 1)
                        nc.vector.tensor_tensor(logit[:, 0:tiles, :], ps[:, banks_of(ahead)[2], 0:tiles * X].rearrange("p (n e) -> p n e", e=X),
                                                br[:, :].unsqueeze(1).to_broadcast([P, tiles, X]), ALU.add
                                                ).then_inc(s_r, 1)
                        dve.wait_ge(s_r, grp * 4 + 1)
                        nc.vector.tensor_reduce(lmax[:, 0:tiles, :], logit[:, 0:tiles, :], AX.X, ALU.max).then_inc(s_r, 1)
                        dve.wait_ge(s_r, grp * 4 + 2)
                        nc.vector.tensor_tensor(logit[:, 0:tiles, :], logit[:, 0:tiles, :],
                                                lmax[:, 0:tiles, :].to_broadcast([P, tiles, X]), ALU.subtract
                                                ).then_inc(s_lm, 1)
                    if k == "shares":
                        dve.wait_ge(s_ex, grp + 1)
                        nc.vector.tensor_reduce(lsum[:, 0:tiles, :], prob_of(grp)[:, 0:tiles, :], AX.X, ALU.add).then_inc(s_r, 1)
                        dve.wait_ge(s_r, grp * 4 + 3)
                        nc.vector.reciprocal(lsum[:, 0:tiles, :], lsum[:, 0:tiles, :]).then_inc(s_r, 1)
                        dve.wait_ge(s_r, grp * 4 + 4)
                        nc.vector.tensor_tensor(prob_of(grp)[:, 0:tiles, :], prob_of(grp)[:, 0:tiles, :],
                                                lsum[:, 0:tiles, :].to_broadcast([P, tiles, X]), ALU.mult
                                                ).then_inc(s_pr, 1)
                    if k == "share_T":
                        dve.wait_ge(s_pt, grp + 1)
                        nc.vector.tensor_copy(probT[:, 0:tiles, :], ps[0:X, banks_of(ahead)[3], 0:T].rearrange("e (n p) -> e n p", p=P)
                                              ).then_inc(s_ptc, 1)
                    if k == "biased":
                        for q in range(tiles):
                            if q % 2 == 0:
                                dve.wait_ge(s_bop, grp * 2 + q // 2 + 1)
                            nc.vector.tensor_tensor(my_tile(q), ps[:, banks_of(ahead)[4 + q // 2], (q % 2) * F:(q % 2 + 1) * F],
                                                    my_tile(q), ALU.add).then_inc(s_yin, 1)
                    if isinstance(k, int):
                        kind, m, e, c, bank = list(products_of(tiles))[k]
                        if kind == "hidden":
                            r = rank[(m, e, c)]
                            dve.wait_ge(s_hhi, grp * CH + r + 1)
                            nc.vector.tensor_tensor(h_lo[:, m, c, 0:T], h_f[:, r % 2, 0:T],
                                                    h_hi[:, m, c, 0:T].bitcast(F32), ALU.subtract).then_inc(s_hlo, 1)
                        else:
                            for q in range(2 * c, min(2 * c + 2, tiles)):
                                n = e * tiles + q
                                if q % 2 == 0:
                                    dve.wait_ge(s_y, outputs_before(grp, tiles, e, c) + 1)
                                if e == 0:
                                    dve.wait_ge(s_yin, grp * GT + q + 1)
                                else:
                                    dve.wait_ge(s_ya, 1 + grp * GT * X + n - tiles + 1)
                                nc.vector.scalar_tensor_tensor(
                                    my_tile(q), ps[:, bank, (q % 2) * F:(q % 2 + 1) * F], prob_of(grp)[:, q, e:e + 1],
                                    my_tile(q), ALU.mult, ALU.add).then_inc(s_ya, 1)

                schedule(dve, ordered, edge, part)

            with dve.If(listed(nc, dve, g, 1) == 0):
                program(True)
            with dve.If(listed(nc, dve, g, 1) == 1):
                program(False)

        @block.tensor
        def _(pe):
            def program(ordered):
                state = {}
                if ordered:
                    parts.tensor_start(pe)
                    parts.node_products(pe, 0, 0)
                    parts.node_products(pe, 0, 1)

                def edge(i, j, last):
                    parts.tensor_step(pe, i, j, last, state)

                def split_product(bank, a_hi, a_lo, b_hi, b_lo):
                    pairs = [(a_hi[k], b_hi[k]) for k in range(KC)] + [(a_lo[k], b_hi[k]) for k in range(KC)] + \
                        [(a_hi[k], b_lo[k]) for k in range(KC)]
                    for n, (a, b) in enumerate(pairs):
                        mm = nc.tensor.matmul(bank, a, b, start=n == 0, stop=n == len(pairs) - 1)
                    return mm

                def part(grp, tiles, k, ahead=False):
                    if grp is None:
                        if k == "bias":
                            pe.wait_ge(s_small, 16 * NSM)
                            for c in range(KC):
                                mm = nc.tensor.transpose(ps[:, 5, c * 10 * X:(c + 1) * 10 * X],
                                                         bn_rows[:, c * P:(c + 1) * P],
                                                         ident[0:10 * X, 0:10 * X])
                            mm.then_inc(s_bnT, 1)
                        return
                    T = tiles * P
                    banks = banks_of(ahead)
                    if k == "transpose":
                        if ahead:
                            pe.wait_ge(s_yin, grp * GT)
                        else:
                            pe.wait_ge(s_ya, 1 + grp * GT * X)
                        pe.wait_ge(s_wlo, NW)
                        pe.wait_ge(s_xn, grp * GT + tiles)
                        for c in range(KC):
                            for q in range(tiles):
                                mm = nc.tensor.transpose(ps[:, banks[c], q * P:(q + 1) * P], xn[:, q, c * P:(c + 1) * P],
                                                         ident[:, :])
                            mm.then_inc(s_tr, 1)
                    if k == "logits":
                        pe.wait_ge(s_xf, grp * KC + KC)
                        for q in range(tiles):
                            for c in range(KC):
                                mm = nc.tensor.matmul(ps[:, banks[2], q * X:(q + 1) * X],
                                                      columns_of(ahead)(c)[:, q * P:(q + 1) * P],
                                                      wr[:, c, :], start=c == 0, stop=c == KC - 1)
                        mm.then_inc(s_log, 1)
                    if k == "shares":
                        pe.wait_ge(s_pr, grp + 1)
                        for q in range(tiles):
                            mm = nc.tensor.transpose(ps[0:X, banks[3], q * P:(q + 1) * P], prob_of(grp)[:, q, :], ident[:, :])
                        mm.then_inc(s_pt, 1)
                    if k == "share_T":
                        pe.wait_ge(s_ptc, grp + 1)
                        for q in range(tiles):
                            mm = nc.tensor.matmul(ps[:, banks[4 + q // 2], (q % 2) * F:(q % 2 + 1) * F], probT[:, q, :],
                                                  bo[:, :], start=True, stop=True)
                            if q % 2 or q == tiles - 1:
                                mm.then_inc(s_bop, 1)
                    if k == 0:
                        pe.wait_ge(s_xlo, grp * KC + KC)
                        pe.wait_ge(s_yin, grp * GT + tiles)
                        pe.wait_ge(s_ya, 1 + grp * GT * X)
                    if not isinstance(k, int):
                        return
                    kind, m, e, c, bank = list(products_of(tiles))[k]
                    done_before = 1 + grp * GT * X
                    if kind == "hidden":
                        if m == 1 and c == 0:
                            pe.wait_ge(s_hlo, grp * CH + rank[(0, e, KC - 1)] + 1)
                        if bank == 6 and e >= 1:
                            pe.wait_ge(s_ya, done_before + (e - 1) * tiles + min(2, tiles))
                        if bank == 7 and e >= 2:
                            pe.wait_ge(s_ya, done_before + (e - 1) * tiles)
                        if m == 0 and c == 1 and e >= 1:
                            pe.wait_ge(s_hhi, grp * CH + rank[(1, e - 1, 0)] + 1)
                        cols = slice(c * P, (c + 1) * P)
                        a_hi = [w_hi[:, m, e, kc, cols] for kc in range(KC)]
                        a_lo = [w_lo[:, m, e, kc, cols] for kc in range(KC)]
                        if m == 0:
                            b_hi, b_lo = [x_hi[:, kc, 0:T] for kc in range(KC)], [x_lo[:, kc, 0:T] for kc in range(KC)]
                        else:
                            b_hi, b_lo = [h_hi[:, 0, kc, 0:T] for kc in range(KC)], [h_lo[:, 0, kc, 0:T] for kc in range(KC)]
                        split_product(ps[:, bank, 0:T], a_hi, a_lo, b_hi, b_lo).then_inc(s_h, 1)
                    else:
                        if c == 0:
                            pe.wait_ge(s_hlo, grp * CH + rank[(1, e, KC - 1)] + 1)
                        elif e + 1 < X:
                            pe.wait_ge(s_hhi, grp * CH + rank[(0, e + 1, 0)] + 1)
                        else:
                            pe.wait_ge(s_ya, done_before + e * tiles)
                        for q in range(2 * c, min(2 * c + 2, tiles)):
                            toks = slice(q * P, (q + 1) * P)
                            mm = split_product(ps[:, bank, (q % 2) * F:(q % 2 + 1) * F],
                                               [h_hi[:, 1, kc, toks] for kc in range(KC)],
                                               [h_lo[:, 1, kc, toks] for kc in range(KC)],
                                               [w_hi[:, 2, e, kc, :] for kc in range(KC)],
                                               [w_lo[:, 2, e, kc, :] for kc in range(KC)])
                        mm.then_inc(s_y, 1)

                schedule(pe, ordered, edge, part)

            with pe.If(listed(nc, pe, g, 1) == 0):
                program(True)
            with pe.If(listed(nc, pe, g, 1) == 1):
                program(False)


_GNN = ("W", "a_src", "a_dst", "b")
_FFN = ("Wr", "br", "W1", "b1", "g1", "be1", "m1", "v1", "W2", "b2", "g2", "be2", "m2", "v2", "Wo", "bo")
_INS = ["x", "src", "dst"] + [f"L0_gnn_{n}{l}" for l in (1, 2) for n in _GNN] + [f"L0_ffn_{n}" for n in _FFN]


def kernel(**inputs):
    import numpy as _np
    import concourse.bacc as _bacc
    from concourse import mybir as _mybir
    from concourse.bass_utils import run_bass_kernel_spmd as _run

    nc = _bacc.Bacc("TRN2", target_bir_lowering=False, num_devices=1)
    arrays, aps = {}, {}
    for name in _INS:
        a = _np.ascontiguousarray(inputs[name])
        arrays[f"in_{name}_dram"] = a
        aps[name] = nc.dram_tensor(f"in_{name}_dram", a.shape, _mybir.dt.from_np(a.dtype), kind="ExternalInput").ap()
    shape = arrays["in_x_dram"].shape
    out = nc.dram_tensor("out_0_dram", shape, _mybir.dt.float32, kind="ExternalOutput").ap()
    gnn = [{n: aps[f"L0_gnn_{n}{l}"] for n in _GNN} for l in (1, 2)]
    ffn = {n: aps[f"L0_ffn_{n}"] for n in _FFN}
    build_program(nc, aps["x"], aps["src"], aps["dst"], gnn, ffn, out)
    r = _run(nc, [arrays], core_ids=[0])
    return r.results[0]["out_0_dram"]
```
